# Optimizing a Trainium2 kernel written in Bass

```python
import numpy as np
import jax
import jax.numpy as jnp

def _softmax(x, axis=-1):
    return jax.nn.softmax(x, axis=axis)

def _gelu(x):
    return jax.nn.gelu(x, approximate=True)

def _silu(x):
    return jax.nn.silu(x)

def _sigmoid(x):
    return jax.nn.sigmoid(x)

def _layernorm(x, axis=-1, eps=1e-05):
    m = jnp.mean(x, axis=axis, keepdims=True)
    v = jnp.var(x, axis=axis, keepdims=True)
    return (x - m) / jnp.sqrt(v + eps)

def _scatter_add(tgt, idx, src, axis=0):
    return tgt.at[idx].add(src)

def _segment_sum(src, seg, n):
    return jax.ops.segment_sum(src, seg, n)
kernel_name = 'mk_decoder_postln_d1_seqx_r8_c1c582'

def setup_inputs(seed: int=0):
    np.random.seed(seed)
    _w = jnp.asarray

    def _rec_inputs():
        import jax
        import jax.numpy as jnp
        _rk = jax.random.key(seed)
        x = -0.0003929 + 0.9999 * jax.random.normal(jax.random.fold_in(_rk, 1), (16, 128, 128), jnp.float32)
        _lenS = 128 - jax.random.randint(jax.random.fold_in(_rk, 7), (16,), 0, max(1, 128 // 4) + 1, jnp.int32)
        _lenS2 = 128 - jax.random.randint(jax.random.fold_in(_rk, 8), (16,), 0, max(1, 128 // 4) + 1, jnp.int32)
        _ctx_768P = jax.random.normal(jax.random.fold_in(_rk, 11), (16, 16, 96), jnp.float32)
        _ctx_768c = jax.random.dirichlet(jax.random.fold_in(_rk, 511), 0.3 * jnp.ones((16,), jnp.float32), (16, 128))
        _ctx_768t = jnp.einsum('bsk,bkd->bsd', _ctx_768c, _ctx_768P)
        _ctx_768t = _ctx_768t * jax.lax.rsqrt(jnp.mean(jnp.square(_ctx_768t)) + 1e-12) * 0.953939
        ctx_768 = -7.36909e-05 + 0.999899 * (_ctx_768t + 0.3 * jax.random.normal(jax.random.fold_in(_rk, 611), (16, 128, 96), jnp.float32))
        return (x, ctx_768)
    x, ctx_768 = _rec_inputs()

    def _L0_attn_setup():
        import jax, jax.numpy as jnp
        import numpy as np
        NUM_HEADS = 16
        HIDDEN = 128
        HEAD_DIM = HIDDEN // NUM_HEADS
        B, L = (2, 256)
        key = jax.random.key(seed)
        ks = jax.random.split(key, 5)
        scale = 1.0 / np.sqrt(HIDDEN)
        return {'x': jax.random.normal(ks[0], (B, L, HIDDEN), dtype=jnp.float32), 'Wq': jax.random.normal(ks[1], (HIDDEN, HIDDEN), dtype=jnp.float32) * scale, 'Wk': jax.random.normal(ks[2], (HIDDEN, HIDDEN), dtype=jnp.float32) * scale, 'Wv': jax.random.normal(ks[3], (HIDDEN, HIDDEN), dtype=jnp.float32) * scale, 'Wo': jax.random.normal(ks[4], (HIDDEN, HIDDEN), dtype=jnp.float32) * scale}
    _L0_attn_all = _L0_attn_setup()
    _L0_attn_in = {k: v for k, v in _L0_attn_all.items() if k in ('Wq', 'Wk', 'Wv', 'Wo')}
    del _L0_attn_all

    def _L0_xattn_setup():
        import jax, jax.numpy as jnp
        import numpy as np
        EPS = 1e-08
        key = jax.random.key(seed)
        kv, kt, k1, k2, k3, k4 = jax.random.split(key, 6)
        B, S = (16, 128)
        VD, TD, H = (128, 96, 64)
        visual_features = jax.random.normal(kv, (B, S, VD), dtype=jnp.float32)
        text_features = jax.random.normal(kt, (B, S, TD), dtype=jnp.float32)
        Wv = jax.random.normal(k1, (H, VD), dtype=jnp.float32) * (1.0 / np.sqrt(VD))
        bv = jax.random.normal(k2, (H,), dtype=jnp.float32) * 0.01
        Wt = jax.random.normal(k3, (H, TD), dtype=jnp.float32) * (1.0 / np.sqrt(TD))
        bt = jax.random.normal(k4, (H,), dtype=jnp.float32) * 0.01
        return {'visual_features': visual_features, 'text_features': text_features, 'Wv': Wv, 'bv': bv, 'Wt': Wt, 'bt': bt}
    _L0_xattn_all = _L0_xattn_setup()
    _L0_xattn_in = {k: v for k, v in _L0_xattn_all.items() if k in ('Wv', 'bv', 'Wt', 'bt')}
    del _L0_xattn_all

    def _L0_ffn_setup():
        import jax, jax.numpy as jnp
        import numpy as np
        TOP_K = 2
        key = jax.random.key(seed)
        ks = jax.random.split(key, 6)
        B, S, D, F, E = (2, 256, 128, 512, 8)
        sd = 1.0 / np.sqrt(D)
        sf = 1.0 / np.sqrt(F)
        return {'x': jax.random.normal(ks[0], (B, S, D), jnp.float32), 'gate_w': jax.random.normal(ks[1], (D, E), jnp.float32) * sd, 'w1': jax.random.normal(ks[2], (E, D, F), jnp.float32) * sd, 'b1': jax.random.normal(ks[3], (E, F), jnp.float32) * 0.01, 'w2': jax.random.normal(ks[4], (E, F, D), jnp.float32) * sf, 'b2': jax.random.normal(ks[5], (E, D), jnp.float32) * 0.01}
    _L0_ffn_all = _L0_ffn_setup()
    _L0_ffn_in = {k: v for k, v in _L0_ffn_all.items() if k in ('gate_w', 'w1', 'b1', 'w2', 'b2')}
    del _L0_ffn_all
    return {'x': x, 'ctx_768': ctx_768, 'L0_attn_Wq': _L0_attn_in['Wq'], 'L0_attn_Wk': _L0_attn_in['Wk'], 'L0_attn_Wv': _L0_attn_in['Wv'], 'L0_attn_Wo': _L0_attn_in['Wo'], 'L0_xattn_Wv': _L0_xattn_in['Wv'], 'L0_xattn_bv': _L0_xattn_in['bv'], 'L0_xattn_Wt': _L0_xattn_in['Wt'], 'L0_xattn_bt': _L0_xattn_in['bt'], 'L0_ffn_gate_w': _L0_ffn_in['gate_w'], 'L0_ffn_w1': _L0_ffn_in['w1'], 'L0_ffn_b1': _L0_ffn_in['b1'], 'L0_ffn_w2': _L0_ffn_in['w2'], 'L0_ffn_b2': _L0_ffn_in['b2']}

def reference(x, ctx_768, L0_attn_Wq, L0_attn_Wk, L0_attn_Wv, L0_attn_Wo, L0_xattn_Wv, L0_xattn_bv, L0_xattn_Wt, L0_xattn_bt, L0_ffn_gate_w, L0_ffn_w1, L0_ffn_b1, L0_ffn_w2, L0_ffn_b2):
    import jax
    import jax.numpy as jnp

    def _L0_attn_ref(x, Wq, Wk, Wv, Wo):
        import jax, jax.numpy as jnp
        import numpy as np
        NUM_HEADS = 16
        HIDDEN = 128
        HEAD_DIM = HIDDEN // NUM_HEADS
        B, L = (2, 256)
        b, l, _ = x.shape
        q = (x @ Wq.T).reshape(b, l, NUM_HEADS, HEAD_DIM)
        k = (x @ Wk.T).reshape(b, l, NUM_HEADS, HEAD_DIM)
        v = (x @ Wv.T).reshape(b, l, NUM_HEADS, HEAD_DIM)
        q = jax.nn.elu(q) + 1.0
        k = jax.nn.elu(k) + 1.0
        kv = jnp.einsum('blhd,blhe->blhde', k, v)
        kv_cumsum = jnp.cumsum(kv, axis=1)
        k_cumsum = jnp.cumsum(k, axis=1)
        out = jnp.einsum('blhd,blhde->blhe', q, kv_cumsum)
        normalizer = jnp.clip(jnp.einsum('blhd,blhd->blh', q, k_cumsum), 1e-06, None)
        out = out / normalizer[..., None]
        out = out.reshape(b, l, HIDDEN)
        return out @ Wo.T

    def _L0_xattn_ref(visual_features, text_features, Wv, bv, Wt, bt):
        import jax, jax.numpy as jnp
        import numpy as np
        EPS = 1e-08
        v = jnp.einsum('bsd,hd->bsh', visual_features, Wv) + bv
        t = jnp.einsum('bsd,hd->bsh', text_features, Wt) + bt
        dots = jnp.einsum('bih,bjh->bij', v, t)
        vn = jnp.linalg.norm(v, axis=-1)
        tn = jnp.linalg.norm(t, axis=-1)
        denom = jnp.maximum(vn[:, :, None] * tn[:, None, :], EPS)
        return dots / denom

    def _L0_ffn_ref(x, gate_w, w1, b1, w2, b2):
        import jax, jax.numpy as jnp
        import numpy as np
        TOP_K = 2
        B, S, D = x.shape
        T = B * S
        xf = x.reshape(T, D)
        gate_scores = jax.nn.softmax(xf @ gate_w, axis=-1)
        topk_scores, topk_idx = jax.lax.top_k(gate_scores, TOP_K)
        topk_scores = topk_scores / jnp.sum(topk_scores, axis=-1, keepdims=True)
        h = jax.nn.gelu(jnp.einsum('td,edf->etf', xf, w1) + b1[:, None, :], approximate=False)
        y = jnp.einsum('etf,efd->etd', h, w2) + b2[:, None, :]
        tok = jnp.arange(T)
        y_sel = y[topk_idx.T, tok[None, :]]
        out = jnp.einsum('kt,ktd->td', topk_scores.T, y_sel)
        return out.reshape(B, S, D)
    x = _layernorm(x + _L0_attn_ref(x, L0_attn_Wq, L0_attn_Wk, L0_attn_Wv, L0_attn_Wo), axis=-1)
    x = _layernorm(x + _L0_xattn_ref(x, ctx_768, L0_xattn_Wv, L0_xattn_bv, L0_xattn_Wt, L0_xattn_bt), axis=-1)
    x = _layernorm(x + _L0_ffn_ref(x, L0_ffn_gate_w, L0_ffn_w1, L0_ffn_b1, L0_ffn_w2, L0_ffn_b2), axis=-1)
    return x

_drawn_inputs = setup_inputs


def setup_inputs(seed=0):
    import zlib

    import numpy as np

    out = dict(_drawn_inputs(seed))
    spreads = {}
    factors = {'L0_xattn_bv': 6.892, 'L0_xattn_bt': 32.025, 'L0_ffn_b1': 8.0, 'L0_ffn_b2': 8.0}
    for name, (base, spread) in spreads.items():
        noise = np.random.default_rng([zlib.crc32(name.encode()), seed]).standard_normal(out[name].shape)
        drawn = base * np.exp(spread * noise) if base else spread * noise
        out[name] = jnp.asarray(drawn.astype(out[name].dtype))
    for name, factor in factors.items():
        out[name] = (out[name] * factor).astype(out[name].dtype)
    return out
```

```python
from contextlib import ExitStack

import concourse.bass as bass
from concourse import mybir

F32 = mybir.dt.float32
F16 = mybir.dt.float16
BF16 = mybir.dt.bfloat16
I32 = mybir.dt.int32
U32 = mybir.dt.uint32
ALU = mybir.AluOpType
ACT = mybir.ActivationFunctionType
AX_X = mybir.AxisListType.X

P = 128
HEADS, HD = 16, 8
EXPERTS, TOP = 8, 2
LN_EPS = 1e-5
NORM_EPS = 1e-6
COS_CAP = 1e8
TINY = 1e-30
W1_SCALE = 16.0


def decoder_layer(nc, x, xT, ctxT, w_qkvT, w_oT, w_xvT, b_v, w_tT, b_t, gate_w, w1, b1T, w2, b2, out):
    T = x.shape[0]
    TILES = T // P
    PAIRS = TILES // 2
    CD, XH = ctxT.shape[0], w_tT.shape[1]
    FF = w1.shape[2]
    FC = FF // P
    SLOTS = TOP * TILES + EXPERTS - 1
    assert SLOTS % 3 == 0 and PAIRS % 2 == 0
    CAP = T + P
    DUMMIES = EXPERTS - 1
    PADS = EXPERTS + DUMMIES
    ROW = P + 1
    SCAN = HEADS * HD * HD

    x_rows = nc.dram_tensor("x_rows", (EXPERTS * CAP + DUMMIES * P, ROW), F32, kind="Internal").ap()
    y_rows = nc.dram_tensor("y_rows", (TOP * T + PADS * P, P), F32, kind="Internal").ap()

    with ExitStack() as ctx:
        def sb(name, shape, dt=F32):
            return ctx.enter_context(nc.sbuf_tensor(name, shape, dt))

        def sem(name):
            return ctx.enter_context(nc.semaphore(name))

        wqkv = sb("wqkv", [P, 3 * P])
        wo = sb("wo", [P, P])
        wxv = sb("wxv", [P, XH])
        bv = sb("bv", [XH, 1])
        wt = sb("wt", [CD, XH])
        bt = sb("bt", [XH, 1])
        gw = sb("gw", [P, EXPERTS])
        ctx_sb = sb("ctx_sb", [CD, T])
        w1_raw = sb("w1_raw", [P, EXPERTS * FF])
        w1_hi = sb("w1_hi", [P, EXPERTS * FF], F16)
        w1_lo = sb("w1_lo", [P, EXPERTS * FF], F16)
        b1_sb = sb("b1_sb", [P, EXPERTS * FC])
        w2_sb = sb("w2_sb", [P, EXPERTS * FC * P])
        b2_sb = sb("b2_sb", [P, EXPERTS * P])
        ident = sb("ident", [P, P])
        ident16 = sb("ident16", [P, P], F16)
        upto = sb("upto", [P, P])
        before = sb("before", [P, P], BF16)
        ones = sb("ones", [P, P])
        ones16 = sb("ones16", [P, P], BF16)
        half = sb("half", [P, TILES])
        iota_e = sb("iota_e", [P, EXPERTS])
        base_e = sb("base_e", [P, EXPERTS])
        iota_j = sb("iota_j", [P, SLOTS])
        iota_ei = sb("iota_ei", [P, EXPERTS], I32)
        base_ei = sb("base_ei", [P, EXPERTS], I32)
        iota_ji = sb("iota_ji", [P, SLOTS], I32)
        returns = sb("returns", [P, TILES, TOP], I32)
        pick = sb("pick", [TILES, TILES, P])
        padding = sb("padding", [P, PADS, ROW])
        tT = sb("tT", [XH, T])
        tsq = sb("tsq", [XH, T])
        tn2 = sb("tn2", [P, TILES])
        itn = sb("itn", [P, TILES])
        itnT = sb("itnT", [TILES, P])
        itn_row = sb("itn_row", [P, T])
        xT_sb = [sb(f"xT_sb{p}", [P, 2 * P]) for p in range(2)]
        x_sb = [sb(f"x_sb{p}", [P, 2, P]) for p in range(2)]
        e_qk = sb("e_qk", [P, 2, 2 * P])
        r_qk = sb("r_qk", [P, 2, 2 * P])
        v_sb = sb("v_sb", [P, 2, P])
        phi = [sb(f"phi{p}", [P, 2, 2 * P]) for p in range(2)]
        kv = sb("kv", [P, 2, SCAN])
        qk = sb("qk", [P, 2, P])
        norm = sb("norm", [P, 2 * HEADS])
        rnorm = sb("rnorm", [P, 2 * HEADS])
        qn = sb("qn", [P, 2, P])
        prod = sb("prod", [P, 2, SCAN])
        oT = sb("oT", [P, 2 * P])
        r1 = sb("r1", [P, 2, P])
        st1 = sb("st1", [P, 2, 6])
        mv1 = sb("mv1", [P, 2, 2])
        ve1 = sb("ve1", [P, 2])
        rstd1 = sb("rstd1", [P, 2])
        nmr1 = sb("nmr1", [P, 2])
        x1 = sb("x1", [P, 2, P])
        x1T = sb("x1T", [P, 2 * P])
        vT = sb("vT", [XH, 2 * P])
        vsq = sb("vsq", [XH, 2 * P])
        vn2 = sb("vn2", [P, 2])
        ivn = sb("ivn", [P, 2])
        wcos = sb("wcos", [P, 2, P])
        ucos = sb("ucos", [P, 2, P])
        r2 = [sb(f"r2{p}", [P, 2, P]) for p in range(2)]
        st2 = sb("st2", [P, 2, 6])
        mv2 = [sb(f"mv2{p}", [P, 2, 2]) for p in range(2)]
        ve2 = sb("ve2", [P, 2])
        rstd2 = sb("rstd2", [P, 2])
        nmr2 = sb("nmr2", [P, 2])
        x2 = [sb(f"x2{p}", [P, 2, P]) for p in range(2)]
        x2_all = sb("x2_all", [P, TILES, P])
        x2T = sb("x2T", [P, 2 * P])
        gmax = sb("gmax", [P, 2])
        gdif = sb("gdif", [P, 2, EXPERTS])
        gexp = sb("gexp", [P, 2, EXPERTS])
        gsum = sb("gsum", [P, 2])
        rgsum = sb("rgsum", [P, 2])
        score = sb("score", [P, 2, EXPERTS])
        top8 = sb("top8", [P, 2, EXPERTS])
        idx8 = sb("idx8", [P, 2, EXPERTS], U32)
        wsum = sb("wsum", [P, 2])
        rwsum = sb("rwsum", [P, 2])
        w_all = sb("w_all", [P, TILES, TOP])
        chosen = sb("chosen", [P, 2, TOP])
        onehot = sb("onehot", [P, 2 * TOP, EXPERTS])
        member = [sb(f"member{p}", [P, 2, EXPERTS], BF16) for p in range(2)]
        macc = [sb(f"macc{p}", [P, EXPERTS], BF16) for p in range(2)]
        msum = sb("msum", [P, EXPERTS], BF16)
        place = sb("place", [P, 2, EXPERTS])
        placed = sb("placed", [P, 2 * TOP, EXPERTS])
        rowf = sb("rowf", [P, 2 * TOP])
        rowi = [sb(f"rowi{p}", [P, 2 * TOP], I32) for p in range(2)]
        pay = [sb(f"pay{p}", [P, 2, TOP, ROW]) for p in range(2)]
        cnt = sb("cnt", [P, EXPERTS])
        cnt_i = sb("cnt_i", [P, EXPERTS], I32)
        cup_i = sb("cup_i", [P, EXPERTS], I32)
        nt_i = sb("nt_i", [P, EXPERTS], I32)
        nt = sb("nt", [P, EXPERTS])
        ntc = sb("ntc", [P, EXPERTS])
        past = sb("past", [P, SLOTS, EXPERTS])
        pnt = sb("pnt", [P, SLOTS, EXPERTS])
        ej = sb("ej", [P, SLOTS])
        first_j = sb("first_j", [P, SLOTS])
        off_j = sb("off_j", [P, SLOTS])
        off128 = sb("off128", [P, SLOTS])
        row_j = sb("row_j", [P, SLOTS])
        ejc = sb("ejc", [P, SLOTS])
        row_i = sb("row_i", [P, SLOTS], I32)
        e_i = sb("e_i", [P, SLOTS], I32)
        xrow = [sb(f"xrow{r}", [P, ROW]) for r in range(3)]
        ridx = [sb(f"ridx{r}", [P, 1], I32) for r in range(3)]
        xeT = [sb(f"xeT{r}", [P, 2 * P], F16) for r in range(3)]
        g_sb = [sb(f"g_sb{r}", [P, FF]) for r in range(3)]
        y_sb = [sb(f"y_sb{r}", [P, P]) for r in range(3)]
        y_in = sb("y_in", [P, TOP, TILES, P])
        z1 = w1_raw[:, 0:TILES * P].rearrange("p (t d) -> p t d", d=P)
        z = w1_raw[:, TILES * P:2 * TILES * P].rearrange("p (t d) -> p t d", d=P)
        st3 = sb("st3", [P, TILES, 6])
        mv3 = sb("mv3", [P, TILES, 2])
        ve3 = sb("ve3", [P, TILES])
        rstd3 = sb("rstd3", [P, TILES])
        nmr3 = sb("nmr3", [P, TILES])
        o_sb = sb("o_sb", [P, TILES, P])

        ps = ctx.enter_context(nc.psum_tensor("ps", [P, 8, 512], F32))
        bank = [ps[:, b, :] for b in range(8)]
        QKV = ps[:, 0:2, :]
        CUM = [bank[2], bank[3]]
        TR, MM, DOT, GATE = bank[4], bank[5], bank[6], bank[7]
        HB = [bank[0], bank[1], bank[2]]
        XB = bank[3]
        YB = [bank[4], bank[5], bank[6]]

        ld_w, ld_ctx, ld_big, ld_w1 = sem("ld_w"), sem("ld_ctx"), sem("ld_big"), sem("ld_w1")
        ld_x = [sem(f"ld_x{p}") for p in range(2)]
        consts, vconsts = sem("consts"), sem("vconsts")
        tproj, tread, tnorm, tn2_ok, itn_ok, itnT_ps, itnT_ok, itnrow_ps, itnrow_ok = (
            sem(n) for n in ("tproj", "tread", "tnorm", "tn2_ok", "itn_ok", "itnT_ps", "itnT_ok", "itnrow_ps", "itnrow_ok"))
        w1hi_ok, w1lo_ok = sem("w1hi_ok"), sem("w1lo_ok")
        qkv_ps, qkv_read, phi_ok, kv_ok, kcum_ps, kcum_read, qn_ok, cum_ps, prod_ok = (
            sem(n) for n in ("qkv_ps", "qkv_read", "phi_ok", "kv_ok", "kcum_ps", "kcum_read", "qn_ok", "cum_ps", "prod_ok"))
        oT_ps, oT_ok, y_ps, y_read, mv1_ok, ve1_ok, rstd1_ok, nmr1_ok, x1_ok, x1T_ps, x1T_ok, vT_ps, vT_ok = (
            sem(n) for n in ("oT_ps", "oT_ok", "y_ps", "y_read", "mv1_ok", "ve1_ok", "rstd1_ok", "nmr1_ok", "x1_ok", "x1T_ps",
                             "x1T_ok", "vT_ps", "vT_ok"))
        dot_ps, vn2_ok, ivn_ok, dot_read, mv2_ok, ve2_ok, rstd2_ok, nmr2_ok, x2_ok, x2T_ps, x2T_ok = (
            sem(n) for n in ("dot_ps", "vn2_ok", "ivn_ok", "dot_read", "mv2_ok", "ve2_ok", "rstd2_ok", "nmr2_ok", "x2_ok",
                             "x2T_ps", "x2T_ok"))
        gate_ps, gdif_ok, gexp_ok, member_ok, macc_ok, pos_ps, pos_read, row_ok, hi_ok, pay_ok = (
            sem(n) for n in ("gate_ps", "gdif_ok", "gexp_ok", "member_ok", "macc_ok", "pos_ps", "pos_read", "row_ok", "hi_ok",
                             "pay_ok"))
        apart = sem("apart")
        kept = [sem(f"kept{p}") for p in range(2)]
        scattered = [sem(f"scattered{p}") for p in range(2)]
        in1, in2, in3 = sem("in1"), sem("in2"), sem("in3")
        cnt_ps, table_ok, tsteps, filled = sem("cnt_ps"), sem("table_ok"), sem("tsteps"), sem("filled")
        ld_row = [sem(f"ld_row{r}") for r in range(3)]
        xe_ps, xe_ok, ridx_ok, h_ps, g_ok, y2_ps, y2_ok = (
            sem(n) for n in ("xe_ps", "xe_ok", "ridx_ok", "h_ps", "g_ok", "y2_ps", "y2_ok"))
        returned = [sem(f"returned{r}") for r in range(3)]
        QUADS = TILES // 4
        ld_y = [sem(f"ld_y{q}") for q in range(QUADS)]
        zsteps, mv3_ok, ve3_ok, rstd3_ok, nmr3_ok, o_ok, stored = (
            sem(n) for n in ("zsteps", "mv3_ok", "ve3_ok", "rstd3_ok", "nmr3_ok", "o_ok", "stored"))

        CONSTS = 16
        VCONSTS = 5
        W_LOADS, CTX_LOADS, BIG_LOADS = 5, 3, 3
        xT_dram = xT.rearrange("d (n c) -> d n c", c=2 * P)
        x_dram = x.rearrange("(n t p) d -> p n t d", t=2, p=P)
        out_dram = out.rearrange("(t p) d -> p t d", p=P)
        y_dram = y_rows[0:TOP * T, :].rearrange("(k t p) d -> p k t d", k=TOP, p=P)

        def pipeline(eng, step):
            for n in range(4):
                step(n, n % 2, n // 2, True, n >= 1, n >= 2)
            with eng.Fori(2, PAIRS // 2) as i:
                for p in range(2):
                    step(2 * i + p, p, i, True, True, True)
            for n in (PAIRS, PAIRS + 1):
                step(n, n % 2, n // 2, False, n == PAIRS, True)

        def wait_apart(eng, *pairs):
            for s, value in pairs:
                at_least(eng, s, value)
            eng.sem_inc(apart, 1)

        def at_least(eng, s, value):
            if not isinstance(value, int) or value > 0:
                eng.wait_ge(s, value)

        block = ctx.enter_context(nc.Block())

        @block.sync
        def _(sp):
            def load_x(n, p):
                at_least(sp, qkv_ps, n - 1)
                at_least(sp, y_read, n - 1)
                sp.dma_start(xT_sb[p][:, :], xT_dram[:, n, :]).then_inc(ld_x[p], 16)
                sp.dma_start(x_sb[p][:, :, :], x_dram[:, n, :, :]).then_inc(ld_x[p], 16)

            def keep_x2(m, p):
                sp.wait_ge(x2_ok, 2 * (m + 1))
                sp.dma_start(x2_all[:, bass.ds(2 * m, 2), :], x2[p][:, :, :]).then_inc(kept[p], 16)

            sp.dma_start(xT_sb[0][:, :], xT_dram[:, 0, :]).then_inc(ld_x[0], 16)
            sp.dma_start(x_sb[0][:, :, :], x_dram[:, 0, :, :]).then_inc(ld_x[0], 16)
            sp.dma_start(xT_sb[1][:, :], xT_dram[:, 1, :]).then_inc(ld_x[1], 16)
            sp.dma_start(x_sb[1][:, :, :], x_dram[:, 1, :, :]).then_inc(ld_x[1], 16)
            sp.dma_start(w1_raw[:, :].rearrange("p (e f) -> p e f", e=EXPERTS),
                         w1.rearrange("e d f -> d e f")).then_inc(ld_w1, 16)
            sp.dma_start(w2_sb[:, :].rearrange("p (a d) -> p a d", d=P),
                         w2.rearrange("e (c p) d -> p (e c) d", p=P)).then_inc(ld_big, 16)
            sp.dma_start(b1_sb[:, :], b1T).then_inc(ld_big, 16)
            sp.dma_start(b2_sb[:, :], b2.rearrange("(a e) d -> a (e d)", a=1).broadcast_to([P, EXPERTS * P])).then_inc(ld_big, 16)
            sp.wait_ge(consts, CONSTS)
            sp.dma_start(x_rows[EXPERTS * CAP:, :].rearrange("(r p) c -> p r c", p=P),
                         padding[:, EXPERTS:, :]).then_inc(filled, 16)
            for n in (2, 3):
                load_x(n, n % 2)
                keep_x2(n - 2, n % 2)
            with sp.Fori(2, PAIRS // 2) as i:
                for p in range(2):
                    load_x(2 * i + p, p)
                    keep_x2(2 * i + p - 2, p)
            for m in (PAIRS - 2, PAIRS - 1):
                keep_x2(m, m % 2)

            sp.wait_ge(table_ok, 1)
            for e in range(EXPERTS):
                n_e = sp.value_load(cnt_i[0:1, e:e + 1], min_val=0, max_val=T)
                sp.dma_start(x_rows[bass.ds(n_e + e * CAP, P), :], padding[:, e, :]).then_inc(filled, 16)
            sp.wait_ge(filled, 16 * (EXPERTS + 1))
            for p in range(2):
                sp.wait_ge(scattered[p], 16 * 2 * TOP * (PAIRS // 2))
            sp.wait_ge(table_ok, 3)

            def load_row(j, i, r):
                at_least(sp, xe_ps, j - 2)
                at_least(sp, ridx_ok, j - 2)
                row = sp.value_load(row_i[0:1, bass.ds(j, 1)], min_val=0, max_val=EXPERTS * CAP + (DUMMIES - 1) * P)
                sp.dma_start(xrow[r][:, :], x_rows[bass.ds(row, P), :]).then_inc(ld_row[r], 16)

            for r in range(3):
                load_row(r, 0, r)
            with sp.Fori(1, SLOTS // 3) as i:
                for r in range(3):
                    load_row(3 * i + r, i, r)

            for r in range(3):
                sp.wait_ge(returned[r], 16 * (SLOTS // 3))
            for q in range(QUADS):
                for k in range(TOP):
                    sp.dma_start(y_in[:, k, 4 * q:4 * q + 4, :], y_dram[:, k, 4 * q:4 * q + 4, :]).then_inc(ld_y[q], 16)
            for q in range(QUADS):
                sp.wait_ge(o_ok, 4 * (q + 1))
                sp.dma_start(out_dram[:, 4 * q:4 * q + 4, :], o_sb[:, 4 * q:4 * q + 4, :]).then_inc(stored, 16)
            sp.wait_ge(stored, 16 * QUADS)

        @block.gpsimd
        def _(pool):
            pool.memset(ident[:, :], 0.0).then_inc(consts, 1)
            pool.memset(upto[:, :], 1.0).then_inc(consts, 1)
            pool.memset(before[:, :], 1.0).then_inc(consts, 1)
            pool.memset(ones[:, :], 1.0).then_inc(consts, 1)
            pool.memset(half[:, :], -0.5).then_inc(consts, 1)
            pool.wait_ge(consts, 5)
            pool.affine_select(out=ident[:, :], in_=ident[:, :], compare_op=ALU.not_equal, fill=1.0, base=0,
                               pattern=[[-1, P]], channel_multiplier=1).then_inc(consts, 1)
            pool.affine_select(out=upto[:, :], in_=upto[:, :], compare_op=ALU.is_ge, fill=0.0, base=0,
                               pattern=[[1, P]], channel_multiplier=-1).then_inc(consts, 1)
            pool.affine_select(out=before[:, :], in_=before[:, :], compare_op=ALU.is_gt, fill=0.0, base=0,
                               pattern=[[1, P]], channel_multiplier=-1).then_inc(consts, 1)
            pool.memset(pick[:, :, :], 1.0).then_inc(consts, 1)
            pool.memset(padding[:, :, :], 0.0).then_inc(consts, 1)
            pool.wait_ge(consts, 10)
            pool.affine_select(out=pick[:, :, :], in_=pick[:, :, :], compare_op=ALU.is_equal, fill=0.0, base=0,
                               pattern=[[1, TILES], [0, P]], channel_multiplier=-1).then_inc(consts, 1)
            pool.iota(padding[:, :, P:ROW].bitcast(I32), [[P, PADS]], base=TOP * T, channel_multiplier=1).then_inc(consts, 1)
            pool.iota(returns[:, :, :], [[P, TILES], [T, TOP]], base=0, channel_multiplier=1).then_inc(consts, 1)
            pool.iota(iota_ei[:, :], [[1, EXPERTS]], base=0, channel_multiplier=0).then_inc(consts, 1)
            pool.iota(base_ei[:, :], [[CAP, EXPERTS]], base=0, channel_multiplier=0).then_inc(consts, 1)
            pool.iota(iota_ji[:, :], [[1, SLOTS]], base=0, channel_multiplier=0).then_inc(consts, 1)
            pool.wait_ge(tn2_ok, 1)
            pool.tensor_tensor(itn[:, :], tn2[:, :], half[:, :], ALU.pow).then_inc(itn_ok, 1)

            def rstd1_of(m):
                wait_apart(pool, (mv1_ok, 2 * (m + 1)), (nmr1_ok, m), (x1_ok, 2 * m))
                pool.tensor_scalar(ve1[:, :], mv1[:, :, 1], LN_EPS, None, ALU.add).then_inc(ve1_ok, 1)
                pool.wait_ge(ve1_ok, m + 1)
                pool.tensor_tensor(rstd1[:, :], ve1[:, :], half[:, 0:2], ALU.pow).then_inc(rstd1_ok, 1)

            def ivn_of(m):
                pool.wait_ge(vn2_ok, m + 1)
                pool.tensor_tensor(ivn[:, :], vn2[:, :], half[:, 0:2], ALU.pow).then_inc(ivn_ok, 1)

            def rstd2_of(m, p):
                wait_apart(pool, (mv2_ok, 2 * (m + 1)), (nmr2_ok, m), (x2_ok, 2 * m))
                pool.tensor_scalar(ve2[:, :], mv2[p][:, :, 1], LN_EPS, None, ALU.add).then_inc(ve2_ok, 1)
                pool.wait_ge(ve2_ok, m + 1)
                pool.tensor_tensor(rstd2[:, :], ve2[:, :], half[:, 0:2], ALU.pow).then_inc(rstd2_ok, 1)

            def scatter(m, p):
                wait_apart(pool, (row_ok, m + 1), (pay_ok, 2 * (m + 1)))
                for c in range(2 * TOP):
                    pool.indirect_dma_start(x_rows, bass.IndirectOffsetOnAxis(ap=rowi[p][:, c:c + 1], axis=0),
                                            pay[p][:, c // TOP, c % TOP, :], None).then_inc(scattered[p], 16)

            def step(n, p, i, s1, s2, s3):
                if s2:
                    rstd1_of(n - 1)
                if s3:
                    scatter(n - 2, p)
                if s2:
                    ivn_of(n - 1)
                    rstd2_of(n - 1, 1 - p)

            pipeline(pool, step)

            def give_back(j, i, r):
                wait_apart(pool, (y2_ok, j + 1), (ridx_ok, j + 1))
                pool.indirect_dma_start(y_rows, bass.IndirectOffsetOnAxis(ap=ridx[r][:, 0:1], axis=0),
                                        y_sb[r][:, :], None).then_inc(returned[r], 16)

            with pool.Fori(0, SLOTS // 3) as i:
                for r in range(3):
                    give_back(3 * i + r, i, r)

            for q in range(QUADS):
                t0, t1 = 4 * q, 4 * q + 4
                pool.wait_ge(mv3_ok, t1)
                pool.tensor_scalar(ve3[:, t0:t1], mv3[:, t0:t1, 1], LN_EPS, None, ALU.add).then_inc(ve3_ok, 1)
                pool.wait_ge(ve3_ok, q + 1)
                pool.tensor_tensor(rstd3[:, t0:t1], ve3[:, t0:t1], half[:, 0:4], ALU.pow).then_inc(rstd3_ok, 1)

        @block.tensor
        def _(pe):
            pe.wait_ge(ld_ctx, 16 * CTX_LOADS)
            for c in range(T // 512):
                pe.matmul(bank[c][0:XH, :], wt[:, :], ctx_sb[:, c * 512:(c + 1) * 512], start=True, stop=True).then_inc(tproj, 1)
            pe.wait_ge(consts, CONSTS)
            pe.wait_ge(tread, 2 * (T // 512))
            for b in range(TILES):
                last = pe.matmul(GATE[:, b:b + 1], tsq[:, b * P:(b + 1) * P], ones[0:XH, 0:1], start=True, stop=True)
            last.then_inc(tnorm, 1)
            pe.wait_ge(itn_ok, 1)
            pe.transpose(TR[0:TILES, 0:P], itn[:, :], ident[:, :]).then_inc(itnT_ps, 1)
            pe.wait_ge(itnT_ok, 1)
            for b in range(TILES):
                last = pe.matmul(bank[b // 4][:, (b % 4) * P:(b % 4 + 1) * P], pick[:, b, :], itnT[:, :], start=True, stop=True)
                if b % 4 == 3:
                    last.then_inc(itnrow_ps, 1)
            pe.wait_ge(itnrow_ok, 4)
            pe.wait_ge(ld_w, 16 * W_LOADS)

            def project(n, i, p):
                pe.wait_ge(ld_x[p], 32 * (i + 1))
                at_least(pe, qkv_read, 3 * n)
                at_least(pe, kcum_read, n)
                for t in range(2):
                    last = pe.matmul(QKV[:, t, 0:3 * P], xT_sb[p][:, t * P:(t + 1) * P], wqkv[:, :], start=True, stop=True)
                last.then_inc(qkv_ps, 1)

            def cum_k(n, p):
                pe.wait_ge(phi_ok, n + 1)
                pe.wait_ge(qkv_read, 3 * (n + 1))
                for t in range(2):
                    last = pe.matmul(QKV[:, t, 3 * P:4 * P], upto[:, :], phi[p][:, t, P:2 * P], start=True, stop=True)
                last.then_inc(kcum_ps, 1)

            def cum_kv(n, u):
                pe.wait_ge(kv_ok, 2 * n + u // 2 + 1)
                at_least(pe, prod_ok, 4 * n + u - 1)
                pe.matmul(CUM[u % 2][:, :], upto[:, :], kv[:, u // 2, (u % 2) * 512:(u % 2 + 1) * 512],
                          start=True, stop=True).then_inc(cum_ps, 1)

            def attend(m):
                pe.wait_ge(prod_ok, 4 * (m + 1))
                at_least(pe, x2T_ok, m)
                for t in range(2):
                    for d in range(HD):
                        last = pe.matmul(TR[:, t * P:(t + 1) * P], prod[:, t, d * P:(d + 1) * P], ident[:, :],
                                         start=(d == 0), stop=(d == HD - 1))
                last.then_inc(oT_ps, 1)

            def out_proj(m):
                pe.wait_ge(oT_ok, m + 1)
                at_least(pe, vT_ok, 2 * m)
                for t in range(2):
                    last = pe.matmul(MM[:, t * P:(t + 1) * P], oT[:, t * P:(t + 1) * P], wo[:, :], start=True, stop=True)
                last.then_inc(y_ps, 1)

            def turn_x1(m):
                pe.wait_ge(x1_ok, 2 * (m + 1))
                for t in range(2):
                    last = pe.transpose(TR[:, t * P:(t + 1) * P], x1[:, t, :], ident[:, :])
                last.then_inc(x1T_ps, 1)

            def cross_v(m):
                pe.wait_ge(x1T_ok, m + 1)
                pe.wait_ge(y_read, m + 1)
                pe.matmul(MM[0:XH, 0:2 * P], wxv[:, :], x1T[:, :], start=True, stop=True).then_inc(vT_ps, 1)

            def cross_dots(m):
                pe.wait_ge(vT_ok, 2 * (m + 1))
                at_least(pe, dot_read, m)
                for t in range(2):
                    pe.matmul(DOT[:, 2 * P + t:2 * P + t + 1], vsq[:, t * P:(t + 1) * P], ones[0:XH, 0:1], start=True, stop=True)
                    last = pe.matmul(DOT[:, t * P:(t + 1) * P], vT[:, t * P:(t + 1) * P],
                                     tT[:, bass.ds(2 * P * m + t * P, P)], start=True, stop=True)
                last.then_inc(dot_ps, 1)

            def turn_x2(m, p):
                pe.wait_ge(x2_ok, 2 * (m + 1))
                pe.wait_ge(x1T_ok, m + 1)
                for t in range(2):
                    last = pe.transpose(TR[:, t * P:(t + 1) * P], x2[p][:, t, :], ident[:, :])
                last.then_inc(x2T_ps, 1)

            def gate(m):
                pe.wait_ge(x2T_ok, m + 1)
                at_least(pe, pos_read, m)
                for t in range(2):
                    last = pe.matmul(GATE[:, t * EXPERTS:(t + 1) * EXPERTS], x2T[:, t * P:(t + 1) * P], gw[:, :],
                                     start=True, stop=True)
                last.then_inc(gate_ps, 1)

            def positions(m, p):
                pe.wait_ge(member_ok, m + 1)
                pe.wait_ge(macc_ok, m + 1)
                for t in range(2):
                    o = GATE[:, (2 + t) * EXPERTS:(3 + t) * EXPERTS]
                    pe.matmul(o, before[:, :], member[p][:, t, :], start=True, stop=False)
                    if t == 1:
                        pe.matmul(o, ones16[:, :], member[p][:, 0, :], start=False, stop=False)
                    last = pe.matmul(o, ones16[:, :], macc[p][:, :], start=False, stop=True)
                last.then_inc(pos_ps, 1)

            def step(n, p, i, s1, s2, s3):
                if s1:
                    project(n, i, p)
                if s3:
                    turn_x2(n - 2, p)
                if s2:
                    attend(n - 1)
                if s3:
                    gate(n - 2)
                if s1:
                    cum_k(n, p)
                    cum_kv(n, 0)
                if s2:
                    out_proj(n - 1)
                if s1:
                    cum_kv(n, 1)
                if s3:
                    positions(n - 2, p)
                if s1:
                    cum_kv(n, 2)
                if s2:
                    turn_x1(n - 1)
                    cross_v(n - 1)
                if s1:
                    cum_kv(n, 3)
                if s2:
                    cross_dots(n - 1)

            pipeline(pe, step)

            pe.wait_ge(vconsts, VCONSTS)
            pe.wait_ge(macc_ok, PAIRS + 1)
            pe.wait_ge(pos_read, PAIRS)
            pe.matmul(GATE[:, 0:EXPERTS], ones16[:, :], macc[PAIRS % 2][:, :], start=True, stop=True).then_inc(cnt_ps, 1)

            pe.wait_ge(w1hi_ok, EXPERTS)
            pe.wait_ge(w1lo_ok, EXPERTS)
            pe.wait_ge(ld_big, 16 * BIG_LOADS)
            pe.wait_ge(table_ok, 3)

            def turn_rows(j, i, r):
                pe.wait_ge(ld_row[r], 16 * (i + 1))
                at_least(pe, xe_ok, j)
                halves16 = xrow[r][:, 0:P].bitcast(F16)
                for c in range(2):
                    last = pe.transpose(XB[:, c * P // 2:(c + 1) * P // 2].bitcast(F16), halves16[:, c * P:(c + 1) * P],
                                        ident16[:, :])
                last.then_inc(xe_ps, 1)

            def layer1(j, i, r):
                e = pe.value_load(e_i[0:1, bass.ds(j, 1)], min_val=0, max_val=EXPERTS - 1)
                pe.wait_ge(xe_ok, j + 1)
                at_least(pe, g_ok, FC * (j - 2))
                for f in range(FC):
                    o = HB[r][:, f * P:(f + 1) * P]
                    hi = w1_hi[:, bass.ds(e * FF + f * P, P)]
                    pe.matmul(o, hi, xeT[r][:, 0:P], start=True, stop=False)
                    pe.matmul(o, hi, xeT[r][:, P:2 * P], start=False, stop=False)
                    last = pe.matmul(o, w1_lo[:, bass.ds(e * FF + f * P, P)], xeT[r][:, 0:P], start=False, stop=True)
                last.then_inc(h_ps, 1)

            def layer2(j, r):
                e = pe.value_load(e_i[0:1, bass.ds(j, 1)], min_val=0, max_val=EXPERTS - 1)
                pe.wait_ge(g_ok, FC * (j + 1))
                at_least(pe, y2_ok, j - 2)
                for f in range(FC):
                    last = pe.matmul(YB[r][:, 0:P], g_sb[r][:, f * P:(f + 1) * P],
                                     w2_sb[:, bass.ds(e * FC * P + f * P, P)], start=(f == 0), stop=(f == FC - 1))
                last.then_inc(y2_ps, 1)

            turn_rows(0, 0, 0)
            for j in range(3):
                if j < 2:
                    turn_rows(j + 1, 0, j + 1)
                else:
                    turn_rows(3, 1, 0)
                layer1(j, 0, j)
                if j:
                    layer2(j - 1, j - 1)
            with pe.Fori(1, SLOTS // 3 - 1) as i:
                for r in range(3):
                    turn_rows(3 * i + r + 1, i + (r + 1) // 3, (r + 1) % 3)
                    layer1(3 * i + r, i, r)
                    layer2(3 * i + r - 1, (r + 2) % 3)
            for j in range(SLOTS - 3, SLOTS):
                if j + 1 < SLOTS:
                    turn_rows(j + 1, (j + 1) // 3, (j + 1) % 3)
                layer1(j, j // 3, j % 3)
                layer2(j - 1, (j - 1) % 3)
            layer2(SLOTS - 1, (SLOTS - 1) % 3)

        @block.scalar
        def _(act):
            act.dma_start(ctx_sb[:, :], ctxT).then_inc(ld_ctx, 16)
            act.dma_start(wt[:, :], w_tT).then_inc(ld_ctx, 16)
            act.dma_start(bt[:, :], b_t).then_inc(ld_ctx, 16)
            for dst, src in ((wqkv, w_qkvT), (wo, w_oT), (wxv, w_xvT), (bv, b_v), (gw, gate_w)):
                act.dma_start(dst[:, :], src).then_inc(ld_w, 16)
            act.preload_act_table(ACT.Exp)
            for c in range(T // 512):
                act.wait_ge(tproj, c + 1)
                cols = slice(c * 512, (c + 1) * 512)
                act.activation(tT[:, cols], bank[c][0:XH, :], ACT.Identity, bias=bt[:, :]).then_inc(tread, 1)
                act.activation(tsq[:, cols], bank[c][0:XH, :], ACT.Square, bias=bt[:, :]).then_inc(tread, 1)
            act.wait_ge(itnT_ps, 1)
            act.activation(itnT[:, :], TR[0:TILES, 0:P], ACT.Copy).then_inc(itnT_ok, 1)
            for c in range(4):
                act.wait_ge(itnrow_ps, c + 1)
                act.activation(itn_row[:, c * 512:(c + 1) * 512], bank[c][:, :], ACT.Copy).then_inc(itnrow_ok, 1)

            def qkv_out(n):
                act.wait_ge(qkv_ps, n + 1)
                at_least(act, phi_ok, n)
                act.activation(e_qk[:, :, :], QKV[:, :, 0:2 * P], ACT.Exp).then_inc(qkv_read, 1)
                act.activation(r_qk[:, :, :], QKV[:, :, 0:2 * P], ACT.Relu).then_inc(qkv_read, 1)
                at_least(act, kv_ok, 2 * n)
                act.activation(v_sb[:, :, :], QKV[:, :, 2 * P:3 * P], ACT.Copy).then_inc(qkv_read, 1)

            def oT_out(m):
                act.wait_ge(oT_ps, m + 1)
                at_least(act, y_ps, m)
                act.activation(oT[:, :], TR[:, 0:2 * P], ACT.Copy).then_inc(oT_ok, 1)

            def norm1(m):
                act.wait_ge(nmr1_ok, m + 1)
                act.wait_ge(rstd1_ok, m + 1)
                at_least(act, x1T_ps, m)
                at_least(act, dot_read, m)
                at_least(act, mv2_ok, 2 * m)
                for t in range(2):
                    act.activation(x1[:, t, :], r1[:, t, :], ACT.Identity, bias=nmr1[:, t:t + 1],
                                   scale=rstd1[:, t:t + 1]).then_inc(x1_ok, 1)

            def x1T_out(m):
                act.wait_ge(x1T_ps, m + 1)
                at_least(act, vT_ps, m)
                act.activation(x1T[:, :], TR[:, 0:2 * P], ACT.Copy).then_inc(x1T_ok, 1)

            def v_out(m):
                act.wait_ge(vT_ps, m + 1)
                at_least(act, dot_ps, m)
                act.activation(vT[:, :], MM[0:XH, 0:2 * P], ACT.Identity, bias=bv[:, :]).then_inc(vT_ok, 1)
                act.activation(vsq[:, :], MM[0:XH, 0:2 * P], ACT.Square, bias=bv[:, :]).then_inc(vT_ok, 1)

            def norm2(m, p, i):
                act.wait_ge(nmr2_ok, m + 1)
                act.wait_ge(rstd2_ok, m + 1)
                at_least(act, kept[p], 16 * i)
                for t in range(2):
                    act.activation(x2[p][:, t, :], r2[p][:, t, :], ACT.Identity, bias=nmr2[:, t:t + 1],
                                   scale=rstd2[:, t:t + 1]).then_inc(x2_ok, 1)

            def x2T_out(m):
                act.wait_ge(x2T_ps, m + 1)
                at_least(act, gate_ps, m)
                act.activation(x2T[:, :], TR[:, 0:2 * P], ACT.Copy).then_inc(x2T_ok, 1)

            def high_half(m, p, i):
                act.wait_ge(x2_ok, 2 * (m + 1))
                at_least(act, scattered[p], 16 * 2 * TOP * i)
                for t in range(2):
                    act.activation(pay[p][:, t, :, 0:P // 2].bitcast(F16),
                                   x2[p][:, t, :].rearrange("p (a c) -> p a c", a=1).broadcast_to([P, TOP, P]),
                                   ACT.Copy).then_inc(hi_ok, 1)

            def gate_exp(m):
                act.wait_ge(gdif_ok, m + 1)
                act.activation(gexp[:, :, :], gdif[:, :, :], ACT.Exp).then_inc(gexp_ok, 1)

            def split_w1(e):
                cols = bass.ds(e * FF, FF)
                act.activation(w1_hi[:, cols], w1_raw[:, cols], ACT.Copy, scale=W1_SCALE).then_inc(w1hi_ok, 1)

            def step(n, p, i, s1, s2, s3):
                if s1:
                    qkv_out(n)
                if s3:
                    norm2(n - 2, p, i - 1)
                    x2T_out(n - 2)
                if s2:
                    oT_out(n - 1)
                if s3:
                    gate_exp(n - 2)
                    high_half(n - 2, p, i - 1)
                if s2:
                    norm1(n - 1)
                    x1T_out(n - 1)
                    v_out(n - 1)
                if s1:
                    split_w1(n)

            act.wait_ge(ld_w1, 16)
            act.preload_act_table(ACT.Exp)
            pipeline(act, step)

            act.preload_act_table(ACT.Gelu)
            act.wait_ge(table_ok, 3)
            act.wait_ge(ld_big, 16 * BIG_LOADS)

            def gelu(j, r):
                e = act.value_load(e_i[0:1, bass.ds(j, 1)], min_val=0, max_val=EXPERTS - 1)
                act.wait_ge(h_ps, j + 1)
                at_least(act, y2_ps, j - 2)
                for f in range(FC):
                    act.activation(g_sb[r][:, f * P:(f + 1) * P], HB[r][:, f * P:(f + 1) * P], ACT.Gelu,
                                   bias=b1_sb[:, bass.ds(e * FC + f, 1)], scale=1.0 / W1_SCALE).then_inc(g_ok, 1)

            for j in range(3):
                gelu(j, j)
            with act.Fori(1, SLOTS // 3) as i:
                for r in range(3):
                    gelu(3 * i + r, r)

            for q in range(QUADS):
                act.wait_ge(nmr3_ok, q + 1)
                act.wait_ge(rstd3_ok, q + 1)
                for t in range(4 * q, 4 * q + 4):
                    act.activation(o_sb[:, t, :], z[:, t, :], ACT.Identity, bias=nmr3[:, t:t + 1],
                                   scale=rstd3[:, t:t + 1]).then_inc(o_ok, 1)

        @block.vector
        def _(dve):
            class Steps:

                def __init__(self, s, total):
                    self.s, self.total, self.at = s, total, 0

                def start(self, m):
                    self.m, self.at = m, 0

                def link(self, ins, apart=False):
                    self.at += 1
                    ins.then_inc(self.s, 1)
                    done = self.m * self.total + self.at
                    if apart:
                        wait_apart(dve, (self.s, done))
                    else:
                        dve.wait_ge(self.s, done)

                def end(self):
                    assert self.at == self.total, self.at

            own1, own2, own3 = Steps(in1, 3), Steps(in2, 7), Steps(in3, 16)

            dve.memset(ones16[:, :], 1.0).then_inc(vconsts, 1)
            dve.memset(macc[0][:, :], 0.0).then_inc(macc_ok, 1)
            dve.wait_ge(consts, CONSTS)
            dve.tensor_copy(ident16[:, :], ident[:, :]).then_inc(vconsts, 1)
            dve.tensor_copy(iota_e[:, :], iota_ei[:, :]).then_inc(vconsts, 1)
            dve.tensor_copy(base_e[:, :], base_ei[:, :]).then_inc(vconsts, 1)
            dve.tensor_copy(iota_j[:, :], iota_ji[:, :]).then_inc(vconsts, 1)
            dve.wait_ge(vconsts, VCONSTS)
            dve.wait_ge(tnorm, 1)
            dve.tensor_scalar(tn2[:, :], GATE[:, 0:TILES], TINY, None, ALU.max).then_inc(tn2_ok, 1)
            dve.wait_ge(itnrow_ok, 4)

            def features(n, p):
                dve.wait_ge(qkv_read, 3 * n + 2)
                dve.scalar_tensor_tensor(out=phi[p][:, :, :], in0=e_qk[:, :, :], scalar=1.0, in1=r_qk[:, :, :],
                                         op0=ALU.min, op1=ALU.add).then_inc(phi_ok, 1)

            def outer(n, p, t):
                dve.wait_ge(qkv_read, 3 * n + 3)
                dve.wait_ge(phi_ok, n + 1)
                k = phi[p][:, t, P:2 * P].rearrange("p (h d o) -> p d h o", d=HD, o=1).broadcast_to([P, HD, HEADS, HD])
                v = v_sb[:, t, :].rearrange("p (o h e) -> p o h e", o=1, e=HD).broadcast_to([P, HD, HEADS, HD])
                dve.tensor_tensor(kv[:, t, :].rearrange("p (d h e) -> p d h e", d=HD, e=HD), k, v, ALU.mult).then_inc(kv_ok, 1)

            def normalize_q(n, p):
                own1.start(n)
                dve.wait_ge(kcum_ps, n + 1)
                dve.tensor_tensor(qk[:, :, :], phi[p][:, :, 0:P], QKV[:, :, 3 * P:4 * P], ALU.mult).then_inc(kcum_read, 1)
                dve.wait_ge(kcum_read, n + 1)
                own1.link(dve.tensor_reduce(norm[:, :], qk[:, :, :].rearrange("p t (h d) -> p (t h) d", d=HD), AX_X, ALU.add))
                own1.link(dve.tensor_scalar(norm[:, :], norm[:, :], NORM_EPS, None, ALU.max))
                own1.link(dve.reciprocal(rnorm[:, :], norm[:, :]))
                dve.tensor_tensor(qn[:, :, :].rearrange("p t (h d) -> p (t h) d", d=HD),
                                  phi[p][:, :, 0:P].rearrange("p t (h d) -> p t h d", d=HD),
                                  rnorm[:, :].rearrange("p (t h o) -> p t h o", t=2, o=1).broadcast_to([P, 2, HEADS, HD]),
                                  ALU.mult).then_inc(qn_ok, 1)
                own1.end()

            def weigh(n, u):
                t, half_u = u // 2, u % 2
                dve.wait_ge(qn_ok, n + 1)
                dve.wait_ge(cum_ps, 4 * n + u + 1)
                at_least(dve, oT_ps, n)
                q = qn[:, t, :].rearrange("p (h d o) -> p d h o", d=HD, o=1)[:, 4 * half_u:4 * half_u + 4, :, :]
                dve.tensor_tensor(prod[:, t, half_u * 512:(half_u + 1) * 512].rearrange("p (d h e) -> p d h e", d=4, e=HD),
                                  q.broadcast_to([P, 4, HEADS, HD]),
                                  CUM[half_u].rearrange("p (d h e) -> p d h e", d=4, e=HD), ALU.mult).then_inc(prod_ok, 1)

            def split_w1(e):
                cols = bass.ds(e * FF, FF)
                dve.wait_ge(w1hi_ok, e + 1)
                dve.scalar_tensor_tensor(out=w1_lo[:, cols], in0=w1_raw[:, cols], scalar=W1_SCALE, in1=w1_hi[:, cols],
                                         op0=ALU.mult, op1=ALU.subtract).then_inc(w1lo_ok, 1)

            def residual1(m, p, i):
                own2.start(m)
                dve.wait_ge(y_ps, m + 1)
                dve.wait_ge(ld_x[p], 32 * (i + 1))
                at_least(dve, x1_ok, 2 * m)
                at_least(dve, ve1_ok, m)
                dve.tensor_tensor(r1[:, :, :], MM[:, 0:2 * P].rearrange("p (t d) -> p t d", t=2), x_sb[p][:, :, :],
                                  ALU.add).then_inc(y_read, 1)
                dve.wait_ge(y_read, m + 1)
                for t in range(2):
                    own2.link(dve.bn_stats(st1[:, t, :], r1[:, t, :]), True)
                for t in range(2):
                    dve.bn_aggr(mv1[:, t, :], st1[:, t, :]).then_inc(mv1_ok, 1)

            def shift1(m):
                dve.wait_ge(rstd1_ok, m + 1)
                dve.wait_ge(mv1_ok, 2 * (m + 1))
                dve.scalar_tensor_tensor(out=nmr1[:, :], in0=mv1[:, :, 0], scalar=-1.0, in1=rstd1[:, :],
                                         op0=ALU.mult, op1=ALU.mult).then_inc(nmr1_ok, 1)

            def cross_norm(m):
                dve.wait_ge(dot_ps, m + 1)
                dve.tensor_scalar(vn2[:, :], DOT[:, 2 * P:2 * P + 2], TINY, None, ALU.max).then_inc(vn2_ok, 1)

            def cross(m, p):
                dve.wait_ge(ivn_ok, m + 1)
                for t in range(2):
                    own2.link(dve.tensor_scalar(wcos[:, t, :], itn_row[:, bass.ds(2 * P * m + t * P, P)], ivn[:, t:t + 1],
                                                COS_CAP, ALU.mult, ALU.min))
                dve.tensor_tensor(ucos[:, :, :], wcos[:, :, :], DOT[:, 0:2 * P].rearrange("p (t d) -> p t d", t=2),
                                  ALU.mult).then_inc(dot_read, 1)
                dve.wait_ge(dot_read, m + 1)
                dve.wait_ge(x1_ok, 2 * (m + 1))
                at_least(dve, x2_ok, 2 * (m - 1))
                own2.link(dve.tensor_tensor(r2[p][:, :, :], ucos[:, :, :], x1[:, :, :], ALU.add))
                for t in range(2):
                    own2.link(dve.bn_stats(st2[:, t, :], r2[p][:, t, :]), True)
                for t in range(2):
                    dve.bn_aggr(mv2[p][:, t, :], st2[:, t, :]).then_inc(mv2_ok, 1)
                own2.end()

            def shift2(m, p):
                dve.wait_ge(rstd2_ok, m + 1)
                dve.wait_ge(mv2_ok, 2 * (m + 1))
                at_least(dve, x2_ok, 2 * m)
                dve.scalar_tensor_tensor(out=nmr2[:, :], in0=mv2[p][:, :, 0], scalar=-1.0, in1=rstd2[:, :],
                                         op0=ALU.mult, op1=ALU.mult).then_inc(nmr2_ok, 1)

            def gate_shift(m):
                own3.start(m)
                dve.wait_ge(gate_ps, m + 1)
                logits = GATE[:, 0:2 * EXPERTS].rearrange("p (t e) -> p t e", t=2)
                own3.link(dve.tensor_reduce(gmax[:, :], logits, AX_X, ALU.max))
                dve.tensor_tensor(gdif[:, :, :], logits, over_experts(gmax), ALU.subtract).then_inc(gdif_ok, 1)

            def over_experts(a):
                return a[:, :].rearrange("p (t o) -> p t o", o=1).broadcast_to([P, 2, EXPERTS])

            def payload(m, p, i):
                dve.wait_ge(hi_ok, 2 * (m + 1))
                dve.wait_ge(x2_ok, 2 * (m + 1))
                at_least(dve, scattered[p], 16 * 2 * TOP * i)
                rows16 = pay[p][:, :, :, 0:P].bitcast(F16)
                both = x2[p][:, :, :].rearrange("p t (o d) -> p t o d", o=1).broadcast_to([P, 2, TOP, P])
                dve.tensor_tensor(rows16[:, :, :, P:2 * P], both, rows16[:, :, :, 0:P], ALU.subtract).then_inc(pay_ok, 1)
                dve.tensor_copy(pay[p][:, :, :, P].bitcast(I32), returns[:, bass.ds(2 * m, 2), :]).then_inc(pay_ok, 1)

            def choose(m, p):
                dve.wait_ge(gexp_ok, m + 1)
                own3.link(dve.tensor_reduce(gsum[:, :], gexp[:, :, :], AX_X, ALU.add))
                own3.link(dve.reciprocal(rgsum[:, :], gsum[:, :]))
                own3.link(dve.tensor_tensor(score[:, :, :], gexp[:, :, :], over_experts(rgsum), ALU.mult), True)
                for t in range(2):
                    own3.link(dve.max(top8[:, t, :], score[:, t, :]), True)
                for t in range(2):
                    own3.link(dve.max_index(idx8[:, t, :], top8[:, t, :], score[:, t, :]), t == 0)
                own3.link(dve.tensor_copy(chosen[:, :, :], idx8[:, :, 0:TOP]))
                own3.link(dve.tensor_tensor(
                    onehot[:, :, :],
                    iota_e[:, :].rearrange("p (o e) -> p o e", o=1).broadcast_to([P, 2 * TOP, EXPERTS]),
                    chosen[:, :, :].rearrange("p t (k o) -> p (t k) o", o=1).broadcast_to([P, 2 * TOP, EXPERTS]),
                    ALU.is_equal))
                hot = onehot[:, :, :].rearrange("p (t k) e -> p t k e", k=TOP)
                dve.tensor_tensor(member[p][:, :, :], hot[:, :, 0, :], hot[:, :, 1, :], ALU.add).then_inc(member_ok, 1)
                own3.link(dve.tensor_tensor(wsum[:, :], top8[:, :, 0], top8[:, :, 1], ALU.add))
                own3.link(dve.reciprocal(rwsum[:, :], wsum[:, :]))
                own3.link(dve.tensor_tensor(w_all[:, bass.ds(2 * m, 2), :], top8[:, :, 0:TOP],
                                            rwsum[:, :].rearrange("p (t o) -> p t o", o=1).broadcast_to([P, 2, TOP]), ALU.mult))
                dve.wait_ge(member_ok, m + 1)
                own3.link(dve.tensor_tensor(msum[:, :], member[p][:, 0, :], member[p][:, 1, :], ALU.add))
                dve.tensor_tensor(macc[1 - p][:, :], macc[p][:, :], msum[:, :], ALU.add).then_inc(macc_ok, 1)

            def rows(m, p):
                dve.wait_ge(pos_ps, m + 1)
                dve.tensor_tensor(place[:, :, :], GATE[:, 2 * EXPERTS:4 * EXPERTS].rearrange("p (t e) -> p t e", t=2),
                                  base_e[:, :].rearrange("p (o e) -> p o e", o=1).broadcast_to([P, 2, EXPERTS]),
                                  ALU.add).then_inc(pos_read, 1)
                dve.wait_ge(pos_read, m + 1)
                own3.link(dve.tensor_tensor(
                    placed[:, :, :].rearrange("p (t k) e -> p t k e", k=TOP),
                    onehot[:, :, :].rearrange("p (t k) e -> p t k e", k=TOP),
                    place[:, :, :].rearrange("p t (o e) -> p t o e", o=1).broadcast_to([P, 2, TOP, EXPERTS]), ALU.mult))
                own3.link(dve.tensor_reduce(rowf[:, :], placed[:, :, :], AX_X, ALU.add))
                dve.tensor_copy(rowi[p][:, :], rowf[:, :]).then_inc(row_ok, 1)
                own3.end()

            def step(n, p, i, s1, s2, s3):
                if s3:
                    shift2(n - 2, p)
                if s1:
                    features(n, p)
                    outer(n, p, 0)
                    outer(n, p, 1)
                if s3:
                    gate_shift(n - 2)
                if s1:
                    normalize_q(n, p)
                if s3:
                    choose(n - 2, p)
                if s1:
                    weigh(n, 0)
                if s2:
                    residual1(n - 1, 1 - p, i + p - 1)
                if s1:
                    weigh(n, 1)
                if s2:
                    shift1(n - 1)
                if s3:
                    payload(n - 2, p, i - 1)
                    rows(n - 2, p)
                if s1:
                    weigh(n, 2)
                    split_w1(n)
                    weigh(n, 3)
                if s2:
                    cross_norm(n - 1)
                    cross(n - 1, 1 - p)

            pipeline(dve, step)

            own = Steps(tsteps, 0)
            own.start(0)
            dve.wait_ge(cnt_ps, 1)
            dve.tensor_copy(cnt_i[:, :], GATE[:, 0:EXPERTS]).then_inc(table_ok, 1)
            dve.wait_ge(table_ok, 1)
            own.link(dve.tensor_scalar(cup_i[:, :], cnt_i[:, :], float(P - 1), None, ALU.add))
            own.link(dve.tensor_scalar(nt_i[:, :], cup_i[:, :], P.bit_length() - 1, None, ALU.logical_shift_right))
            own.link(dve.tensor_copy(nt[:, :], nt_i[:, :]))
            own.link(dve.tensor_tensor_scan(ntc[:, :], ones[:, 0:EXPERTS], nt[:, :], 0.0, ALU.mult, ALU.add))
            own.link(dve.tensor_tensor(
                past[:, :, :], ntc[:, :].rearrange("p (o e) -> p o e", o=1).broadcast_to([P, SLOTS, EXPERTS]),
                iota_j[:, :].rearrange("p (j o) -> p j o", o=1).broadcast_to([P, SLOTS, EXPERTS]), ALU.is_le))
            own.link(dve.tensor_reduce(ej[:, :], past[:, :, :], AX_X, ALU.add))
            own.link(dve.tensor_tensor(
                pnt[:, :, :], past[:, :, :], nt[:, :].rearrange("p (o e) -> p o e", o=1).broadcast_to([P, SLOTS, EXPERTS]),
                ALU.mult))
            own.link(dve.tensor_reduce(first_j[:, :], pnt[:, :, :], AX_X, ALU.add))
            own.link(dve.tensor_tensor(off_j[:, :], iota_j[:, :], first_j[:, :], ALU.subtract))
            own.link(dve.tensor_scalar(off128[:, :], off_j[:, :], float(P), None, ALU.mult))
            own.link(dve.scalar_tensor_tensor(out=row_j[:, :], in0=ej[:, :], scalar=float(CAP), in1=off128[:, :],
                                              op0=ALU.mult, op1=ALU.add))
            dve.tensor_copy(row_i[:, :], row_j[:, :]).then_inc(table_ok, 1)
            dve.tensor_scalar(e_i[:, :], ej[:, :], float(EXPERTS - 1), None, ALU.min).then_inc(table_ok, 1)
            dve.wait_ge(table_ok, 3)
            dve.wait_ge(ld_big, 16 * BIG_LOADS)

            def take(j, i, r):
                dve.wait_ge(xe_ps, j + 1)
                at_least(dve, h_ps, j - 2)
                dve.tensor_copy(xeT[r][:, :], XB[:, 0:P].bitcast(F16)).then_inc(xe_ok, 1)
                dve.wait_ge(ld_row[r], 16 * (i + 1))
                at_least(dve, returned[r], 16 * i)
                dve.tensor_copy(ridx[r][:, :], xrow[r][:, P:ROW].bitcast(I32)).then_inc(ridx_ok, 1)

            def give(j, i, r):
                e = dve.value_load(e_i[0:1, bass.ds(j, 1)], min_val=0, max_val=EXPERTS - 1)
                dve.wait_ge(y2_ps, j + 1)
                at_least(dve, returned[r], 16 * i)
                dve.tensor_tensor(y_sb[r][:, :], YB[r][:, 0:P], b2_sb[:, bass.ds(e * P, P)], ALU.add).then_inc(y2_ok, 1)

            take(0, 0, 0)
            take(1, 0, 1)
            for j in range(3):
                take(j + 2, (j + 2) // 3, (j + 2) % 3)
                give(j, 0, j)
            with dve.Fori(1, SLOTS // 3 - 1) as i:
                for r in range(3):
                    take(3 * i + r + 2, i + (r + 2) // 3, (r + 2) % 3)
                    give(3 * i + r, i, r)
            for j in range(SLOTS - 3, SLOTS):
                if j + 2 < SLOTS:
                    take(j + 2, (j + 2) // 3, (j + 2) % 3)
                give(j, j // 3, j % 3)

            for p in range(2):
                dve.wait_ge(kept[p], 16 * (PAIRS // 2))
            def shift3(q):
                t0, t1 = 4 * q, 4 * q + 4
                dve.wait_ge(rstd3_ok, q + 1)
                dve.scalar_tensor_tensor(out=nmr3[:, t0:t1], in0=mv3[:, t0:t1, 0], scalar=-1.0, in1=rstd3[:, t0:t1],
                                         op0=ALU.mult, op1=ALU.mult).then_inc(nmr3_ok, 1)

            done = 0
            for q in range(QUADS):
                quad = range(4 * q, 4 * q + 4)
                dve.wait_ge(ld_y[q], 16 * TOP)
                for t in quad:
                    dve.scalar_tensor_tensor(out=z1[:, t, :], in0=y_in[:, 0, t, :], scalar=w_all[:, t, 0:1],
                                             in1=x2_all[:, t, :], op0=ALU.mult, op1=ALU.add).then_inc(zsteps, 1)
                for k, t in enumerate(quad):
                    dve.wait_ge(zsteps, done + k + 1)
                    dve.scalar_tensor_tensor(out=z[:, t, :], in0=y_in[:, 1, t, :], scalar=w_all[:, t, 1:2],
                                             in1=z1[:, t, :], op0=ALU.mult, op1=ALU.add).then_inc(zsteps, 1)
                for k, t in enumerate(quad):
                    dve.wait_ge(zsteps, done + 4 + k + 1)
                    dve.bn_stats(st3[:, t, :], z[:, t, :]).then_inc(zsteps, 1)
                for k, t in enumerate(quad):
                    dve.wait_ge(zsteps, done + 8 + k + 1)
                    dve.bn_aggr(mv3[:, t, :], st3[:, t, :]).then_inc(mv3_ok, 1)
                done += 12
                if q:
                    shift3(q - 1)
            shift3(QUADS - 1)


def kernel(x, ctx_768, L0_attn_Wq, L0_attn_Wk, L0_attn_Wv, L0_attn_Wo, L0_xattn_Wv, L0_xattn_bv, L0_xattn_Wt, L0_xattn_bt,
           L0_ffn_gate_w, L0_ffn_w1, L0_ffn_b1, L0_ffn_w2, L0_ffn_b2):
    import numpy as np
    import concourse.bacc as bacc
    from concourse.bass_utils import run_bass_kernel_spmd

    def flat(a):
        a = np.asarray(a)
        return a.reshape(-1, a.shape[-1])

    def columns(a):
        return np.ascontiguousarray(np.asarray(a).T)

    batch, seq, hidden = np.shape(x)
    experts, ff = np.shape(L0_ffn_b1)
    arrays = {
        "x": np.ascontiguousarray(flat(x)),
        "xT": columns(flat(x)),
        "ctxT": columns(flat(ctx_768)),
        "w_qkvT": np.ascontiguousarray(np.concatenate([np.asarray(w) for w in (L0_attn_Wq, L0_attn_Wk, L0_attn_Wv)]).T),
        "w_oT": columns(L0_attn_Wo),
        "w_xvT": columns(L0_xattn_Wv),
        "b_v": np.ascontiguousarray(np.asarray(L0_xattn_bv).reshape(-1, 1)),
        "w_tT": columns(L0_xattn_Wt),
        "b_t": np.ascontiguousarray(np.asarray(L0_xattn_bt).reshape(-1, 1)),
        "gate_w": np.ascontiguousarray(L0_ffn_gate_w),
        "w1": np.ascontiguousarray(L0_ffn_w1),
        "b1T": columns(np.asarray(L0_ffn_b1).reshape(experts * ff // 128, 128)),
        "w2": np.ascontiguousarray(L0_ffn_w2),
        "b2": np.ascontiguousarray(L0_ffn_b2),
    }
    nc = bacc.Bacc("TRN2", target_bir_lowering=False, num_devices=1)
    ins = {n: nc.dram_tensor(f"{n}_dram", a.shape, mybir.dt.from_np(a.dtype), kind="ExternalInput").ap()
           for n, a in arrays.items()}
    out = nc.dram_tensor("out_dram", (batch * seq, hidden), mybir.dt.float32, kind="ExternalOutput").ap()
    decoder_layer(nc, **ins, out=out)
    r = run_bass_kernel_spmd(nc, [{f"{n}_dram": a for n, a in arrays.items()}], core_ids=[0])
    return r.results[0]["out_dram"].reshape(batch, seq, hidden)
```

```python
from contextlib import ExitStack

import concourse.bass as bass
from concourse import mybir

F32 = mybir.dt.float32
F16 = mybir.dt.float16
BF16 = mybir.dt.bfloat16
I32 = mybir.dt.int32
U32 = mybir.dt.uint32
ALU = mybir.AluOpType
ACT = mybir.ActivationFunctionType
AX_X = mybir.AxisListType.X

P = 128
HEADS, HD = 16, 8
EXPERTS, TOP = 8, 2
LN_EPS = 1e-5
NORM_EPS = 1e-6
COS_CAP = 1e8
TINY = 1e-30
W1_SCALE = 16.0


def decoder_layer(nc, x, xT, ctxT, w_qkvT, w_oT, w_xvT, b_v, w_tT, b_t, gate_w, w1, b1T, w2, b2, out):
    T = x.shape[0]
    TILES = T // P
    PAIRS = TILES // 2
    CD, XH = ctxT.shape[0], w_tT.shape[1]
    FF = w1.shape[2]
    FC = FF // P
    ET = 2 * P
    SLOTS = TOP * T // ET + EXPERTS - 1
    RING = 4
    assert RING % 2 == 0 and PAIRS % 2 == 0
    CAP = T + ET
    DUMMIES = EXPERTS - 1
    PADS = (EXPERTS + DUMMIES) * ET // P
    ROW = P + 1
    SCAN = HEADS * HD * HD

    x_rows = nc.dram_tensor("x_rows", (EXPERTS * CAP + DUMMIES * ET, ROW), F32, kind="Internal").ap()
    y_rows = nc.dram_tensor("y_rows", (TOP * T + PADS * P, P), F32, kind="Internal").ap()

    with ExitStack() as ctx:
        def sb(name, shape, dt=F32):
            return ctx.enter_context(nc.sbuf_tensor(name, shape, dt))

        def sem(name):
            return ctx.enter_context(nc.semaphore(name))

        wqkv = sb("wqkv", [P, 3 * P])
        wo = sb("wo", [P, P])
        wxv = sb("wxv", [P, XH])
        bv = sb("bv", [XH, 1])
        wt = sb("wt", [CD, XH])
        bt = sb("bt", [XH, 1])
        gw = sb("gw", [P, EXPERTS])
        ctx_sb = sb("ctx_sb", [CD, T])
        w1_raw = sb("w1_raw", [P, EXPERTS * FF])
        w1_hi = sb("w1_hi", [P, EXPERTS * FF], F16)
        w1_lo = sb("w1_lo", [P, EXPERTS * FF], F16)
        b1_sb = sb("b1_sb", [P, EXPERTS * FC])
        w2_sb = sb("w2_sb", [P, EXPERTS * FC * P])
        b2_sb = sb("b2_sb", [P, EXPERTS * P])
        ident = sb("ident", [P, P])
        ident16 = sb("ident16", [P, P], F16)
        upto = sb("upto", [P, P])
        before = sb("before", [P, P], BF16)
        ones = sb("ones", [P, P])
        ones16 = sb("ones16", [P, P], BF16)
        half = sb("half", [P, TILES])
        iota_e = sb("iota_e", [P, EXPERTS])
        base_e = sb("base_e", [P, EXPERTS])
        iota_j = sb("iota_j", [P, SLOTS])
        iota_ei = sb("iota_ei", [P, EXPERTS], I32)
        base_ei = sb("base_ei", [P, EXPERTS], I32)
        iota_ji = sb("iota_ji", [P, SLOTS], I32)
        returns = sb("returns", [P, TILES, TOP], I32)
        pick = sb("pick", [TILES, TILES, P])
        padding = sb("padding", [P, PADS, ROW])
        tT = sb("tT", [XH, T])
        tsq = sb("tsq", [XH, T])
        tn2 = sb("tn2", [P, TILES])
        itn = sb("itn", [P, TILES])
        itnT = sb("itnT", [TILES, P])
        itn_row = sb("itn_row", [P, T])
        xT_sb = [sb(f"xT_sb{p}", [P, 2 * P]) for p in range(2)]
        x_sb = [sb(f"x_sb{p}", [P, 2, P]) for p in range(2)]
        e_qk = sb("e_qk", [P, 2, 2 * P])
        r_qk = sb("r_qk", [P, 2, 2 * P])
        v_sb = sb("v_sb", [P, 2, P])
        phi = [sb(f"phi{p}", [P, 2, 2 * P]) for p in range(2)]
        kv = sb("kv", [P, 2, SCAN])
        qk = sb("qk", [P, 2, P])
        norm = sb("norm", [P, 2 * HEADS])
        normf = sb("normf", [P, 2 * HEADS])
        rnorm = sb("rnorm", [P, 2 * HEADS])
        qn = sb("qn", [P, 2, P])
        prod = sb("prod", [P, 2, SCAN])
        oT = sb("oT", [P, 2 * P])
        r1 = sb("r1", [P, 2, P])
        st1 = sb("st1", [P, 2, 6])
        mv1 = sb("mv1", [P, 2, 2])
        ve1 = sb("ve1", [P, 2])
        rstd1 = sb("rstd1", [P, 2])
        nmr1 = sb("nmr1", [P, 2])
        x1 = sb("x1", [P, 2, P])
        x1T = sb("x1T", [P, 2 * P])
        vT = sb("vT", [XH, 2 * P])
        vsq = sb("vsq", [XH, 2 * P])
        vn2 = sb("vn2", [P, 2])
        ivn = sb("ivn", [P, 2])
        wcos = sb("wcos", [P, 2, P])
        ucos = sb("ucos", [P, 2, P])
        r2 = [sb(f"r2{p}", [P, 2, P]) for p in range(2)]
        st2 = sb("st2", [P, 2, 6])
        mv2 = [sb(f"mv2{p}", [P, 2, 2]) for p in range(2)]
        ve2 = sb("ve2", [P, 2])
        rstd2 = sb("rstd2", [P, 2])
        nmr2 = sb("nmr2", [P, 2])
        x2 = [sb(f"x2{p}", [P, 2, P]) for p in range(2)]
        x2_all = sb("x2_all", [P, TILES, P])
        x2T = sb("x2T", [P, 2 * P])
        gmax = sb("gmax", [P, 2])
        gdif = sb("gdif", [P, 2, EXPERTS])
        gexp = sb("gexp", [P, 2, EXPERTS])
        gsum = sb("gsum", [P, 2])
        rgsum = sb("rgsum", [P, 2])
        score = sb("score", [P, 2, EXPERTS])
        top8 = sb("top8", [P, 2, EXPERTS])
        idx8 = sb("idx8", [P, 2, EXPERTS], U32)
        wsum = sb("wsum", [P, 2])
        rwsum = sb("rwsum", [P, 2])
        w_all = sb("w_all", [P, TILES, TOP])
        chosen = sb("chosen", [P, 2, TOP])
        onehot = sb("onehot", [P, 2 * TOP, EXPERTS])
        member = [sb(f"member{p}", [P, 2, EXPERTS], BF16) for p in range(2)]
        macc = [sb(f"macc{p}", [P, EXPERTS], BF16) for p in range(2)]
        msum = sb("msum", [P, EXPERTS], BF16)
        place = sb("place", [P, 2, EXPERTS])
        placed = sb("placed", [P, 2 * TOP, EXPERTS])
        rowf = sb("rowf", [P, 2 * TOP])
        rowi = [sb(f"rowi{p}", [P, 2 * TOP], I32) for p in range(2)]
        pay = [sb(f"pay{p}", [P, 2, TOP, ROW]) for p in range(2)]
        cnt = sb("cnt", [P, EXPERTS])
        cnt_i = sb("cnt_i", [P, EXPERTS], I32)
        cup_i = sb("cup_i", [P, EXPERTS], I32)
        nt_i = sb("nt_i", [P, EXPERTS], I32)
        nt = sb("nt", [P, EXPERTS])
        ntc = sb("ntc", [P, EXPERTS])
        past = sb("past", [P, SLOTS, EXPERTS])
        pnt = sb("pnt", [P, SLOTS, EXPERTS])
        ej = sb("ej", [P, SLOTS])
        first_j = sb("first_j", [P, SLOTS])
        off_j = sb("off_j", [P, SLOTS])
        off_rows = sb("off_rows", [P, SLOTS])
        row_j = sb("row_j", [P, SLOTS])
        ejc = sb("ejc", [P, SLOTS])
        row_i = sb("row_i", [P, SLOTS], I32)
        e_i = sb("e_i", [P, SLOTS], I32)
        def cut_up(buffer, width):
            flat = buffer[:, :, :].rearrange("p t c -> p (t c)")
            return [flat[:, r * 2 * width:(r + 1) * 2 * width].rearrange("p (t c) -> p t c", t=2) for r in range(RING)]

        xrow = cut_up(kv, ROW)
        y_sb = cut_up(prod, P)
        ridx = [sb(f"ridx{r}", [P, 2], I32) for r in range(RING)]
        xeT = [sb(f"xeT{r}", [P, 2 * ET], F16) for r in range(2)]
        g_sb = [sb(f"g_sb{r}", [P, FC * ET]) for r in range(2)]
        y_in = sb("y_in", [P, TOP, TILES, P])
        z1 = w1_raw[:, 0:TILES * P].rearrange("p (t d) -> p t d", d=P)
        z = w1_raw[:, TILES * P:2 * TILES * P].rearrange("p (t d) -> p t d", d=P)
        st3 = sb("st3", [P, TILES, 6])
        mv3 = sb("mv3", [P, TILES, 2])
        ve3 = sb("ve3", [P, TILES])
        rstd3 = sb("rstd3", [P, TILES])
        nmr3 = sb("nmr3", [P, TILES])
        o_sb = itn_row[:, :].rearrange("p (t d) -> p t d", d=P)

        ps = ctx.enter_context(nc.psum_tensor("ps", [P, 8, 512], F32))
        bank = [ps[:, b, :] for b in range(8)]
        QKV = ps[:, 0:2, :]
        CUM = [bank[2], bank[3]]
        TR, MM, DOT, GATE = bank[4], bank[5], bank[6], bank[7]
        HB = [[bank[2 * h + f // 2][:, f % 2 * ET:(f % 2 + 1) * ET] for f in range(FC)] for h in range(2)]
        XB = [bank[4], bank[5]]
        YB = [bank[6], bank[7]]

        ld_w, ld_ctx, ld_big, ld_w1 = sem("ld_w"), sem("ld_ctx"), sem("ld_big"), sem("ld_w1")
        ld_x = [sem(f"ld_x{p}") for p in range(2)]
        ld_xT = [sem(f"ld_xT{p}") for p in range(2)]
        consts, vconsts = sem("consts"), sem("vconsts")
        tproj, tread, tnorm, tn2_ok, itn_ok, itnT_ps, itnT_ok, itnrow_ps, itnrow_ok = (
            sem(n) for n in ("tproj", "tread", "tnorm", "tn2_ok", "itn_ok", "itnT_ps", "itnT_ok", "itnrow_ps", "itnrow_ok"))
        w1s_ok, w1hi_ok, w1lo_ok = sem("w1s_ok"), sem("w1hi_ok"), sem("w1lo_ok")
        qkv_ps, qkv_read, phi_ok, kv_ok, kcum_ps, kcum_read, qn_ok, cum_ps, prod_ok = (
            sem(n) for n in ("qkv_ps", "qkv_read", "phi_ok", "kv_ok", "kcum_ps", "kcum_read", "qn_ok", "cum_ps", "prod_ok"))
        oT_ps, oT_ok, y_ps, y_read, mv1_ok, ve1_ok, rstd1_ok, nmr1_ok, x1_ok, x1T_ps, x1T_ok, vT_ps, vT_ok = (
            sem(n) for n in ("oT_ps", "oT_ok", "y_ps", "y_read", "mv1_ok", "ve1_ok", "rstd1_ok", "nmr1_ok", "x1_ok", "x1T_ps",
                             "x1T_ok", "vT_ps", "vT_ok"))
        dot_ps, vn2_ok, ivn_ok, dot_read, mv2_ok, ve2_ok, rstd2_ok, nmr2_ok, x2_ok, x2T_ps, x2T_ok = (
            sem(n) for n in ("dot_ps", "vn2_ok", "ivn_ok", "dot_read", "mv2_ok", "ve2_ok", "rstd2_ok", "nmr2_ok", "x2_ok",
                             "x2T_ps", "x2T_ok"))
        gate_ps, gdif_ok, gexp_ok, member_ok, macc_ok, pos_ps, pos_read, row_ok, hi_ok, pay_ok = (
            sem(n) for n in ("gate_ps", "gdif_ok", "gexp_ok", "member_ok", "macc_ok", "pos_ps", "pos_read", "row_ok", "hi_ok",
                             "pay_ok"))
        apart, w_ok, msum_ok = sem("apart"), sem("w_ok"), sem("msum_ok")
        sent = sem("sent")
        kept = [sem(f"kept{p}") for p in range(2)]
        scattered = [sem(f"scattered{p}") for p in range(2)]
        norm_in, st1_in, wcos_ok, r2_ok, st2_in, gate_in, row_in = (
            sem(n) for n in ("norm_in", "st1_in", "wcos_ok", "r2_ok", "st2_in", "gate_in", "row_in"))
        cnt_ps, table_ok, tsteps, filled = sem("cnt_ps"), sem("table_ok"), sem("tsteps"), sem("filled")
        ld_row = [sem(f"ld_row{r}") for r in range(RING)]
        xe_ps, xe_ok, ridx_ok, h_ps, g_ok, y2_ps, y2_ok = (
            sem(n) for n in ("xe_ps", "xe_ok", "ridx_ok", "h_ps", "g_ok", "y2_ps", "y2_ok"))
        returned = [sem(f"returned{r}") for r in range(RING)]
        QUADS = TILES // 4
        ld_y = [sem(f"ld_y{q}") for q in range(QUADS)]
        zsteps, mv3_ok, ve3_ok, rstd3_ok, nmr3_ok, o_ok, stored = (
            sem(n) for n in ("zsteps", "mv3_ok", "ve3_ok", "rstd3_ok", "nmr3_ok", "o_ok", "stored"))

        CONSTS = 16
        VCONSTS = 5
        W_LOADS, CTX_LOADS, BIG_LOADS = 5, 3, 3
        xT_dram = xT.rearrange("d (n c) -> d n c", c=2 * P)
        x_dram = x.rearrange("(n t p) d -> p n t d", t=2, p=P)
        out_dram = out.rearrange("(t p) d -> p t d", p=P)
        y_dram = y_rows[0:TOP * T, :].rearrange("(k t p) d -> p k t d", k=TOP, p=P)

        def pipeline(eng, step):
            for n in range(3):
                step(n, n % 2, n // 2, True, True, n >= 1, n >= 2)
            with eng.Fori(1, (PAIRS - 2) // 2) as i:
                step(2 * i + 1, 1, i, True, True, True, True)
                step(2 * i + 2, 0, i + 1, True, True, True, True)
            for n in range(PAIRS - 1, PAIRS + 2):
                step(n, n % 2, n // 2, n + 1 < PAIRS, n < PAIRS, n <= PAIRS, True)

        def expert_tiles(eng, step, behind=0):
            for j in range(RING):
                step(j, 0, j)
            with eng.Fori(1, SLOTS // RING) as i:
                for r in range(RING):
                    step(RING * i + r, i, r)
            for j in range(SLOTS // RING * RING, SLOTS + behind):
                step(j, j // RING, j % RING)

        def near(j, i, r, d):
            return j + d, i + (r + d) // RING, (r + d) % RING

        def there(j):
            return not isinstance(j, int) or 0 <= j < SLOTS

        def wait_apart(eng, *pairs):
            for s, value in pairs:
                at_least(eng, s, value)
            eng.sem_inc(apart, 1)

        def at_least(eng, s, value):
            if not isinstance(value, int) or value > 0:
                eng.wait_ge(s, value)

        block = ctx.enter_context(nc.Block())

        @block.sync
        def _(sp):
            def load_xT(n, p):
                at_least(sp, qkv_ps, n - 1)
                sp.dma_start(xT_sb[p][:, :], xT_dram[:, n, :]).then_inc(ld_xT[p], 16)

            def load_x(n, p):
                at_least(sp, y_read, n - 1)
                sp.dma_start(x_sb[p][:, :, :], x_dram[:, n, :, :]).then_inc(ld_x[p], 16)

            def keep_x2(m, p):
                sp.wait_ge(x2_ok, 2 * (m + 1))
                sp.dma_start(x2_all[:, bass.ds(2 * m, 2), :], x2[p][:, :, :]).then_inc(kept[p], 16)

            sp.sem_inc(kept[0], 16)
            sp.sem_inc(kept[1], 16)
            load_xT(0, 0)
            sp.dma_start(w1_raw[:, :].rearrange("p (e f) -> p e f", e=EXPERTS),
                         w1.rearrange("e d f -> d e f")).then_inc(ld_w1, 16)
            sp.dma_start(w2_sb[:, :].rearrange("p (a d) -> p a d", d=P),
                         w2.rearrange("e (c p) d -> p (e c) d", p=P)).then_inc(ld_big, 16)
            sp.dma_start(b1_sb[:, :], b1T).then_inc(ld_big, 16)
            sp.dma_start(b2_sb[:, :], b2.rearrange("(a e) d -> a (e d)", a=1).broadcast_to([P, EXPERTS * P])).then_inc(ld_big, 16)
            sp.wait_ge(consts, CONSTS)
            sp.dma_start(x_rows[EXPERTS * CAP:, :].rearrange("(r p) c -> p r c", p=P),
                         padding[:, EXPERTS * ET // P:, :]).then_inc(filled, 16)

            def step(n, p, h, s0, s1, s2, s3):
                if s0:
                    load_xT(n + 1, 1 - p)
                if s1:
                    load_x(n, p)
                if s3:
                    keep_x2(n - 2, p)

            pipeline(sp, step)

            sp.wait_ge(table_ok, 1)
            for e in range(EXPERTS):
                n_e = sp.value_load(cnt_i[0:1, e:e + 1], min_val=0, max_val=T)
                sp.dma_start(x_rows[bass.ds(n_e + e * CAP, ET), :].rearrange("(t p) c -> p t c", p=P),
                             padding[:, e * ET // P:(e + 1) * ET // P, :]).then_inc(filled, 16)
            sp.wait_ge(filled, 16 * (EXPERTS + 1))
            for p in range(2):
                sp.wait_ge(scattered[p], 16 * 2 * TOP * (PAIRS // 2))
            sp.wait_ge(table_ok, 3)

            def load_row(j, i, r):
                at_least(sp, xe_ps, j - RING + 1)
                at_least(sp, ridx_ok, j - RING + 1)
                row = sp.value_load(row_i[0:1, bass.ds(j, 1)], min_val=0, max_val=EXPERTS * CAP + (DUMMIES - 1) * ET)
                sp.dma_start(xrow[r], x_rows[bass.ds(row, ET), :].rearrange("(t p) c -> p t c", p=P)).then_inc(ld_row[r], 16)

            expert_tiles(sp, load_row)

            for r in range(RING):
                sp.wait_ge(returned[r], 2 * 16 * len(range(r, SLOTS, RING)))
            for q in range(QUADS):
                for k in range(TOP):
                    sp.dma_start(y_in[:, k, 4 * q:4 * q + 4, :], y_dram[:, k, 4 * q:4 * q + 4, :]).then_inc(ld_y[q], 16)
            for q in range(QUADS):
                sp.wait_ge(o_ok, 4 * (q + 1))
                sp.dma_start(out_dram[:, 4 * q:4 * q + 4, :], o_sb[:, 4 * q:4 * q + 4, :]).then_inc(stored, 16)
            sp.wait_ge(stored, 16 * QUADS)

        @block.gpsimd
        def _(pool):
            pool.memset(ident[:, :], 0.0).then_inc(consts, 1)
            pool.memset(upto[:, :], 1.0).then_inc(consts, 1)
            pool.memset(before[:, :], 1.0).then_inc(consts, 1)
            pool.memset(ones[:, :], 1.0).then_inc(consts, 1)
            pool.memset(half[:, :], -0.5).then_inc(consts, 1)
            pool.wait_ge(consts, 5)
            pool.affine_select(out=ident[:, :], in_=ident[:, :], compare_op=ALU.not_equal, fill=1.0, base=0,
                               pattern=[[-1, P]], channel_multiplier=1).then_inc(consts, 1)
            pool.affine_select(out=upto[:, :], in_=upto[:, :], compare_op=ALU.is_ge, fill=0.0, base=0,
                               pattern=[[1, P]], channel_multiplier=-1).then_inc(consts, 1)
            pool.affine_select(out=before[:, :], in_=before[:, :], compare_op=ALU.is_gt, fill=0.0, base=0,
                               pattern=[[1, P]], channel_multiplier=-1).then_inc(consts, 1)
            pool.memset(pick[:, :, :], 1.0).then_inc(consts, 1)
            pool.memset(padding[:, :, :], 0.0).then_inc(consts, 1)
            pool.wait_ge(consts, 10)
            pool.affine_select(out=pick[:, :, :], in_=pick[:, :, :], compare_op=ALU.is_equal, fill=0.0, base=0,
                               pattern=[[1, TILES], [0, P]], channel_multiplier=-1).then_inc(consts, 1)
            pool.iota(padding[:, :, P:ROW].bitcast(I32), [[P, PADS]], base=TOP * T, channel_multiplier=1).then_inc(consts, 1)
            pool.iota(returns[:, :, :], [[P, TILES], [T, TOP]], base=0, channel_multiplier=1).then_inc(consts, 1)
            pool.iota(iota_ei[:, :], [[1, EXPERTS]], base=0, channel_multiplier=0).then_inc(consts, 1)
            pool.iota(base_ei[:, :], [[CAP, EXPERTS]], base=0, channel_multiplier=0).then_inc(consts, 1)
            pool.iota(iota_ji[:, :], [[1, SLOTS]], base=0, channel_multiplier=0).then_inc(consts, 1)
            pool.wait_ge(tn2_ok, 1)
            pool.tensor_tensor(itn[:, :], tn2[:, :], half[:, :], ALU.pow).then_inc(itn_ok, 1)

            def rstd1_of(m):
                wait_apart(pool, (mv1_ok, 2 * (m + 1)), (nmr1_ok, m), (x1_ok, 2 * m))
                pool.tensor_scalar(ve1[:, :], mv1[:, :, 1], LN_EPS, None, ALU.add).then_inc(ve1_ok, 1)
                pool.wait_ge(ve1_ok, m + 1)
                pool.tensor_tensor(rstd1[:, :], ve1[:, :], half[:, 0:2], ALU.pow).then_inc(rstd1_ok, 1)

            def ivn_of(m):
                pool.wait_ge(vn2_ok, m + 1)
                pool.tensor_tensor(ivn[:, :], vn2[:, :], half[:, 0:2], ALU.pow).then_inc(ivn_ok, 1)

            def rstd2_of(m, p):
                wait_apart(pool, (mv2_ok, 2 * (m + 1)), (nmr2_ok, m), (x2_ok, 2 * m))
                pool.tensor_scalar(ve2[:, :], mv2[p][:, :, 1], LN_EPS, None, ALU.add).then_inc(ve2_ok, 1)
                pool.wait_ge(ve2_ok, m + 1)
                pool.tensor_tensor(rstd2[:, :], ve2[:, :], half[:, 0:2], ALU.pow).then_inc(rstd2_ok, 1)

            def sent_before(m, p, h):
                pool.wait_ge(scattered[1 - p], 16 * 2 * TOP * (h + p))
                pool.sem_inc(sent, 1)

            def scatter(m, p):
                wait_apart(pool, (row_ok, m + 1), (pay_ok, 2 * (m + 1)))
                for c in range(2 * TOP):
                    pool.indirect_dma_start(x_rows, bass.IndirectOffsetOnAxis(ap=rowi[p][:, c:c + 1], axis=0),
                                            pay[p][:, c // TOP, c % TOP, :], None).then_inc(scattered[p], 16)

            def low_w1(e):
                cols = bass.ds(e * FF, FF)
                pool.wait_ge(w1hi_ok, e + 1)
                pool.tensor_tensor(w1_lo[:, cols], w1_raw[:, cols], w1_hi[:, cols], ALU.subtract).then_inc(w1lo_ok, 1)

            pool.sem_inc(sent, 1)

            def step(n, p, h, s0, s1, s2, s3):
                if s3:
                    ivn_of(n - 2)
                    rstd2_of(n - 2, p)
                if s2:
                    rstd1_of(n - 1)
                if s1:
                    low_w1(n)
                if s3 and not (isinstance(n, int) and n == 2):
                    sent_before(n - 2, p, h - 1)
                if s3:
                    scatter(n - 2, p)

            pipeline(pool, step)

            def give_back(j, i, r):
                wait_apart(pool, (y2_ok, j + 1), (ridx_ok, j + 1))
                for t in range(2):
                    pool.indirect_dma_start(y_rows, bass.IndirectOffsetOnAxis(ap=ridx[r][:, t:t + 1], axis=0),
                                            y_sb[r][:, t, :], None).then_inc(returned[r], 16)

            expert_tiles(pool, give_back)

            for q in range(QUADS):
                t0, t1 = 4 * q, 4 * q + 4
                pool.wait_ge(mv3_ok, t1)
                pool.tensor_scalar(ve3[:, t0:t1], mv3[:, t0:t1, 1], LN_EPS, None, ALU.add).then_inc(ve3_ok, 1)
                pool.wait_ge(ve3_ok, q + 1)
                pool.tensor_tensor(rstd3[:, t0:t1], ve3[:, t0:t1], half[:, 0:4], ALU.pow).then_inc(rstd3_ok, 1)

        @block.tensor
        def _(pe):
            pe.wait_ge(ld_ctx, 16 * CTX_LOADS)
            for c in range(T // 512):
                pe.matmul(bank[c][0:XH, :], wt[:, :], ctx_sb[:, c * 512:(c + 1) * 512], start=True, stop=True).then_inc(tproj, 1)
            pe.wait_ge(consts, CONSTS)
            pe.wait_ge(tread, 2 * (T // 512))
            for b in range(TILES):
                last = pe.matmul(GATE[:, b:b + 1], tsq[:, b * P:(b + 1) * P], ones[0:XH, 0:1], start=True, stop=True)
            last.then_inc(tnorm, 1)
            pe.wait_ge(itn_ok, 1)
            pe.transpose(TR[0:TILES, 0:P], itn[:, :], ident[:, :]).then_inc(itnT_ps, 1)
            pe.wait_ge(itnT_ok, 1)
            for b in range(TILES):
                last = pe.matmul(bank[b // 4][:, (b % 4) * P:(b % 4 + 1) * P], pick[:, b, :], itnT[:, :], start=True, stop=True)
                if b % 4 == 3:
                    last.then_inc(itnrow_ps, 1)
            pe.wait_ge(itnrow_ok, 4)
            pe.wait_ge(ld_w, 16 * W_LOADS)

            def project(n, p, h):
                pe.wait_ge(ld_xT[p], 16 * (h + 1))
                at_least(pe, qkv_read, 3 * n)
                at_least(pe, kcum_read, n)
                for t in range(2):
                    last = pe.matmul(QKV[:, t, 0:3 * P], xT_sb[p][:, t * P:(t + 1) * P], wqkv[:, :], start=True, stop=True)
                last.then_inc(qkv_ps, 1)

            def cum_k(n, p):
                pe.wait_ge(phi_ok, n + 1)
                pe.wait_ge(qkv_read, 3 * (n + 1))
                for t in range(2):
                    last = pe.matmul(QKV[:, t, 3 * P:4 * P], upto[:, :], phi[p][:, t, P:2 * P], start=True, stop=True)
                last.then_inc(kcum_ps, 1)

            def cum_kv(n, u):
                pe.wait_ge(kv_ok, 2 * n + u // 2 + 1)
                at_least(pe, prod_ok, 4 * n + u - 1)
                pe.matmul(CUM[u % 2][:, :], upto[:, :], kv[:, u // 2, (u % 2) * 512:(u % 2 + 1) * 512],
                          start=True, stop=True).then_inc(cum_ps, 1)

            def attend(m, t):
                pe.wait_ge(prod_ok, 4 * m + 2 * t + 2)
                at_least(pe, x1T_ok, m)
                for d in range(HD):
                    last = pe.matmul(TR[:, t * P:(t + 1) * P], prod[:, t, d * P:(d + 1) * P], ident[:, :],
                                     start=(d == 0), stop=(d == HD - 1))
                last.then_inc(oT_ps, 1)

            def out_proj(m):
                pe.wait_ge(oT_ok, m + 1)
                at_least(pe, vT_ok, 2 * m)
                at_least(pe, x2T_ok, m)
                for t in range(2):
                    last = pe.matmul(MM[:, t * P:(t + 1) * P], oT[:, t * P:(t + 1) * P], wo[:, :], start=True, stop=True)
                last.then_inc(y_ps, 1)

            def turn_x1(m):
                pe.wait_ge(x1_ok, 2 * (m + 1))
                pe.wait_ge(oT_ok, m + 1)
                for t in range(2):
                    last = pe.transpose(TR[:, t * P:(t + 1) * P], x1[:, t, :], ident[:, :])
                last.then_inc(x1T_ps, 1)

            def cross_v(m):
                pe.wait_ge(x1T_ok, m + 1)
                pe.wait_ge(y_read, m + 1)
                pe.matmul(MM[0:XH, 0:2 * P], wxv[:, :], x1T[:, :], start=True, stop=True).then_inc(vT_ps, 1)

            def cross_dots(m):
                pe.wait_ge(vT_ok, 2 * (m + 1))
                at_least(pe, dot_read, m)
                for t in range(2):
                    pe.matmul(DOT[:, 2 * P + t:2 * P + t + 1], vsq[:, t * P:(t + 1) * P], ones[0:XH, 0:1], start=True, stop=True)
                    last = pe.matmul(DOT[:, t * P:(t + 1) * P], vT[:, t * P:(t + 1) * P],
                                     tT[:, bass.ds(2 * P * m + t * P, P)], start=True, stop=True)
                last.then_inc(dot_ps, 1)

            def turn_x2(m, p):
                pe.wait_ge(x2_ok, 2 * (m + 1))
                pe.wait_ge(vT_ok, 2 * (m + 1))
                pe.wait_ge(y_read, m + 1)
                for t in range(2):
                    last = pe.transpose(MM[:, t * P:(t + 1) * P], x2[p][:, t, :], ident[:, :])
                last.then_inc(x2T_ps, 1)

            def gate(m):
                pe.wait_ge(x2T_ok, m + 1)
                at_least(pe, pos_read, m)
                for t in range(2):
                    last = pe.matmul(GATE[:, t * EXPERTS:(t + 1) * EXPERTS], x2T[:, t * P:(t + 1) * P], gw[:, :],
                                     start=True, stop=True)
                last.then_inc(gate_ps, 1)

            def positions(m, p):
                pe.wait_ge(member_ok, m + 1)
                pe.wait_ge(macc_ok, m + 1)
                for t in range(2):
                    o = GATE[:, (2 + t) * EXPERTS:(3 + t) * EXPERTS]
                    pe.matmul(o, before[:, :], member[p][:, t, :], start=True, stop=False)
                    if t == 1:
                        pe.matmul(o, ones16[:, :], member[p][:, 0, :], start=False, stop=False)
                    last = pe.matmul(o, ones16[:, :], macc[p][:, :], start=False, stop=True)
                last.then_inc(pos_ps, 1)

            def step(n, p, h, s0, s1, s2, s3):
                if s2:
                    attend(n - 1, 0)
                if s1:
                    cum_k(n, p)
                if s2:
                    attend(n - 1, 1)
                if s1:
                    cum_kv(n, 0)
                if s3:
                    turn_x2(n - 2, p)
                if s2:
                    out_proj(n - 1)
                if s1:
                    cum_kv(n, 1)
                if s3:
                    gate(n - 2)
                if s0:
                    project(n + 1, 1 - p, h + p)
                if s1:
                    cum_kv(n, 2)
                    cum_kv(n, 3)
                if s2:
                    turn_x1(n - 1)
                    cross_v(n - 1)
                if s3:
                    positions(n - 2, p)
                if s2:
                    cross_dots(n - 1)

            project(0, 0, 0)
            pipeline(pe, step)

            pe.wait_ge(vconsts, VCONSTS)
            pe.wait_ge(macc_ok, PAIRS + 1)
            pe.wait_ge(pos_read, PAIRS)
            pe.matmul(GATE[:, 0:EXPERTS], ones16[:, :], macc[PAIRS % 2][:, :], start=True, stop=True).then_inc(cnt_ps, 1)

            pe.wait_ge(w1hi_ok, EXPERTS)
            pe.wait_ge(w1lo_ok, EXPERTS)
            pe.wait_ge(ld_big, 16 * BIG_LOADS)
            pe.wait_ge(table_ok, 3)

            def turn_rows(j, i, r):
                pe.wait_ge(ld_row[r], 16 * (i + 1))
                at_least(pe, xe_ok, j - 1)
                for c in range(2):
                    for t in range(2):
                        half_row = xrow[r][:, t, 0:P].bitcast(F16)[:, c * P:(c + 1) * P]
                        last = pe.transpose(XB[r % 2][:, (2 * c + t) * P // 2:(2 * c + t + 1) * P // 2].bitcast(F16),
                                            half_row, ident16[:, :])
                last.then_inc(xe_ps, 1)

            def expert_of(j):
                return pe.value_load(e_i[0:1, bass.ds(j, 1)], min_val=0, max_val=EXPERTS - 1)

            def layer1(j, i, r, e):
                pe.wait_ge(xe_ok, j + 1)
                at_least(pe, g_ok, FC * (j - 1))
                for f in range(FC):
                    o = HB[r % 2][f]
                    hi = w1_hi[:, bass.ds(e * FF + f * P, P)]
                    pe.matmul(o, hi, xeT[r % 2][:, 0:ET], start=True, stop=False)
                    pe.matmul(o, hi, xeT[r % 2][:, ET:2 * ET], start=False, stop=False)
                    last = pe.matmul(o, w1_lo[:, bass.ds(e * FF + f * P, P)], xeT[r % 2][:, 0:ET], start=False, stop=True)
                last.then_inc(h_ps, 1)

            def layer2(j, i, r, e):
                pe.wait_ge(g_ok, FC * (j + 1))
                at_least(pe, y2_ok, j - 1)
                for t in range(2):
                    for f in range(FC):
                        g = g_sb[r % 2][:, f * ET + t * P:f * ET + (t + 1) * P]
                        last = pe.matmul(YB[r % 2][:, t * P:(t + 1) * P], g, w2_sb[:, bass.ds(e * FF + f * P, P)],
                                         start=(f == 0), stop=(f == FC - 1))
                last.then_inc(y2_ps, 1)

            experts = [None] * RING

            def expert_tile(j, i, r):
                if there(j + 1):
                    turn_rows(*near(j, i, r, 1))
                if there(j):
                    experts[r] = expert_of(j)
                    layer1(j, i, r, experts[r])
                if there(j - 1):
                    layer2(*near(j, i, r, -1), experts[r - 1] if r else expert_of(j - 1))

            turn_rows(0, 0, 0)
            expert_tiles(pe, expert_tile, behind=1)

        @block.scalar
        def _(act):
            act.dma_start(ctx_sb[:, :], ctxT).then_inc(ld_ctx, 16)
            act.dma_start(wt[:, :], w_tT).then_inc(ld_ctx, 16)
            act.dma_start(bt[:, :], b_t).then_inc(ld_ctx, 16)
            for dst, src in ((wqkv, w_qkvT), (wo, w_oT), (wxv, w_xvT), (bv, b_v), (gw, gate_w)):
                act.dma_start(dst[:, :], src).then_inc(ld_w, 16)
            act.preload_act_table(ACT.Exp)
            for c in range(T // 512):
                act.wait_ge(tproj, c + 1)
                cols = slice(c * 512, (c + 1) * 512)
                act.activation(tT[:, cols], bank[c][0:XH, :], ACT.Identity, bias=bt[:, :]).then_inc(tread, 1)
                act.activation(tsq[:, cols], bank[c][0:XH, :], ACT.Square, bias=bt[:, :]).then_inc(tread, 1)
            act.wait_ge(itnT_ps, 1)
            act.activation(itnT[:, :], TR[0:TILES, 0:P], ACT.Copy).then_inc(itnT_ok, 1)
            for c in range(4):
                act.wait_ge(itnrow_ps, c + 1)
                act.activation(itn_row[:, c * 512:(c + 1) * 512], bank[c][:, :], ACT.Copy).then_inc(itnrow_ok, 1)

            def qkv_out(n):
                act.wait_ge(qkv_ps, n + 1)
                at_least(act, phi_ok, n)
                act.activation(e_qk[:, :, :], QKV[:, :, 0:2 * P], ACT.Exp).then_inc(qkv_read, 1)
                act.activation(r_qk[:, :, :], QKV[:, :, 0:2 * P], ACT.Relu).then_inc(qkv_read, 1)
                at_least(act, kv_ok, 2 * n)
                act.activation(v_sb[:, :, :], QKV[:, :, 2 * P:3 * P], ACT.Copy).then_inc(qkv_read, 1)

            def oT_out(m):
                act.wait_ge(oT_ps, 2 * (m + 1))
                at_least(act, y_ps, m)
                act.activation(oT[:, :], TR[:, 0:2 * P], ACT.Copy).then_inc(oT_ok, 1)

            def norm1(m):
                act.wait_ge(nmr1_ok, m + 1)
                act.wait_ge(rstd1_ok, m + 1)
                at_least(act, x1T_ps, m)
                at_least(act, r2_ok, m)
                for t in range(2):
                    act.activation(x1[:, t, :], r1[:, t, :], ACT.Identity, bias=nmr1[:, t:t + 1],
                                   scale=rstd1[:, t:t + 1]).then_inc(x1_ok, 1)

            def x1T_out(m):
                act.wait_ge(x1T_ps, m + 1)
                at_least(act, vT_ps, m)
                act.activation(x1T[:, :], TR[:, 0:2 * P], ACT.Copy).then_inc(x1T_ok, 1)

            def v_out(m):
                act.wait_ge(vT_ps, m + 1)
                at_least(act, dot_ps, m)
                act.activation(vT[:, :], MM[0:XH, 0:2 * P], ACT.Identity, bias=bv[:, :]).then_inc(vT_ok, 1)
                act.activation(vsq[:, :], MM[0:XH, 0:2 * P], ACT.Square, bias=bv[:, :]).then_inc(vT_ok, 1)

            def norm2(m, p, i):
                act.wait_ge(nmr2_ok, m + 1)
                act.wait_ge(rstd2_ok, m + 1)
                act.wait_ge(kept[p], 16 * (i + 1))
                for t in range(2):
                    act.activation(x2[p][:, t, :], r2[p][:, t, :], ACT.Identity, bias=nmr2[:, t:t + 1],
                                   scale=rstd2[:, t:t + 1]).then_inc(x2_ok, 1)

            def x2T_out(m):
                act.wait_ge(x2T_ps, m + 1)
                at_least(act, gate_ps, m)
                act.activation(x2T[:, :], MM[:, 0:2 * P], ACT.Copy).then_inc(x2T_ok, 1)

            def high_half(m, p):
                act.wait_ge(x2_ok, 2 * (m + 1))
                at_least(act, sent, m)
                for t in range(2):
                    act.activation(pay[p][:, t, :, 0:P // 2].bitcast(F16),
                                   x2[p][:, t, :].rearrange("p (a c) -> p a c", a=1).broadcast_to([P, TOP, P]),
                                   ACT.Copy).then_inc(hi_ok, 1)

            def gate_exp(m):
                act.wait_ge(gdif_ok, m + 1)
                act.activation(gexp[:, :, :], gdif[:, :, :], ACT.Exp).then_inc(gexp_ok, 1)

            def cosine_scale(m):
                act.wait_ge(ivn_ok, m + 1)
                for t in range(2):
                    act.activation(wcos[:, t, :], itn_row[:, bass.ds(2 * P * m + t * P, P)], ACT.Copy,
                                   scale=ivn[:, t:t + 1]).then_inc(wcos_ok, 1)

            def high_w1(e):
                cols = bass.ds(e * FF, FF)
                act.activation(w1_raw[:, cols], w1_raw[:, cols], ACT.Copy, scale=W1_SCALE).then_inc(w1s_ok, 1)
                act.wait_ge(w1s_ok, e + 1)
                act.activation(w1_hi[:, cols], w1_raw[:, cols], ACT.Copy).then_inc(w1hi_ok, 1)

            def step(n, p, h, s0, s1, s2, s3):
                if s3:
                    cosine_scale(n - 2)
                if s2:
                    oT_out(n - 1)
                if s3:
                    norm2(n - 2, p, h - 1)
                    x2T_out(n - 2)
                if s0:
                    qkv_out(n + 1)
                if s3:
                    high_half(n - 2, p)
                    gate_exp(n - 2)
                if s2:
                    norm1(n - 1)
                    x1T_out(n - 1)
                if s1:
                    high_w1(n)
                if s2:
                    v_out(n - 1)

            act.wait_ge(ld_w1, 16)
            act.preload_act_table(ACT.Exp)
            qkv_out(0)
            pipeline(act, step)

            act.preload_act_table(ACT.Gelu)
            act.wait_ge(table_ok, 3)
            act.wait_ge(ld_big, 16 * BIG_LOADS)

            def gelu(j, i, r):
                e = act.value_load(e_i[0:1, bass.ds(j, 1)], min_val=0, max_val=EXPERTS - 1)
                act.wait_ge(h_ps, j + 1)
                at_least(act, y2_ps, j - 1)
                for f in range(FC):
                    act.activation(g_sb[r % 2][:, f * ET:(f + 1) * ET], HB[r % 2][f], ACT.Gelu,
                                   bias=b1_sb[:, bass.ds(e * FC + f, 1)], scale=1.0 / W1_SCALE).then_inc(g_ok, 1)

            expert_tiles(act, gelu)

            for q in range(QUADS):
                act.wait_ge(nmr3_ok, q + 1)
                act.wait_ge(rstd3_ok, q + 1)
                for t in range(4 * q, 4 * q + 4):
                    act.activation(o_sb[:, t, :], z[:, t, :], ACT.Identity, bias=nmr3[:, t:t + 1],
                                   scale=rstd3[:, t:t + 1]).then_inc(o_ok, 1)

        @block.vector
        def _(dve):
            def link(s, count, ins):
                ins.then_inc(s, 1)
                dve.wait_ge(s, count)

            dve.memset(ones16[:, :], 1.0).then_inc(vconsts, 1)
            dve.memset(macc[0][:, :], 0.0).then_inc(macc_ok, 1)
            dve.wait_ge(consts, CONSTS)
            dve.tensor_copy(ident16[:, :], ident[:, :]).then_inc(vconsts, 1)
            dve.tensor_copy(iota_e[:, :], iota_ei[:, :]).then_inc(vconsts, 1)
            dve.tensor_copy(base_e[:, :], base_ei[:, :]).then_inc(vconsts, 1)
            dve.tensor_copy(iota_j[:, :], iota_ji[:, :]).then_inc(vconsts, 1)
            dve.wait_ge(vconsts, VCONSTS)
            dve.wait_ge(tnorm, 1)
            dve.tensor_scalar(tn2[:, :], GATE[:, 0:TILES], TINY, None, ALU.max).then_inc(tn2_ok, 1)
            dve.wait_ge(itnrow_ok, 4)

            def features(n, p):
                dve.wait_ge(qkv_read, 3 * n + 2)
                dve.scalar_tensor_tensor(out=phi[p][:, :, :], in0=e_qk[:, :, :], scalar=1.0, in1=r_qk[:, :, :],
                                         op0=ALU.min, op1=ALU.add).then_inc(phi_ok, 1)

            def outer(n, p, t):
                dve.wait_ge(qkv_read, 3 * n + 3)
                dve.wait_ge(phi_ok, n + 1)
                k = phi[p][:, t, P:2 * P].rearrange("p (h d o) -> p d h o", d=HD, o=1).broadcast_to([P, HD, HEADS, HD])
                v = v_sb[:, t, :].rearrange("p (o h e) -> p o h e", o=1, e=HD).broadcast_to([P, HD, HEADS, HD])
                dve.tensor_tensor(kv[:, t, :].rearrange("p (d h e) -> p d h e", d=HD, e=HD), k, v, ALU.mult).then_inc(kv_ok, 1)

            def q_dot_sum(n, p):
                dve.wait_ge(kcum_ps, n + 1)
                dve.tensor_tensor(qk[:, :, :], phi[p][:, :, 0:P], QKV[:, :, 3 * P:4 * P], ALU.mult).then_inc(kcum_read, 1)

            def norm_sum(n):
                dve.wait_ge(kcum_read, n + 1)
                dve.tensor_reduce(norm[:, :], qk[:, :, :].rearrange("p t (h d) -> p (t h) d", d=HD), AX_X,
                                  ALU.add).then_inc(norm_in, 1)

            def norm_floor(n):
                dve.wait_ge(norm_in, 3 * n + 1)
                dve.tensor_scalar(normf[:, :], norm[:, :], NORM_EPS, None, ALU.max).then_inc(norm_in, 1)

            def norm_inverse(n):
                dve.wait_ge(norm_in, 3 * n + 2)
                dve.reciprocal(rnorm[:, :], normf[:, :]).then_inc(norm_in, 1)

            def normalize_q(n, p):
                dve.wait_ge(norm_in, 3 * n + 3)
                dve.tensor_tensor(qn[:, :, :].rearrange("p t (h d) -> p (t h) d", d=HD),
                                  phi[p][:, :, 0:P].rearrange("p t (h d) -> p t h d", d=HD),
                                  rnorm[:, :].rearrange("p (t h o) -> p t h o", t=2, o=1).broadcast_to([P, 2, HEADS, HD]),
                                  ALU.mult).then_inc(qn_ok, 1)

            def weigh(n, u):
                t, half_u = u // 2, u % 2
                dve.wait_ge(qn_ok, n + 1)
                dve.wait_ge(cum_ps, 4 * n + u + 1)
                at_least(dve, oT_ps, 2 * n)
                q = qn[:, t, :].rearrange("p (h d o) -> p d h o", d=HD, o=1)[:, 4 * half_u:4 * half_u + 4, :, :]
                dve.tensor_tensor(prod[:, t, half_u * 512:(half_u + 1) * 512].rearrange("p (d h e) -> p d h e", d=4, e=HD),
                                  q.broadcast_to([P, 4, HEADS, HD]),
                                  CUM[half_u].rearrange("p (d h e) -> p d h e", d=4, e=HD), ALU.mult).then_inc(prod_ok, 1)

            def residual1(m, p, h):
                dve.wait_ge(y_ps, m + 1)
                dve.wait_ge(ld_x[p], 16 * (h + 1))
                at_least(dve, x1_ok, 2 * m)
                dve.tensor_tensor(r1[:, :, :], MM[:, 0:2 * P].rearrange("p (t d) -> p t d", t=2), x_sb[p][:, :, :],
                                  ALU.add).then_inc(y_read, 1)

            def stats1(m, t):
                dve.wait_ge(y_read, m + 1)
                dve.bn_stats(st1[:, t, :], r1[:, t, :]).then_inc(st1_in, 1)

            def moments1(m):
                wait_apart(dve, (st1_in, 2 * (m + 1)), (ve1_ok, m))
                for t in range(2):
                    dve.bn_aggr(mv1[:, t, :], st1[:, t, :]).then_inc(mv1_ok, 1)

            def shift1(m):
                dve.wait_ge(rstd1_ok, m + 1)
                dve.wait_ge(mv1_ok, 2 * (m + 1))
                dve.scalar_tensor_tensor(out=nmr1[:, :], in0=mv1[:, :, 0], scalar=-1.0, in1=rstd1[:, :],
                                         op0=ALU.mult, op1=ALU.mult).then_inc(nmr1_ok, 1)

            def cross_norm(m):
                dve.wait_ge(dot_ps, m + 1)
                dve.tensor_scalar(vn2[:, :], DOT[:, 2 * P:2 * P + 2], TINY, None, ALU.max).then_inc(vn2_ok, 1)

            def cosines(m):
                dve.wait_ge(wcos_ok, 2 * (m + 1))
                dve.scalar_tensor_tensor(out=ucos[:, :, :], in0=wcos[:, :, :], scalar=COS_CAP,
                                         in1=DOT[:, 0:2 * P].rearrange("p (t d) -> p t d", t=2),
                                         op0=ALU.min, op1=ALU.mult).then_inc(dot_read, 1)

            def residual2(m, p):
                dve.wait_ge(dot_read, m + 1)
                dve.wait_ge(x1_ok, 2 * (m + 1))
                at_least(dve, x2_ok, 2 * m)
                dve.tensor_tensor(r2[p][:, :, :], ucos[:, :, :], x1[:, :, :], ALU.add).then_inc(r2_ok, 1)

            def stats2(m, p, t):
                dve.wait_ge(r2_ok, m + 1)
                dve.bn_stats(st2[:, t, :], r2[p][:, t, :]).then_inc(st2_in, 1)

            def moments2(m, p):
                wait_apart(dve, (st2_in, 2 * (m + 1)), (ve2_ok, m))
                for t in range(2):
                    dve.bn_aggr(mv2[p][:, t, :], st2[:, t, :]).then_inc(mv2_ok, 1)

            def shift2(m, p):
                dve.wait_ge(rstd2_ok, m + 1)
                dve.wait_ge(mv2_ok, 2 * (m + 1))
                at_least(dve, x2_ok, 2 * m)
                dve.scalar_tensor_tensor(out=nmr2[:, :], in0=mv2[p][:, :, 0], scalar=-1.0, in1=rstd2[:, :],
                                         op0=ALU.mult, op1=ALU.mult).then_inc(nmr2_ok, 1)

            def over_experts(a):
                return a[:, :].rearrange("p (t o) -> p t o", o=1).broadcast_to([P, 2, EXPERTS])

            logits = GATE[:, 0:2 * EXPERTS].rearrange("p (t e) -> p t e", t=2)
            G = 12

            def gate_max(m):
                dve.wait_ge(gate_ps, m + 1)
                dve.tensor_reduce(gmax[:, :], logits, AX_X, ALU.max).then_inc(gate_in, 1)

            def gate_shift(m):
                dve.wait_ge(gate_in, G * m + 1)
                dve.tensor_tensor(gdif[:, :, :], logits, over_experts(gmax), ALU.subtract).then_inc(gdif_ok, 1)

            def gate_sum(m):
                dve.wait_ge(gexp_ok, m + 1)
                dve.tensor_reduce(gsum[:, :], gexp[:, :, :], AX_X, ALU.add).then_inc(gate_in, 1)

            def gate_inverse(m):
                dve.wait_ge(gate_in, G * m + 2)
                dve.reciprocal(rgsum[:, :], gsum[:, :]).then_inc(gate_in, 1)

            def gate_scores(m):
                dve.wait_ge(gate_in, G * m + 3)
                dve.tensor_tensor(score[:, :, :], gexp[:, :, :], over_experts(rgsum), ALU.mult).then_inc(gate_in, 1)

            def gate_top(m):
                wait_apart(dve, (gate_in, G * m + 4))
                for t in range(2):
                    dve.max(top8[:, t, :], score[:, t, :]).then_inc(gate_in, 1)

            def gate_index(m):
                wait_apart(dve, (gate_in, G * m + 6))
                for t in range(2):
                    dve.max_index(idx8[:, t, :], top8[:, t, :], score[:, t, :]).then_inc(gate_in, 1)

            def gate_chosen(m):
                dve.wait_ge(gate_in, G * m + 8)
                dve.tensor_copy(chosen[:, :, :], idx8[:, :, 0:TOP]).then_inc(gate_in, 1)

            def gate_weight_sum(m):
                dve.wait_ge(gate_in, G * m + 6)
                dve.tensor_tensor(wsum[:, :], top8[:, :, 0], top8[:, :, 1], ALU.add).then_inc(gate_in, 1)

            def gate_onehot(m):
                dve.wait_ge(gate_in, G * m + 9)
                dve.tensor_tensor(
                    onehot[:, :, :],
                    iota_e[:, :].rearrange("p (o e) -> p o e", o=1).broadcast_to([P, 2 * TOP, EXPERTS]),
                    chosen[:, :, :].rearrange("p t (k o) -> p (t k) o", o=1).broadcast_to([P, 2 * TOP, EXPERTS]),
                    ALU.is_equal).then_inc(gate_in, 1)

            def gate_weight_inverse(m):
                dve.wait_ge(gate_in, G * m + 10)
                dve.reciprocal(rwsum[:, :], wsum[:, :]).then_inc(gate_in, 1)

            def gate_members(m, p):
                dve.wait_ge(gate_in, G * m + 11)
                hot = onehot[:, :, :].rearrange("p (t k) e -> p t k e", k=TOP)
                dve.tensor_tensor(member[p][:, :, :], hot[:, :, 0, :], hot[:, :, 1, :], ALU.add).then_inc(member_ok, 1)

            def gate_weights(m):
                dve.wait_ge(gate_in, G * m + 12)
                dve.tensor_tensor(w_all[:, bass.ds(2 * m, 2), :], top8[:, :, 0:TOP],
                                  rwsum[:, :].rearrange("p (t o) -> p t o", o=1).broadcast_to([P, 2, TOP]),
                                  ALU.mult).then_inc(w_ok, 1)

            def members_sum(m, p):
                dve.wait_ge(member_ok, m + 1)
                dve.tensor_tensor(msum[:, :], member[p][:, 0, :], member[p][:, 1, :], ALU.add).then_inc(msum_ok, 1)

            def members_count(m, p):
                dve.wait_ge(msum_ok, m + 1)
                dve.tensor_tensor(macc[1 - p][:, :], macc[p][:, :], msum[:, :], ALU.add).then_inc(macc_ok, 1)

            def payload(m, p):
                dve.wait_ge(hi_ok, 2 * (m + 1))
                dve.wait_ge(x2_ok, 2 * (m + 1))
                at_least(dve, sent, m)
                rows16 = pay[p][:, :, :, 0:P].bitcast(F16)
                both = x2[p][:, :, :].rearrange("p t (o d) -> p t o d", o=1).broadcast_to([P, 2, TOP, P])
                dve.tensor_tensor(rows16[:, :, :, P:2 * P], both, rows16[:, :, :, 0:P], ALU.subtract).then_inc(pay_ok, 1)
                dve.tensor_copy(pay[p][:, :, :, P].bitcast(I32), returns[:, bass.ds(2 * m, 2), :]).then_inc(pay_ok, 1)

            def row_base(m):
                dve.wait_ge(pos_ps, m + 1)
                dve.tensor_tensor(place[:, :, :], GATE[:, 2 * EXPERTS:4 * EXPERTS].rearrange("p (t e) -> p t e", t=2),
                                  base_e[:, :].rearrange("p (o e) -> p o e", o=1).broadcast_to([P, 2, EXPERTS]),
                                  ALU.add).then_inc(pos_read, 1)

            def row_pick(m):
                dve.wait_ge(pos_read, m + 1)
                dve.tensor_tensor(
                    placed[:, :, :].rearrange("p (t k) e -> p t k e", k=TOP),
                    onehot[:, :, :].rearrange("p (t k) e -> p t k e", k=TOP),
                    place[:, :, :].rearrange("p t (o e) -> p t o e", o=1).broadcast_to([P, 2, TOP, EXPERTS]),
                    ALU.mult).then_inc(row_in, 1)

            def row_sum(m):
                dve.wait_ge(row_in, 2 * m + 1)
                dve.tensor_reduce(rowf[:, :], placed[:, :, :], AX_X, ALU.add).then_inc(row_in, 1)

            def row_index(m, p):
                dve.wait_ge(row_in, 2 * m + 2)
                dve.tensor_copy(rowi[p][:, :], rowf[:, :]).then_inc(row_ok, 1)

            def step(n, p, h, s0, s1, s2, s3):
                m2, m3 = n - 1, n - 2
                if s3:
                    cross_norm(m3)
                if s1:
                    features(n, p)
                    outer(n, p, 0)
                if s3:
                    cosines(m3)
                if s1:
                    q_dot_sum(n, p)
                if s3:
                    residual2(m3, p)
                if s1:
                    norm_sum(n)
                if s3:
                    stats2(m3, p, 0)
                    stats2(m3, p, 1)
                if s1:
                    norm_floor(n)
                if s3:
                    moments2(m3, p)
                if s1:
                    norm_inverse(n)
                    outer(n, p, 1)
                if s3:
                    shift2(m3, p)
                if s1:
                    normalize_q(n, p)
                if s2:
                    residual1(m2, 1 - p, h - 1 + p)
                if s1:
                    weigh(n, 0)
                if s2:
                    stats1(m2, 0)
                    stats1(m2, 1)
                if s1:
                    weigh(n, 1)
                if s2:
                    moments1(m2)
                if s3:
                    gate_max(m3)
                if s1:
                    weigh(n, 2)
                if s3:
                    gate_shift(m3)
                    payload(m3, p)
                    gate_sum(m3)
                if s2:
                    shift1(m2)
                if s1:
                    weigh(n, 3)
                if s3:
                    gate_inverse(m3)
                    gate_scores(m3)
                    gate_top(m3)
                    gate_index(m3)
                    gate_chosen(m3)
                    gate_weight_sum(m3)
                    gate_onehot(m3)
                    gate_weight_inverse(m3)
                    gate_members(m3, p)
                    gate_weights(m3)
                    members_sum(m3, p)
                    members_count(m3, p)
                    row_base(m3)
                    row_pick(m3)
                    row_sum(m3)
                    row_index(m3, p)

            pipeline(dve, step)

            dve.wait_ge(cnt_ps, 1)
            dve.tensor_copy(cnt_i[:, :], GATE[:, 0:EXPERTS]).then_inc(table_ok, 1)
            dve.wait_ge(table_ok, 1)
            link(tsteps, 1, dve.tensor_scalar(cup_i[:, :], cnt_i[:, :], float(ET - 1), None, ALU.add))
            link(tsteps, 2, dve.tensor_scalar(nt_i[:, :], cup_i[:, :], ET.bit_length() - 1, None, ALU.logical_shift_right))
            link(tsteps, 3, dve.tensor_copy(nt[:, :], nt_i[:, :]))
            link(tsteps, 4, dve.tensor_tensor_scan(ntc[:, :], ones[:, 0:EXPERTS], nt[:, :], 0.0, ALU.mult, ALU.add))
            link(tsteps, 5, dve.tensor_tensor(
                past[:, :, :], ntc[:, :].rearrange("p (o e) -> p o e", o=1).broadcast_to([P, SLOTS, EXPERTS]),
                iota_j[:, :].rearrange("p (j o) -> p j o", o=1).broadcast_to([P, SLOTS, EXPERTS]), ALU.is_le))
            link(tsteps, 6, dve.tensor_reduce(ej[:, :], past[:, :, :], AX_X, ALU.add))
            link(tsteps, 7, dve.tensor_tensor(
                pnt[:, :, :], past[:, :, :], nt[:, :].rearrange("p (o e) -> p o e", o=1).broadcast_to([P, SLOTS, EXPERTS]),
                ALU.mult))
            link(tsteps, 8, dve.tensor_reduce(first_j[:, :], pnt[:, :, :], AX_X, ALU.add))
            link(tsteps, 9, dve.tensor_tensor(off_j[:, :], iota_j[:, :], first_j[:, :], ALU.subtract))
            link(tsteps, 10, dve.tensor_scalar(off_rows[:, :], off_j[:, :], float(ET), None, ALU.mult))
            link(tsteps, 11, dve.scalar_tensor_tensor(out=row_j[:, :], in0=ej[:, :], scalar=float(CAP), in1=off_rows[:, :],
                                              op0=ALU.mult, op1=ALU.add))
            dve.tensor_copy(row_i[:, :], row_j[:, :]).then_inc(table_ok, 1)
            dve.tensor_scalar(e_i[:, :], ej[:, :], float(EXPERTS - 1), None, ALU.min).then_inc(table_ok, 1)
            dve.wait_ge(table_ok, 3)
            dve.wait_ge(ld_big, 16 * BIG_LOADS)

            def take(j, i, r):
                dve.wait_ge(xe_ps, j + 1)
                at_least(dve, h_ps, j - 1)
                dve.tensor_copy(xeT[r % 2][:, :], XB[r % 2][:, 0:ET].bitcast(F16)).then_inc(xe_ok, 1)

            def take_returns(j, i, r):
                dve.wait_ge(ld_row[r], 16 * (i + 1))
                at_least(dve, returned[r], 2 * 16 * i)
                dve.tensor_copy(ridx[r][:, :], xrow[r][:, :, P].bitcast(I32)).then_inc(ridx_ok, 1)

            def give(j, i, r):
                e = dve.value_load(e_i[0:1, bass.ds(j, 1)], min_val=0, max_val=EXPERTS - 1)
                dve.wait_ge(y2_ps, j + 1)
                dve.tensor_tensor(y_sb[r], YB[r % 2][:, 0:2 * P].rearrange("p (t d) -> p t d", t=2),
                                  b2_sb[:, bass.ds(e * P, P)].rearrange("p (o d) -> p o d", o=1).broadcast_to([P, 2, P]),
                                  ALU.add).then_inc(y2_ok, 1)

            def expert_tile(j, i, r):
                if there(j + 1):
                    take(*near(j, i, r, 1))
                if there(j - 1):
                    give(*near(j, i, r, -1))
                if there(j):
                    take_returns(j, i, r)

            take(0, 0, 0)
            expert_tiles(dve, expert_tile, behind=1)

            for p in range(2):
                dve.wait_ge(kept[p], 16 * (PAIRS // 2 + 1))
            def shift3(q):
                t0, t1 = 4 * q, 4 * q + 4
                dve.wait_ge(rstd3_ok, q + 1)
                dve.scalar_tensor_tensor(out=nmr3[:, t0:t1], in0=mv3[:, t0:t1, 0], scalar=-1.0, in1=rstd3[:, t0:t1],
                                         op0=ALU.mult, op1=ALU.mult).then_inc(nmr3_ok, 1)

            done = 0
            for q in range(QUADS):
                quad = range(4 * q, 4 * q + 4)
                dve.wait_ge(ld_y[q], 16 * TOP)
                for t in quad:
                    dve.scalar_tensor_tensor(out=z1[:, t, :], in0=y_in[:, 0, t, :], scalar=w_all[:, t, 0:1],
                                             in1=x2_all[:, t, :], op0=ALU.mult, op1=ALU.add).then_inc(zsteps, 1)
                for k, t in enumerate(quad):
                    dve.wait_ge(zsteps, done + k + 1)
                    dve.scalar_tensor_tensor(out=z[:, t, :], in0=y_in[:, 1, t, :], scalar=w_all[:, t, 1:2],
                                             in1=z1[:, t, :], op0=ALU.mult, op1=ALU.add).then_inc(zsteps, 1)
                for k, t in enumerate(quad):
                    dve.wait_ge(zsteps, done + 4 + k + 1)
                    dve.bn_stats(st3[:, t, :], z[:, t, :]).then_inc(zsteps, 1)
                for k, t in enumerate(quad):
                    dve.wait_ge(zsteps, done + 8 + k + 1)
                    dve.bn_aggr(mv3[:, t, :], st3[:, t, :]).then_inc(mv3_ok, 1)
                done += 12
                if q:
                    shift3(q - 1)
            shift3(QUADS - 1)


def kernel(x, ctx_768, L0_attn_Wq, L0_attn_Wk, L0_attn_Wv, L0_attn_Wo, L0_xattn_Wv, L0_xattn_bv, L0_xattn_Wt, L0_xattn_bt,
           L0_ffn_gate_w, L0_ffn_w1, L0_ffn_b1, L0_ffn_w2, L0_ffn_b2):
    import numpy as np
    import concourse.bacc as bacc
    from concourse.bass_utils import run_bass_kernel_spmd

    def flat(a):
        a = np.asarray(a)
        return a.reshape(-1, a.shape[-1])

    def columns(a):
        return np.ascontiguousarray(np.asarray(a).T)

    batch, seq, hidden = np.shape(x)
    experts, ff = np.shape(L0_ffn_b1)
    arrays = {
        "x": np.ascontiguousarray(flat(x)),
        "xT": columns(flat(x)),
        "ctxT": columns(flat(ctx_768)),
        "w_qkvT": np.ascontiguousarray(np.concatenate([np.asarray(w) for w in (L0_attn_Wq, L0_attn_Wk, L0_attn_Wv)]).T),
        "w_oT": columns(L0_attn_Wo),
        "w_xvT": columns(L0_xattn_Wv),
        "b_v": np.ascontiguousarray(np.asarray(L0_xattn_bv).reshape(-1, 1)),
        "w_tT": columns(L0_xattn_Wt),
        "b_t": np.ascontiguousarray(np.asarray(L0_xattn_bt).reshape(-1, 1)),
        "gate_w": np.ascontiguousarray(L0_ffn_gate_w),
        "w1": np.ascontiguousarray(L0_ffn_w1),
        "b1T": columns(np.asarray(L0_ffn_b1).reshape(experts * ff // 128, 128)),
        "w2": np.ascontiguousarray(L0_ffn_w2),
        "b2": np.ascontiguousarray(L0_ffn_b2),
    }
    nc = bacc.Bacc("TRN2", target_bir_lowering=False, num_devices=1)
    ins = {n: nc.dram_tensor(f"{n}_dram", a.shape, mybir.dt.from_np(a.dtype), kind="ExternalInput").ap()
           for n, a in arrays.items()}
    out = nc.dram_tensor("out_dram", (batch * seq, hidden), mybir.dt.float32, kind="ExternalOutput").ap()
    decoder_layer(nc, **ins, out=out)
    r = run_bass_kernel_spmd(nc, [{f"{n}_dram": a for n, a in arrays.items()}], core_ids=[0])
    return r.results[0]["out_dram"].reshape(batch, seq, hidden)
```

```python
from contextlib import ExitStack

import concourse.bass as bass
from concourse import mybir

F32 = mybir.dt.float32
F16 = mybir.dt.float16
BF16 = mybir.dt.bfloat16
I32 = mybir.dt.int32
U32 = mybir.dt.uint32
ALU = mybir.AluOpType
ACT = mybir.ActivationFunctionType
AX_X = mybir.AxisListType.X

P = 128
HEADS, HD = 16, 8
EXPERTS, TOP = 8, 2
LN_EPS = 1e-5
NORM_EPS = 1e-6
COS_CAP = 1e8
TINY = 1e-30
W1_SCALE = 16.0


def decoder_layer(nc, x, xT, ctxT, w_qkvT, w_oT, w_xvT, b_v, w_tT, b_t, gate_w, w1, b1T, w2, b2, out):
    T = x.shape[0]
    TILES = T // P
    PAIRS = TILES // 2
    CD, XH = ctxT.shape[0], w_tT.shape[1]
    FF = w1.shape[2]
    FC = FF // P
    ET = 2 * P
    SLOTS = TOP * T // ET + EXPERTS - 1
    RING = 4
    assert RING % 2 == 0 and PAIRS % 2 == 0
    CAP = T + ET
    DUMMIES = EXPERTS - 1
    PADS = (EXPERTS + DUMMIES) * ET // P
    RETURN, WEIGHT = P, P + 1
    ROW = P + 2
    SCAN = HEADS * HD * HD

    x_rows = nc.dram_tensor("x_rows", (EXPERTS * CAP + DUMMIES * ET, ROW), F32, kind="Internal").ap()
    y_rows = nc.dram_tensor("y_rows", (TOP * T + PADS * P, P), F32, kind="Internal").ap()

    with ExitStack() as ctx:
        def sb(name, shape, dt=F32):
            return ctx.enter_context(nc.sbuf_tensor(name, shape, dt))

        def sem(name):
            return ctx.enter_context(nc.semaphore(name))

        wqkv = sb("wqkv", [P, 3 * P])
        wo = sb("wo", [P, P])
        wxv = sb("wxv", [P, XH])
        bv = sb("bv", [XH, 1])
        wt = sb("wt", [CD, XH])
        bt = sb("bt", [XH, 1])
        gw = sb("gw", [P, EXPERTS])
        ctx_sb = sb("ctx_sb", [CD, T])
        w1_raw = sb("w1_raw", [P, EXPERTS * FF])
        w1_hi = sb("w1_hi", [P, EXPERTS * FF], F16)
        w1_lo = sb("w1_lo", [P, EXPERTS * FF], F16)
        b1_sb = sb("b1_sb", [P, EXPERTS * FC])
        w2_sb = sb("w2_sb", [P, EXPERTS * FC * P])
        b2_sb = sb("b2_sb", [P, EXPERTS * P])
        ident = sb("ident", [P, P])
        ident16 = sb("ident16", [P, P], F16)
        upto = sb("upto", [P, P])
        before = sb("before", [P, P], BF16)
        ones = sb("ones", [P, P])
        ones16 = sb("ones16", [P, P], BF16)
        half = sb("half", [P, TILES])
        iota_e = sb("iota_e", [P, EXPERTS])
        base_e = sb("base_e", [P, EXPERTS])
        iota_j = sb("iota_j", [P, SLOTS])
        iota_ei = sb("iota_ei", [P, EXPERTS], I32)
        base_ei = sb("base_ei", [P, EXPERTS], I32)
        iota_ji = sb("iota_ji", [P, SLOTS], I32)
        returns = sb("returns", [P, TILES, TOP], I32)
        pick = sb("pick", [TILES, TILES, P])
        padding = sb("padding", [P, PADS, ROW])
        tT = sb("tT", [XH, T])
        tsq = sb("tsq", [XH, T])
        tn2 = sb("tn2", [P, TILES])
        itn = sb("itn", [P, TILES])
        itnT = sb("itnT", [TILES, P])
        itn_row = sb("itn_row", [P, T])
        xT_sb = [sb(f"xT_sb{p}", [P, 2 * P]) for p in range(2)]
        x_sb = [sb(f"x_sb{p}", [P, 2, P]) for p in range(2)]
        e_qk = sb("e_qk", [P, 2, 2 * P])
        r_qk = sb("r_qk", [P, 2, 2 * P])
        v_sb = sb("v_sb", [P, 2, P])
        phi = [sb(f"phi{p}", [P, 2, 2 * P]) for p in range(2)]
        kv = sb("kv", [P, 2, SCAN])
        qk = sb("qk", [P, 2, P])
        norm = sb("norm", [P, 2 * HEADS])
        normf = sb("normf", [P, 2 * HEADS])
        rnorm = sb("rnorm", [P, 2 * HEADS])
        qn = sb("qn", [P, 2, P])
        prod = sb("prod", [P, 2, SCAN])
        oT = sb("oT", [P, 2 * P])
        r1 = sb("r1", [P, 2, P])
        st1 = sb("st1", [P, 2, 6])
        mv1 = sb("mv1", [P, 2, 2])
        ve1 = sb("ve1", [P, 2])
        rstd1 = sb("rstd1", [P, 2])
        nmr1 = sb("nmr1", [P, 2])
        x1 = [sb(f"x1{p}", [P, 2, P]) for p in range(2)]
        x1T = sb("x1T", [P, 2 * P])
        vT = sb("vT", [XH, 2 * P])
        vsq = sb("vsq", [XH, 2 * P])
        vn2 = sb("vn2", [P, 2])
        ivn = sb("ivn", [P, 2])
        wcos = sb("wcos", [P, 2, P])
        ucos = sb("ucos", [P, 2, P])
        r2 = [sb(f"r2{p}", [P, 2, P]) for p in range(2)]
        st2 = sb("st2", [P, 2, 6])
        mv2 = [sb(f"mv2{p}", [P, 2, 2]) for p in range(2)]
        ve2 = sb("ve2", [P, 2])
        rstd2 = sb("rstd2", [P, 2])
        nmr2 = sb("nmr2", [P, 2])
        x2 = [sb(f"x2{p}", [P, 2, P]) for p in range(2)]
        x2_all = sb("x2_all", [P, TILES, P])
        x2T = sb("x2T", [P, 2 * P])
        gmax = sb("gmax", [P, 2])
        gdif = sb("gdif", [P, 2, EXPERTS])
        gexp = sb("gexp", [P, 2, EXPERTS])
        gsum = sb("gsum", [P, 2])
        rgsum = sb("rgsum", [P, 2])
        score = sb("score", [P, 2, EXPERTS])
        top8 = sb("top8", [P, 2, EXPERTS])
        idx8 = sb("idx8", [P, 2, EXPERTS], U32)
        wsum = sb("wsum", [P, 2])
        rwsum = sb("rwsum", [P, 2])
        chosen = sb("chosen", [P, 2, TOP])
        onehot = sb("onehot", [P, 2 * TOP, EXPERTS])
        member = [sb(f"member{p}", [P, 2, EXPERTS], BF16) for p in range(2)]
        macc = [sb(f"macc{p}", [P, EXPERTS], BF16) for p in range(2)]
        msum = sb("msum", [P, EXPERTS], BF16)
        place = sb("place", [P, 2, EXPERTS])
        placed = sb("placed", [P, 2 * TOP, EXPERTS])
        rowf = sb("rowf", [P, 2 * TOP])
        rowi = [sb(f"rowi{p}", [P, 2 * TOP], I32) for p in range(2)]
        pay = [sb(f"pay{p}", [P, 2, TOP, ROW]) for p in range(2)]
        cnt_i = sb("cnt_i", [P, EXPERTS], I32)
        cup_i = sb("cup_i", [P, EXPERTS], I32)
        nt_i = sb("nt_i", [P, EXPERTS], I32)
        nt = sb("nt", [P, EXPERTS])
        ntc = sb("ntc", [P, EXPERTS])
        past = sb("past", [P, SLOTS, EXPERTS])
        pnt = sb("pnt", [P, SLOTS, EXPERTS])
        ej = sb("ej", [P, SLOTS])
        first_j = sb("first_j", [P, SLOTS])
        off_j = sb("off_j", [P, SLOTS])
        off_rows = sb("off_rows", [P, SLOTS])
        row_j = sb("row_j", [P, SLOTS])
        row_i = sb("row_i", [P, SLOTS], I32)
        e_i = sb("e_i", [P, SLOTS], I32)
        def cut_up(buffer, width):
            flat = buffer[:, :, :].rearrange("p t c -> p (t c)")
            return [flat[:, r * 2 * width:(r + 1) * 2 * width].rearrange("p (t c) -> p t c", t=2) for r in range(RING)]

        xrow = cut_up(kv, ROW)
        y_sb = cut_up(prod, P)
        ridx = [sb(f"ridx{r}", [P, 2], I32) for r in range(RING)]
        wrow = [sb(f"wrow{r}", [P, 2]) for r in range(RING)]
        ysum = sb("ysum", [P, 2, P])
        xeT = [sb(f"xeT{r}", [P, 2 * ET], F16) for r in range(2)]
        g_sb = [sb(f"g_sb{r}", [P, FC * ET]) for r in range(2)]
        y_in = sb("y_in", [P, TOP, TILES, P])
        z1 = w1_raw[:, 0:TILES * P].rearrange("p (t d) -> p t d", d=P)
        z = w1_raw[:, TILES * P:2 * TILES * P].rearrange("p (t d) -> p t d", d=P)
        st3 = sb("st3", [P, TILES, 6])
        mv3 = sb("mv3", [P, TILES, 2])
        ve3 = sb("ve3", [P, TILES])
        rstd3 = sb("rstd3", [P, TILES])
        nmr3 = sb("nmr3", [P, TILES])
        o_sb = itn_row[:, :].rearrange("p (t d) -> p t d", d=P)

        ps = ctx.enter_context(nc.psum_tensor("ps", [P, 8, 512], F32))
        bank = [ps[:, b, :] for b in range(8)]
        QKV = ps[:, 0:2, :]
        CUM = [bank[2], bank[3]]
        TR, MM, DOT, GATE = bank[4], bank[5], bank[6], bank[7]
        HB = [[bank[2 * h + f // 2][:, f % 2 * ET:(f % 2 + 1) * ET] for f in range(FC)] for h in range(2)]
        XB = [bank[4], bank[5]]
        YB = [bank[6], bank[7]]

        ld_wqkv, ld_w, ld_ctx, ld_big, ld_w1 = sem("ld_wqkv"), sem("ld_w"), sem("ld_ctx"), sem("ld_big"), sem("ld_w1")
        ld_x = [sem(f"ld_x{p}") for p in range(2)]
        ld_xT = [sem(f"ld_xT{p}") for p in range(2)]
        consts, vconsts = sem("consts"), sem("vconsts")
        tproj, tread, tnorm, tn2_ok, itn_ok, itnT_ps, itnT_ok, itnrow_ps, itnrow_ok = (
            sem(n) for n in ("tproj", "tread", "tnorm", "tn2_ok", "itn_ok", "itnT_ps", "itnT_ok", "itnrow_ps", "itnrow_ok"))
        w1s_ok, w1hi_ok, w1lo_ok = sem("w1s_ok"), sem("w1hi_ok"), sem("w1lo_ok")
        qkv_ps, qkv_read, phi_ok, kv_ok, kcum_ps, kcum_read, qn_ok, cum_ps, prod_ok = (
            sem(n) for n in ("qkv_ps", "qkv_read", "phi_ok", "kv_ok", "kcum_ps", "kcum_read", "qn_ok", "cum_ps", "prod_ok"))
        oT_ps, oT_ok, y_ps, y_read, mv1_ok, ve1_ok, rstd1_ok, nmr1_ok, x1_ok, x1T_ps, x1T_ok, vT_ps, vT_ok = (
            sem(n) for n in ("oT_ps", "oT_ok", "y_ps", "y_read", "mv1_ok", "ve1_ok", "rstd1_ok", "nmr1_ok", "x1_ok", "x1T_ps",
                             "x1T_ok", "vT_ps", "vT_ok"))
        dot_ps, vn2_ok, ivn_ok, dot_read, mv2_ok, ve2_ok, rstd2_ok, nmr2_ok, x2_ok, x2T_ps, x2T_ok = (
            sem(n) for n in ("dot_ps", "vn2_ok", "ivn_ok", "dot_read", "mv2_ok", "ve2_ok", "rstd2_ok", "nmr2_ok", "x2_ok",
                             "x2T_ps", "x2T_ok"))
        gate_ps, gdif_ok, gexp_ok, member_ok, macc_ok, pos_ps, pos_read, row_ok, hi_ok, low_ok = (
            sem(n) for n in ("gate_ps", "gdif_ok", "gexp_ok", "member_ok", "macc_ok", "pos_ps", "pos_read", "row_ok", "hi_ok",
                             "low_ok"))
        apart, w_ok, msum_ok = sem("apart"), sem("w_ok"), sem("msum_ok")
        sent, returns_ok = sem("sent"), sem("returns_ok")
        kept = [sem(f"kept{p}") for p in range(2)]
        scattered = [sem(f"scattered{p}") for p in range(2)]
        norm_in, st1_in, wcos_ok, r2_ok, st2_in, gate_in, row_in = (
            sem(n) for n in ("norm_in", "st1_in", "wcos_ok", "r2_ok", "st2_in", "gate_in", "row_in"))
        cnt_ps, table_ok, tsteps, filled = sem("cnt_ps"), sem("table_ok"), sem("tsteps"), sem("filled")
        ld_row = [sem(f"ld_row{r}") for r in range(RING)]
        xe_ps, xe_ok, ridx_ok, wrow_ok, h_ps, g_ok, y2_ps, y2_ok, yw_ok = (
            sem(n) for n in ("xe_ps", "xe_ok", "ridx_ok", "wrow_ok", "h_ps", "g_ok", "y2_ps", "y2_ok", "yw_ok"))
        returned = [sem(f"returned{r}") for r in range(RING)]
        GROUPS = [(0, 3), (3, 7), (7, 11), (11, 14), (14, TILES)]
        ld_y = [sem(f"ld_y{q}") for q in range(len(GROUPS))]
        POOL_GROUPS = (2, 3)
        kv_pool = sem("kv_pool")
        z1_ok, z1_pool, z_ok = sem("z1_ok"), sem("z1_pool"), sem("z_ok")
        zsteps, mv3_ok, ve3_ok, rstd3_ok, nmr3_ok, o_ok, stored = (
            sem(n) for n in ("zsteps", "mv3_ok", "ve3_ok", "rstd3_ok", "nmr3_ok", "o_ok", "stored"))

        CONSTS = 16
        VCONSTS = 5
        W_LOADS, CTX_LOADS, BIG_LOADS = 4, 3, 3
        xT_dram = xT.rearrange("d (n c) -> d n c", c=2 * P)
        x_dram = x.rearrange("(n t p) d -> p n t d", t=2, p=P)
        out_dram = out.rearrange("(t p) d -> p t d", p=P)
        y_dram = y_rows[0:TOP * T, :].rearrange("(k t p) d -> p k t d", k=TOP, p=P)

        def pipeline(eng, step):
            for n in range(3):
                step(n, n % 2, n // 2, True, True, n >= 1, n >= 2, False)
            with eng.Fori(1, (PAIRS - 2) // 2) as i:
                step(2 * i + 1, 1, i, True, True, True, True, True)
                step(2 * i + 2, 0, i + 1, True, True, True, True, True)
            for n in range(PAIRS - 1, PAIRS + 3):
                step(n, n % 2, n // 2, n + 1 < PAIRS, n < PAIRS, n <= PAIRS, n <= PAIRS + 1, True)

        def at(n, k):
            return isinstance(n, int) and n == k

        def expert_tiles(eng, step, behind=0):
            for j in range(RING):
                step(j, 0, j)
            with eng.Fori(1, SLOTS // RING) as i:
                for r in range(RING):
                    step(RING * i + r, i, r)
            for j in range(SLOTS // RING * RING, SLOTS + behind):
                step(j, j // RING, j % RING)

        def near(j, i, r, d):
            return j + d, i + (r + d) // RING, (r + d) % RING

        def there(j):
            return not isinstance(j, int) or 0 <= j < SLOTS

        def wait_apart(eng, *pairs):
            for s, value in pairs:
                at_least(eng, s, value)
            eng.sem_inc(apart, 1)

        def at_least(eng, s, value):
            if not isinstance(value, int) or value > 0:
                eng.wait_ge(s, value)

        def pad_experts(eng, experts):
            for e in experts:
                n_e = eng.value_load(cnt_i[0:1, e:e + 1], min_val=0, max_val=T)
                eng.dma_start(x_rows[bass.ds(n_e + e * CAP, ET), :].rearrange("(t p) c -> p t c", p=P),
                              padding[:, e * ET // P:(e + 1) * ET // P, :]).then_inc(filled, 16)

        def row_of(eng, j):
            return eng.value_load(row_i[0:1, bass.ds(j, 1)], min_val=0, max_val=EXPERTS * CAP + (DUMMIES - 1) * ET)

        def outer_operands(p, t, d0, ds):
            k = phi[p][:, t, P:2 * P].rearrange("p (h d o) -> p d h o", d=HD, o=1)[:, d0:d0 + ds, :, :]
            v = v_sb[:, t, :].rearrange("p (o h e) -> p o h e", o=1, e=HD)
            o = kv[:, t, d0 * P:(d0 + ds) * P].rearrange("p (d h e) -> p d h e", d=ds, e=HD)
            return k.broadcast_to([P, ds, HEADS, HD]), v.broadcast_to([P, ds, HEADS, HD]), o

        def load_results(eng, k):
            for r in range(RING):
                eng.wait_ge(returned[r], 2 * 16 * len(range(r, SLOTS, RING)))
            for q, (t0, t1) in enumerate(GROUPS):
                eng.dma_start(y_in[:, k, t0:t1, :], y_dram[:, k, t0:t1, :]).then_inc(ld_y[q], 16)

        block = ctx.enter_context(nc.Block())

        @block.sync
        def _(sp):
            def load_xT(n, p):
                at_least(sp, qkv_ps, n - 1)
                sp.dma_start(xT_sb[p][:, :], xT_dram[:, n, :]).then_inc(ld_xT[p], 16)

            def load_x(n, p):
                at_least(sp, y_read, n - 1)
                sp.dma_start(x_sb[p][:, :, :], x_dram[:, n, :, :]).then_inc(ld_x[p], 16)

            def keep_x2(m, p):
                sp.wait_ge(x2_ok, 2 * (m + 1))
                sp.dma_start(x2_all[:, bass.ds(2 * m, 2), :], x2[p][:, :, :]).then_inc(kept[p], 16)

            sp.sem_inc(kept[0], 16)
            sp.sem_inc(kept[1], 16)
            load_xT(0, 0)
            load_xT(1, 1)
            load_x(0, 0)
            for dst, src in ((wo, w_oT), (wxv, w_xvT), (bv, b_v), (gw, gate_w)):
                sp.dma_start(dst[:, :], src).then_inc(ld_w, 16)
            sp.dma_start(w1_raw[:, :].rearrange("p (e f) -> p e f", e=EXPERTS),
                         w1.rearrange("e d f -> d e f")).then_inc(ld_w1, 16)
            sp.dma_start(w2_sb[:, :].rearrange("p (a d) -> p a d", d=P),
                         w2.rearrange("e (c p) d -> p (e c) d", p=P)).then_inc(ld_big, 16)
            sp.dma_start(b1_sb[:, :], b1T).then_inc(ld_big, 16)
            sp.dma_start(b2_sb[:, :], b2.rearrange("(a e) d -> a (e d)", a=1).broadcast_to([P, EXPERTS * P])).then_inc(ld_big, 16)

            def step(n, p, h, s0, s1, s2, s3, s4):
                if s0 and not at(n, 0):
                    load_xT(n + 1, 1 - p)
                if s1 and not at(n, 0):
                    load_x(n, p)
                if s3:
                    keep_x2(n - 2, p)

            pipeline(sp, step)

            sp.wait_ge(table_ok, 1)
            pad_experts(sp, range(0, EXPERTS, 2))
            sp.wait_ge(table_ok, 3)
            first_rows = [row_of(sp, j) for j in range(RING)]
            sp.wait_ge(filled, 16 * EXPERTS)
            for p in range(2):
                sp.wait_ge(scattered[p], 16 * (p + 2 * TOP * (PAIRS // 2)))

            def load_row(j, i, r):
                at_least(sp, xe_ps, j - RING + 1)
                at_least(sp, wrow_ok, j - RING + 1)
                row = first_rows[j] if isinstance(j, int) and j < RING else row_of(sp, j)
                sp.dma_start(xrow[r], x_rows[bass.ds(row, ET), :].rearrange("(t p) c -> p t c", p=P)).then_inc(ld_row[r], 16)

            expert_tiles(sp, load_row)

            load_results(sp, 0)
            for q, (t0, t1) in enumerate(GROUPS):
                sp.wait_ge(o_ok, t1)
                sp.dma_start(out_dram[:, t0:t1, :], o_sb[:, t0:t1, :]).then_inc(stored, 16)
            sp.wait_ge(stored, 16 * len(GROUPS))

        @block.gpsimd
        def _(pool):
            pool.memset(ident[:, :], 0.0).then_inc(consts, 1)
            pool.memset(upto[:, :], 1.0).then_inc(consts, 1)
            pool.memset(before[:, :], 1.0).then_inc(consts, 1)
            pool.memset(ones[:, :], 1.0).then_inc(consts, 1)
            pool.memset(half[:, :], -0.5).then_inc(consts, 1)
            pool.wait_ge(consts, 5)
            pool.affine_select(out=ident[:, :], in_=ident[:, :], compare_op=ALU.not_equal, fill=1.0, base=0,
                               pattern=[[-1, P]], channel_multiplier=1).then_inc(consts, 1)
            pool.affine_select(out=upto[:, :], in_=upto[:, :], compare_op=ALU.is_ge, fill=0.0, base=0,
                               pattern=[[1, P]], channel_multiplier=-1).then_inc(consts, 1)
            pool.affine_select(out=before[:, :], in_=before[:, :], compare_op=ALU.is_gt, fill=0.0, base=0,
                               pattern=[[1, P]], channel_multiplier=-1).then_inc(consts, 1)
            pool.memset(pick[:, :, :], 1.0).then_inc(consts, 1)
            pool.memset(padding[:, :, :], 0.0).then_inc(consts, 1)
            pool.wait_ge(consts, 10)
            pool.affine_select(out=pick[:, :, :], in_=pick[:, :, :], compare_op=ALU.is_equal, fill=0.0, base=0,
                               pattern=[[1, TILES], [0, P]], channel_multiplier=-1).then_inc(consts, 1)
            pool.iota(padding[:, :, RETURN:RETURN + 1].bitcast(I32), [[P, PADS]], base=TOP * T,
                      channel_multiplier=1).then_inc(consts, 1)
            pool.iota(returns[:, :, :], [[P, TILES], [T, TOP]], base=0, channel_multiplier=1).then_inc(consts, 1)
            pool.iota(iota_ei[:, :], [[1, EXPERTS]], base=0, channel_multiplier=0).then_inc(consts, 1)
            pool.iota(base_ei[:, :], [[CAP, EXPERTS]], base=0, channel_multiplier=0).then_inc(consts, 1)
            pool.iota(iota_ji[:, :], [[1, SLOTS]], base=0, channel_multiplier=0).then_inc(consts, 1)
            def inverse_norms():
                pool.wait_ge(tn2_ok, 1)
                pool.tensor_tensor(itn[:, :], tn2[:, :], half[:, :], ALU.pow).then_inc(itn_ok, 1)

            def rstd1_of(m):
                wait_apart(pool, (mv1_ok, 2 * (m + 1)), (nmr1_ok, m), (x1_ok, 2 * m))
                pool.tensor_scalar(ve1[:, :], mv1[:, :, 1], LN_EPS, None, ALU.add).then_inc(ve1_ok, 1)
                pool.wait_ge(ve1_ok, m + 1)
                pool.tensor_tensor(rstd1[:, :], ve1[:, :], half[:, 0:2], ALU.pow).then_inc(rstd1_ok, 1)

            def ivn_of(m):
                pool.wait_ge(vn2_ok, m + 1)
                pool.tensor_tensor(ivn[:, :], vn2[:, :], half[:, 0:2], ALU.pow).then_inc(ivn_ok, 1)

            def outer_rest(n, p):
                pool.wait_ge(qkv_read, 3 * n + 3)
                pool.wait_ge(phi_ok, n + 1)
                at_least(pool, cum_ps, 4 * n)
                k, v, o = outer_operands(p, 1, HD // 2, HD // 2)
                pool.tensor_tensor(o, k, v, ALU.mult).then_inc(kv_pool, 1)

            def rstd2_of(m, p):
                wait_apart(pool, (mv2_ok, 2 * (m + 1)), (nmr2_ok, m), (x2_ok, 2 * m))
                pool.tensor_scalar(ve2[:, :], mv2[p][:, :, 1], LN_EPS, None, ALU.add).then_inc(ve2_ok, 1)
                pool.wait_ge(ve2_ok, m + 1)
                pool.tensor_tensor(rstd2[:, :], ve2[:, :], half[:, 0:2], ALU.pow).then_inc(rstd2_ok, 1)

            def low_half(m, p):
                pool.wait_ge(hi_ok, 2 * (m + 1))
                rows16 = pay[p][:, :, :, 0:P].bitcast(F16)
                both = x2[p][:, :, :].rearrange("p t (o d) -> p t o d", o=1).broadcast_to([P, 2, TOP, P])
                pool.tensor_tensor(rows16[:, :, :, P:2 * P], both, rows16[:, :, :, 0:P], ALU.subtract).then_inc(low_ok, 1)

            def sent_before(m, p, h):
                pool.wait_ge(scattered[1 - p], 16 * (2 * TOP * (h + p) + 1 - p))
                pool.sem_inc(sent, 1)

            def scatter(m, p, tiles=(0, 1)):
                wait_apart(pool, (row_ok, m + 1), (returns_ok, m + 1), (w_ok, m + 1), (low_ok, m + 1))
                for c in range(TOP * tiles[0], TOP * (tiles[-1] + 1)):
                    pool.indirect_dma_start(x_rows, bass.IndirectOffsetOnAxis(ap=rowi[p][:, c:c + 1], axis=0),
                                            pay[p][:, c // TOP, c % TOP, :], None).then_inc(scattered[p], 16)

            def low_w1(e):
                cols = bass.ds(e * FF, FF)
                pool.wait_ge(w1hi_ok, e + 1)
                pool.tensor_tensor(w1_lo[:, cols], w1_raw[:, cols], w1_hi[:, cols], ALU.subtract).then_inc(w1lo_ok, 1)

            pool.wait_ge(consts, CONSTS)
            pool.dma_start(x_rows[EXPERTS * CAP:, :].rearrange("(r p) c -> p r c", p=P),
                           padding[:, EXPERTS * ET // P:, :]).then_inc(scattered[1], 16)
            pool.sem_inc(sent, 1)

            def step(n, p, h, s0, s1, s2, s3, s4):
                if at(n, PAIRS):
                    low_half(n - 3, 1 - p)
                    rstd1_of(n - 1)
                    ivn_of(n - 2)
                    sent_before(n - 3, 1 - p, h - 2 + p)
                    scatter(n - 3, 1 - p, [0])
                    rstd2_of(n - 2, p)
                    return
                if at(n, PAIRS + 1):
                    ivn_of(n - 2)
                    scatter(n - 4, p, [1])
                    low_half(n - 3, 1 - p)
                    rstd2_of(n - 2, p)
                    low_w1(n - 2)
                    sent_before(n - 3, 1 - p, h - 2 + p)
                    scatter(n - 3, 1 - p)
                    return
                if at(n, 1):
                    inverse_norms()
                if s4:
                    low_half(n - 3, 1 - p)
                if s3:
                    ivn_of(n - 2)
                if s1:
                    outer_rest(n, p)
                if s2:
                    low_w1(n - 1)
                if s3:
                    rstd2_of(n - 2, p)
                if s2:
                    rstd1_of(n - 1)
                if s4:
                    sent_before(n - 3, 1 - p, h - 2 + p)
                    scatter(n - 3, 1 - p)

            pipeline(pool, step)

            def give_back(j, i, r):
                wait_apart(pool, (yw_ok, 2 * (j + 1)), (ridx_ok, j + 1))
                for t in range(2):
                    pool.indirect_dma_start(y_rows, bass.IndirectOffsetOnAxis(ap=ridx[r][:, t:t + 1], axis=0),
                                            y_sb[r][:, t, :], None).then_inc(returned[r], 16)

            expert_tiles(pool, give_back)

            def add_choices(q):
                t0, t1 = GROUPS[q]
                pool.wait_ge(ld_y[q], 16 * TOP)
                pool.tensor_tensor(z1[:, t0:t1, :], y_in[:, 0, t0:t1, :], y_in[:, 1, t0:t1, :], ALU.add).then_inc(z1_pool, 1)

            for q, (t0, t1) in enumerate(GROUPS):
                if q + 1 in POOL_GROUPS:
                    add_choices(q + 1)
                pool.wait_ge(mv3_ok, t1)
                pool.tensor_scalar(ve3[:, t0:t1], mv3[:, t0:t1, 1], LN_EPS, None, ALU.add).then_inc(ve3_ok, 1)
                pool.wait_ge(ve3_ok, q + 1)
                pool.tensor_tensor(rstd3[:, t0:t1], ve3[:, t0:t1], half[:, 0:t1 - t0], ALU.pow).then_inc(rstd3_ok, 1)

        @block.tensor
        def _(pe):
            def ctx_project():
                pe.wait_ge(ld_ctx, 16 * CTX_LOADS)
                for c in range(T // 512):
                    pe.matmul(bank[4 + c][0:XH, :], wt[:, :], ctx_sb[:, c * 512:(c + 1) * 512],
                              start=True, stop=True).then_inc(tproj, 1)

            def ctx_norms():
                pe.wait_ge(tread, 2 * (T // 512))
                for b in range(TILES):
                    last = pe.matmul(GATE[:, b:b + 1], tsq[:, b * P:(b + 1) * P], ones[0:XH, 0:1], start=True, stop=True)
                last.then_inc(tnorm, 1)

            def ctx_turn():
                pe.wait_ge(itn_ok, 1)
                pe.wait_ge(consts, CONSTS)
                pe.transpose(DOT[0:TILES, 0:P], itn[:, :], ident[:, :]).then_inc(itnT_ps, 1)

            def ctx_row(c):
                pe.wait_ge(itnT_ok, 1)
                at_least(pe, itnrow_ok, c - 1)
                for b in range(4):
                    last = pe.matmul([DOT, GATE][c % 2][:, b * P:(b + 1) * P], pick[:, 4 * c + b, :], itnT[:, :],
                                     start=True, stop=True)
                last.then_inc(itnrow_ps, 1)

            def project(n, p, h):
                if at(n, 0):
                    pe.wait_ge(ld_wqkv, 16)
                pe.wait_ge(ld_xT[p], 16 * (h + 1))
                at_least(pe, qkv_read, 3 * n)
                at_least(pe, kcum_read, n)
                for t in range(2):
                    last = pe.matmul(QKV[:, t, 0:3 * P], xT_sb[p][:, t * P:(t + 1) * P], wqkv[:, :], start=True, stop=True)
                last.then_inc(qkv_ps, 1)

            def cum_k(n, p):
                if at(n, 0):
                    pe.wait_ge(consts, 8)
                pe.wait_ge(phi_ok, n + 1)
                pe.wait_ge(qkv_read, 3 * (n + 1))
                for t in range(2):
                    last = pe.matmul(QKV[:, t, 3 * P:4 * P], upto[:, :], phi[p][:, t, P:2 * P], start=True, stop=True)
                last.then_inc(kcum_ps, 1)

            def cum_kv(n, u):
                pe.wait_ge(kv_ok, 2 * n + u // 2 + 1)
                if u == 3:
                    pe.wait_ge(kv_pool, n + 1)
                at_least(pe, prod_ok, 4 * n + u - 1)
                pe.matmul(CUM[u % 2][:, :], upto[:, :], kv[:, u // 2, (u % 2) * 512:(u % 2 + 1) * 512],
                          start=True, stop=True).then_inc(cum_ps, 1)

            def attend(m, t):
                pe.wait_ge(prod_ok, 4 * m + 2 * t + 2)
                at_least(pe, oT_ok, m)
                for d in range(HD):
                    last = pe.matmul(TR[:, t * P:(t + 1) * P], prod[:, t, d * P:(d + 1) * P], ident[:, :],
                                     start=(d == 0), stop=(d == HD - 1))
                last.then_inc(oT_ps, 1)

            def out_proj(m, early=False):
                pe.wait_ge(oT_ok, m + 1)
                if early:
                    pe.wait_ge(x2T_ok, m - 1)
                else:
                    at_least(pe, vT_ok, 2 * m)
                for t in range(2):
                    last = pe.matmul(MM[:, t * P:(t + 1) * P], oT[:, t * P:(t + 1) * P], wo[:, :], start=True, stop=True)
                last.then_inc(y_ps, 1)

            def turn_x1(m, p):
                pe.wait_ge(x1_ok, 2 * (m + 1))
                at_least(pe, dot_read, m)
                for t in range(2):
                    last = pe.transpose(DOT[:, t * P:(t + 1) * P], x1[p][:, t, :], ident[:, :])
                last.then_inc(x1T_ps, 1)

            def cross_v(m, turned, late=False):
                pe.wait_ge(x1T_ok, m + 1)
                pe.wait_ge(y_read, PAIRS if late else m + 1)
                if turned:
                    at_least(pe, x2T_ok, m)
                pe.matmul(MM[0:XH, 0:2 * P], wxv[:, :], x1T[:, :], start=True, stop=True).then_inc(vT_ps, 1)

            def cross_dots(m):
                pe.wait_ge(vT_ok, 2 * (m + 1))
                for t in range(2):
                    pe.matmul(DOT[:, 2 * P + t:2 * P + t + 1], vsq[:, t * P:(t + 1) * P], ones[0:XH, 0:1], start=True, stop=True)
                    last = pe.matmul(DOT[:, t * P:(t + 1) * P], vT[:, t * P:(t + 1) * P],
                                     tT[:, bass.ds(2 * P * m + t * P, P)], start=True, stop=True)
                last.then_inc(dot_ps, 1)

            def turn_x2(m, p):
                pe.wait_ge(x2_ok, 2 * (m + 1))
                pe.wait_ge(vT_ok, 2 * PAIRS if isinstance(m, int) and m >= PAIRS - 2 else 2 * (m + 1))
                pe.wait_ge(y_read, min(m + 2, PAIRS) if isinstance(m, int) else m + 2)
                for t in range(2):
                    last = pe.transpose(MM[:, t * P:(t + 1) * P], x2[p][:, t, :], ident[:, :])
                last.then_inc(x2T_ps, 1)

            def gate(m):
                pe.wait_ge(x2T_ok, m + 1)
                pe.wait_ge(pos_read, m + 1)
                for t in range(2):
                    last = pe.matmul(GATE[:, t * EXPERTS:(t + 1) * EXPERTS], x2T[:, t * P:(t + 1) * P], gw[:, :],
                                     start=True, stop=True)
                last.then_inc(gate_ps, 1)

            def positions(m, p):
                pe.wait_ge(member_ok, m + 1)
                pe.wait_ge(macc_ok, m + 1)
                for t in range(2):
                    o = GATE[:, (2 + t) * EXPERTS:(3 + t) * EXPERTS]
                    pe.matmul(o, before[:, :], member[p][:, t, :], start=True, stop=False)
                    if t == 1:
                        pe.matmul(o, ones16[:, :], member[p][:, 0, :], start=False, stop=False)
                    last = pe.matmul(o, ones16[:, :], macc[p][:, :], start=False, stop=True)
                last.then_inc(pos_ps, 1)

            def step(n, p, h, s0, s1, s2, s3, s4):
                if at(n, PAIRS):
                    attend(n - 1, 0)
                    turn_x2(n - 3, 1 - p)
                    turn_x1(n - 2, p)
                    attend(n - 1, 1)
                    gate(n - 3)
                    out_proj(n - 1, early=True)
                    cross_v(n - 2, True, late=True)
                    cross_dots(n - 2)
                    positions(n - 3, 1 - p)
                    return
                if at(n, PAIRS + 1):
                    turn_x1(n - 2, p)
                    cross_v(n - 2, False, late=True)
                    cross_dots(n - 2)
                    turn_x2(n - 3, 1 - p)
                    gate(n - 3)
                    positions(n - 3, 1 - p)
                    return
                if at(n, 1):
                    pe.wait_ge(ld_w, 16 * W_LOADS)
                if at(n, 2):
                    pe.wait_ge(itnrow_ok, 4)
                if s1:
                    cum_k(n, p)
                if s2:
                    attend(n - 1, 0)
                if s4:
                    turn_x2(n - 3, 1 - p)
                if s3:
                    turn_x1(n - 2, p)
                if s1:
                    cum_kv(n, 0)
                if s3:
                    cross_v(n - 2, s4)
                if s4:
                    gate(n - 3)
                if at(n, 1):
                    ctx_turn()
                if s1:
                    cum_kv(n, 1)
                if s3:
                    cross_dots(n - 2)
                if at(n, 1):
                    ctx_row(0)
                if s2:
                    attend(n - 1, 1)
                if at(n, 1):
                    ctx_row(1)
                if s0:
                    project(n + 1, 1 - p, h + p)
                if at(n, 0):
                    ctx_norms()
                if s2:
                    out_proj(n - 1)
                if s4:
                    positions(n - 3, 1 - p)
                if at(n, 1):
                    ctx_row(2)
                if s1:
                    cum_kv(n, 2)
                if at(n, 1):
                    ctx_row(3)
                if s1:
                    cum_kv(n, 3)

            project(0, 0, 0)
            ctx_project()
            pipeline(pe, step)

            pe.wait_ge(vconsts, VCONSTS)
            pe.wait_ge(macc_ok, PAIRS + 1)
            pe.wait_ge(pos_read, PAIRS + 1)
            pe.matmul(GATE[:, 0:EXPERTS], ones16[:, :], macc[PAIRS % 2][:, :], start=True, stop=True).then_inc(cnt_ps, 1)

            pe.wait_ge(w1hi_ok, EXPERTS)
            pe.wait_ge(w1lo_ok, EXPERTS)
            pe.wait_ge(ld_big, 16 * BIG_LOADS)
            pe.wait_ge(table_ok, 3)

            def turn_rows(j, i, r):
                pe.wait_ge(ld_row[r], 16 * (i + 1))
                at_least(pe, xe_ok, j - 1)
                for c in range(2):
                    for t in range(2):
                        half_row = xrow[r][:, t, 0:P].bitcast(F16)[:, c * P:(c + 1) * P]
                        last = pe.transpose(XB[r % 2][:, (2 * c + t) * P // 2:(2 * c + t + 1) * P // 2].bitcast(F16),
                                            half_row, ident16[:, :])
                last.then_inc(xe_ps, 1)

            def expert_of(j):
                return pe.value_load(e_i[0:1, bass.ds(j, 1)], min_val=0, max_val=EXPERTS - 1)

            def layer1(j, i, r, e):
                pe.wait_ge(xe_ok, j + 1)
                at_least(pe, g_ok, FC * (j - 1))
                for f in range(FC):
                    o = HB[r % 2][f]
                    hi = w1_hi[:, bass.ds(e * FF + f * P, P)]
                    pe.matmul(o, hi, xeT[r % 2][:, 0:ET], start=True, stop=False)
                    pe.matmul(o, hi, xeT[r % 2][:, ET:2 * ET], start=False, stop=False)
                    last = pe.matmul(o, w1_lo[:, bass.ds(e * FF + f * P, P)], xeT[r % 2][:, 0:ET], start=False, stop=True)
                last.then_inc(h_ps, 1)

            def layer2(j, i, r, e):
                pe.wait_ge(g_ok, FC * (j + 1))
                at_least(pe, y2_ok, j - 1)
                for t in range(2):
                    for f in range(FC):
                        g = g_sb[r % 2][:, f * ET + t * P:f * ET + (t + 1) * P]
                        last = pe.matmul(YB[r % 2][:, t * P:(t + 1) * P], g, w2_sb[:, bass.ds(e * FF + f * P, P)],
                                         start=(f == 0), stop=(f == FC - 1))
                last.then_inc(y2_ps, 1)

            experts = [None] * RING

            def expert_tile(j, i, r):
                if there(j + 1):
                    turn_rows(*near(j, i, r, 1))
                if there(j):
                    experts[r] = expert_of(j)
                    layer1(j, i, r, experts[r])
                if there(j - 1):
                    layer2(*near(j, i, r, -1), experts[r - 1] if r else expert_of(j - 1))

            turn_rows(0, 0, 0)
            expert_tiles(pe, expert_tile, behind=1)

        @block.scalar
        def _(act):
            act.dma_start(wqkv[:, :], w_qkvT).then_inc(ld_wqkv, 16)
            act.preload_act_table(ACT.Exp)
            act.dma_start(ctx_sb[:, :], ctxT).then_inc(ld_ctx, 16)
            act.dma_start(wt[:, :], w_tT).then_inc(ld_ctx, 16)
            act.dma_start(bt[:, :], b_t).then_inc(ld_ctx, 16)

            def ctx_out():
                act.wait_ge(ld_ctx, 16 * CTX_LOADS)
                for c in range(T // 512):
                    act.wait_ge(tproj, c + 1)
                    cols = slice(c * 512, (c + 1) * 512)
                    act.activation(tT[:, cols], bank[4 + c][0:XH, :], ACT.Identity, bias=bt[:, :]).then_inc(tread, 1)
                    act.activation(tsq[:, cols], bank[4 + c][0:XH, :], ACT.Square, bias=bt[:, :]).then_inc(tread, 1)

            def ctx_turned():
                act.wait_ge(itnT_ps, 1)
                act.activation(itnT[:, :], DOT[0:TILES, 0:P], ACT.Copy).then_inc(itnT_ok, 1)

            def ctx_row_out(c):
                act.wait_ge(itnrow_ps, c + 1)
                act.activation(itn_row[:, c * 512:(c + 1) * 512], [DOT, GATE][c % 2][:, :], ACT.Copy).then_inc(itnrow_ok, 1)

            def qkv_out(n):
                act.wait_ge(qkv_ps, n + 1)
                at_least(act, phi_ok, n)
                act.activation(e_qk[:, :, :], QKV[:, :, 0:2 * P], ACT.Exp).then_inc(qkv_read, 1)
                act.activation(r_qk[:, :, :], QKV[:, :, 0:2 * P], ACT.Relu).then_inc(qkv_read, 1)
                at_least(act, kv_ok, 2 * n)
                at_least(act, kv_pool, n)
                act.activation(v_sb[:, :, :], QKV[:, :, 2 * P:3 * P], ACT.Copy).then_inc(qkv_read, 1)

            def oT_out(m):
                act.wait_ge(oT_ps, 2 * (m + 1))
                at_least(act, y_ps, m)
                act.activation(oT[:, :], TR[:, 0:2 * P], ACT.Copy).then_inc(oT_ok, 1)

            def norm1(m, p):
                act.wait_ge(nmr1_ok, m + 1)
                act.wait_ge(rstd1_ok, m + 1)
                at_least(act, r2_ok, m - 1)
                for t in range(2):
                    act.activation(x1[p][:, t, :], r1[:, t, :], ACT.Identity, bias=nmr1[:, t:t + 1],
                                   scale=rstd1[:, t:t + 1]).then_inc(x1_ok, 1)

            def x1T_out(m):
                act.wait_ge(x1T_ps, m + 1)
                at_least(act, vT_ps, m)
                act.activation(x1T[:, :], DOT[:, 0:2 * P], ACT.Copy).then_inc(x1T_ok, 1)

            def v_out(m):
                act.wait_ge(vT_ps, m + 1)
                at_least(act, dot_ps, m)
                act.activation(vT[:, :], MM[0:XH, 0:2 * P], ACT.Identity, bias=bv[:, :]).then_inc(vT_ok, 1)
                act.activation(vsq[:, :], MM[0:XH, 0:2 * P], ACT.Square, bias=bv[:, :]).then_inc(vT_ok, 1)

            def norm2(m, p, i):
                act.wait_ge(nmr2_ok, m + 1)
                act.wait_ge(rstd2_ok, m + 1)
                act.wait_ge(kept[p], 16 * (i + 1))
                for t in range(2):
                    act.activation(x2[p][:, t, :], r2[p][:, t, :], ACT.Identity, bias=nmr2[:, t:t + 1],
                                   scale=rstd2[:, t:t + 1]).then_inc(x2_ok, 1)

            def x2T_out(m):
                act.wait_ge(x2T_ps, m + 1)
                act.activation(x2T[:, :], MM[:, 0:2 * P], ACT.Copy).then_inc(x2T_ok, 1)

            def high_half(m, p):
                act.wait_ge(x2_ok, 2 * (m + 1))
                act.wait_ge(sent, m + 1)
                for t in range(2):
                    act.activation(pay[p][:, t, :, 0:P // 2].bitcast(F16),
                                   x2[p][:, t, :].rearrange("p (a c) -> p a c", a=1).broadcast_to([P, TOP, P]),
                                   ACT.Copy).then_inc(hi_ok, 1)

            def gate_exp(m):
                act.wait_ge(gdif_ok, m + 1)
                act.activation(gexp[:, :, :], gdif[:, :, :], ACT.Exp).then_inc(gexp_ok, 1)

            def cosine_scale(m):
                act.wait_ge(ivn_ok, m + 1)
                for t in range(2):
                    act.activation(wcos[:, t, :], itn_row[:, bass.ds(2 * P * m + t * P, P)], ACT.Copy,
                                   scale=ivn[:, t:t + 1]).then_inc(wcos_ok, 1)

            def high_w1(e):
                if at(e, 0):
                    act.wait_ge(ld_w1, 16)
                cols = bass.ds(e * FF, FF)
                act.activation(w1_raw[:, cols], w1_raw[:, cols], ACT.Copy, scale=W1_SCALE).then_inc(w1s_ok, 1)
                act.wait_ge(w1s_ok, e + 1)
                act.activation(w1_hi[:, cols], w1_raw[:, cols], ACT.Copy).then_inc(w1hi_ok, 1)

            def step(n, p, h, s0, s1, s2, s3, s4):
                if at(n, PAIRS):
                    x2T_out(n - 3)
                    x1T_out(n - 2)
                    high_half(n - 3, 1 - p)
                    oT_out(n - 1)
                    gate_exp(n - 3)
                    v_out(n - 2)
                    norm1(n - 1, 1 - p)
                    cosine_scale(n - 2)
                    high_w1(n - 1)
                    x1T_out(n - 1)
                    v_out(n - 1)
                    norm2(n - 2, p, h - 1)
                    return
                if at(n, PAIRS + 1):
                    x2T_out(n - 3)
                    high_half(n - 3, 1 - p)
                    cosine_scale(n - 2)
                    gate_exp(n - 3)
                    norm2(n - 2, p, h - 1)
                    return
                if s4:
                    x2T_out(n - 3)
                if s3:
                    x1T_out(n - 2)
                if s4:
                    high_half(n - 3, 1 - p)
                if s3:
                    v_out(n - 2)
                if s4:
                    gate_exp(n - 3)
                if s2:
                    high_w1(n - 1)
                if s3:
                    cosine_scale(n - 2)
                if at(n, 1):
                    ctx_turned()
                    ctx_row_out(0)
                if s2:
                    oT_out(n - 1)
                if at(n, 1):
                    ctx_row_out(1)
                if s0:
                    qkv_out(n + 1)
                if at(n, 1):
                    ctx_row_out(2)
                    ctx_row_out(3)
                if s3:
                    norm2(n - 2, p, h - 1)
                if s2:
                    norm1(n - 1, 1 - p)

            qkv_out(0)
            ctx_out()
            pipeline(act, step)

            act.preload_act_table(ACT.Gelu)
            act.wait_ge(table_ok, 1)
            pad_experts(act, range(1, EXPERTS, 2))
            act.wait_ge(table_ok, 3)
            act.wait_ge(ld_big, 16 * BIG_LOADS)

            def gelu(j, i, r):
                e = act.value_load(e_i[0:1, bass.ds(j, 1)], min_val=0, max_val=EXPERTS - 1)
                act.wait_ge(h_ps, j + 1)
                at_least(act, y2_ps, j - 1)
                for f in range(FC):
                    act.activation(g_sb[r % 2][:, f * ET:(f + 1) * ET], HB[r % 2][f], ACT.Gelu,
                                   bias=b1_sb[:, bass.ds(e * FC + f, 1)], scale=1.0 / W1_SCALE).then_inc(g_ok, 1)

            expert_tiles(act, gelu)

            load_results(act, 1)
            for q, (t0, t1) in enumerate(GROUPS):
                act.wait_ge(nmr3_ok, q + 1)
                act.wait_ge(rstd3_ok, q + 1)
                for t in range(t0, t1):
                    act.activation(o_sb[:, t, :], z[:, t, :], ACT.Identity, bias=nmr3[:, t:t + 1],
                                   scale=rstd3[:, t:t + 1]).then_inc(o_ok, 1)

        @block.vector
        def _(dve):
            def link(s, count, ins):
                ins.then_inc(s, 1)
                dve.wait_ge(s, count)

            dve.memset(ones16[:, :], 1.0).then_inc(vconsts, 1)
            dve.sem_inc(pos_read, 1)
            dve.memset(macc[0][:, :], 0.0).then_inc(macc_ok, 1)

            def more_constants():
                dve.wait_ge(consts, CONSTS)
                dve.tensor_copy(ident16[:, :], ident[:, :]).then_inc(vconsts, 1)
                dve.tensor_copy(iota_e[:, :], iota_ei[:, :]).then_inc(vconsts, 1)
                dve.tensor_copy(base_e[:, :], base_ei[:, :]).then_inc(vconsts, 1)
                dve.tensor_copy(iota_j[:, :], iota_ji[:, :]).then_inc(vconsts, 1)
                dve.wait_ge(vconsts, VCONSTS)

            def ctx_norms_out():
                dve.wait_ge(tnorm, 1)
                dve.tensor_scalar(tn2[:, :], GATE[:, 0:TILES], TINY, None, ALU.max).then_inc(tn2_ok, 1)

            def features(n, p):
                dve.wait_ge(qkv_read, 3 * n + 2)
                dve.scalar_tensor_tensor(out=phi[p][:, :, :], in0=e_qk[:, :, :], scalar=1.0, in1=r_qk[:, :, :],
                                         op0=ALU.min, op1=ALU.add).then_inc(phi_ok, 1)

            def outer(n, p, t, parts=1):
                dve.wait_ge(qkv_read, 3 * n + 3)
                dve.wait_ge(phi_ok, n + 1)
                k, v, o = outer_operands(p, t, 0, HD // parts)
                dve.tensor_tensor(o, k, v, ALU.mult).then_inc(kv_ok, 1)

            def q_dot_sum(n, p):
                dve.wait_ge(kcum_ps, n + 1)
                dve.tensor_tensor(qk[:, :, :], phi[p][:, :, 0:P], QKV[:, :, 3 * P:4 * P], ALU.mult).then_inc(kcum_read, 1)

            def norm_sum(n):
                dve.wait_ge(kcum_read, n + 1)
                dve.tensor_reduce(norm[:, :], qk[:, :, :].rearrange("p t (h d) -> p (t h) d", d=HD), AX_X,
                                  ALU.add).then_inc(norm_in, 1)

            def norm_floor(n):
                dve.wait_ge(norm_in, 3 * n + 1)
                dve.tensor_scalar(normf[:, :], norm[:, :], NORM_EPS, None, ALU.max).then_inc(norm_in, 1)

            def norm_inverse(n):
                dve.wait_ge(norm_in, 3 * n + 2)
                dve.reciprocal(rnorm[:, :], normf[:, :]).then_inc(norm_in, 1)

            def normalize_q(n, p):
                dve.wait_ge(norm_in, 3 * n + 3)
                dve.tensor_tensor(qn[:, :, :].rearrange("p t (h d) -> p (t h) d", d=HD),
                                  phi[p][:, :, 0:P].rearrange("p t (h d) -> p t h d", d=HD),
                                  rnorm[:, :].rearrange("p (t h o) -> p t h o", t=2, o=1).broadcast_to([P, 2, HEADS, HD]),
                                  ALU.mult).then_inc(qn_ok, 1)

            def weigh(n, u):
                t, half_u = u // 2, u % 2
                if u == 0:
                    dve.wait_ge(qn_ok, n + 1)
                dve.wait_ge(cum_ps, 4 * n + u + 1)
                if half_u == 0 and not at(n, 0):
                    dve.wait_ge(oT_ps, 2 * n - 1 + t)
                q = qn[:, t, :].rearrange("p (h d o) -> p d h o", d=HD, o=1)[:, 4 * half_u:4 * half_u + 4, :, :]
                dve.tensor_tensor(prod[:, t, half_u * 512:(half_u + 1) * 512].rearrange("p (d h e) -> p d h e", d=4, e=HD),
                                  q.broadcast_to([P, 4, HEADS, HD]),
                                  CUM[half_u].rearrange("p (d h e) -> p d h e", d=4, e=HD), ALU.mult).then_inc(prod_ok, 1)

            def residual1(m, p, h):
                dve.wait_ge(y_ps, m + 1)
                dve.wait_ge(ld_x[p], 16 * (h + 1))
                at_least(dve, x1_ok, 2 * m)
                dve.tensor_tensor(r1[:, :, :], MM[:, 0:2 * P].rearrange("p (t d) -> p t d", t=2), x_sb[p][:, :, :],
                                  ALU.add).then_inc(y_read, 1)

            def stats1(m, t):
                dve.wait_ge(y_read, m + 1)
                dve.bn_stats(st1[:, t, :], r1[:, t, :]).then_inc(st1_in, 1)

            def moments1(m):
                wait_apart(dve, (st1_in, 2 * (m + 1)), (ve1_ok, m))
                for t in range(2):
                    dve.bn_aggr(mv1[:, t, :], st1[:, t, :]).then_inc(mv1_ok, 1)

            def shift1(m):
                dve.wait_ge(rstd1_ok, m + 1)
                dve.wait_ge(mv1_ok, 2 * (m + 1))
                dve.scalar_tensor_tensor(out=nmr1[:, :], in0=mv1[:, :, 0], scalar=-1.0, in1=rstd1[:, :],
                                         op0=ALU.mult, op1=ALU.mult).then_inc(nmr1_ok, 1)

            def cross_norm(m):
                dve.wait_ge(dot_ps, m + 1)
                dve.tensor_scalar(vn2[:, :], DOT[:, 2 * P:2 * P + 2], TINY, None, ALU.max).then_inc(vn2_ok, 1)

            def cosines(m):
                dve.wait_ge(wcos_ok, 2 * (m + 1))
                dve.scalar_tensor_tensor(out=ucos[:, :, :], in0=wcos[:, :, :], scalar=COS_CAP,
                                         in1=DOT[:, 0:2 * P].rearrange("p (t d) -> p t d", t=2),
                                         op0=ALU.min, op1=ALU.mult).then_inc(dot_read, 1)

            def residual2(m, p):
                dve.wait_ge(dot_read, m + 1)
                dve.wait_ge(x1_ok, 2 * (m + 1))
                at_least(dve, x2_ok, 2 * m)
                dve.tensor_tensor(r2[p][:, :, :], ucos[:, :, :], x1[p][:, :, :], ALU.add).then_inc(r2_ok, 1)

            def stats2(m, p, t):
                dve.wait_ge(r2_ok, m + 1)
                dve.bn_stats(st2[:, t, :], r2[p][:, t, :]).then_inc(st2_in, 1)

            def moments2(m, p):
                wait_apart(dve, (st2_in, 2 * (m + 1)), (ve2_ok, m))
                for t in range(2):
                    dve.bn_aggr(mv2[p][:, t, :], st2[:, t, :]).then_inc(mv2_ok, 1)

            def shift2(m, p):
                dve.wait_ge(rstd2_ok, m + 1)
                dve.wait_ge(mv2_ok, 2 * (m + 1))
                at_least(dve, x2_ok, 2 * m)
                dve.scalar_tensor_tensor(out=nmr2[:, :], in0=mv2[p][:, :, 0], scalar=-1.0, in1=rstd2[:, :],
                                         op0=ALU.mult, op1=ALU.mult).then_inc(nmr2_ok, 1)

            def over_experts(a):
                return a[:, :].rearrange("p (t o) -> p t o", o=1).broadcast_to([P, 2, EXPERTS])

            logits = GATE[:, 0:2 * EXPERTS].rearrange("p (t e) -> p t e", t=2)
            G = 12

            def gate_max(m):
                dve.wait_ge(gate_ps, m + 1)
                dve.tensor_reduce(gmax[:, :], logits, AX_X, ALU.max).then_inc(gate_in, 1)

            def gate_shift(m):
                dve.wait_ge(gate_in, G * m + 1)
                dve.tensor_tensor(gdif[:, :, :], logits, over_experts(gmax), ALU.subtract).then_inc(gdif_ok, 1)

            def gate_sum(m):
                dve.wait_ge(gexp_ok, m + 1)
                dve.tensor_reduce(gsum[:, :], gexp[:, :, :], AX_X, ALU.add).then_inc(gate_in, 1)

            def gate_inverse(m):
                dve.wait_ge(gate_in, G * m + 2)
                dve.reciprocal(rgsum[:, :], gsum[:, :]).then_inc(gate_in, 1)

            def gate_scores(m):
                dve.wait_ge(gate_in, G * m + 3)
                dve.tensor_tensor(score[:, :, :], gexp[:, :, :], over_experts(rgsum), ALU.mult).then_inc(gate_in, 1)

            def gate_top(m):
                wait_apart(dve, (gate_in, G * m + 4))
                for t in range(2):
                    dve.max(top8[:, t, :], score[:, t, :]).then_inc(gate_in, 1)

            def gate_index(m):
                wait_apart(dve, (gate_in, G * m + 6))
                for t in range(2):
                    dve.max_index(idx8[:, t, :], top8[:, t, :], score[:, t, :]).then_inc(gate_in, 1)

            def gate_chosen(m):
                dve.wait_ge(gate_in, G * m + 8)
                dve.tensor_copy(chosen[:, :, :], idx8[:, :, 0:TOP]).then_inc(gate_in, 1)

            def gate_weight_sum(m):
                dve.wait_ge(gate_in, G * m + 6)
                dve.tensor_tensor(wsum[:, :], top8[:, :, 0], top8[:, :, 1], ALU.add).then_inc(gate_in, 1)

            def gate_onehot(m):
                dve.wait_ge(gate_in, G * m + 9)
                dve.tensor_tensor(
                    onehot[:, :, :],
                    iota_e[:, :].rearrange("p (o e) -> p o e", o=1).broadcast_to([P, 2 * TOP, EXPERTS]),
                    chosen[:, :, :].rearrange("p t (k o) -> p (t k) o", o=1).broadcast_to([P, 2 * TOP, EXPERTS]),
                    ALU.is_equal).then_inc(gate_in, 1)

            def gate_weight_inverse(m):
                dve.wait_ge(gate_in, G * m + 10)
                dve.reciprocal(rwsum[:, :], wsum[:, :]).then_inc(gate_in, 1)

            def gate_members(m, p):
                dve.wait_ge(gate_in, G * m + 11)
                hot = onehot[:, :, :].rearrange("p (t k) e -> p t k e", k=TOP)
                dve.tensor_tensor(member[p][:, :, :], hot[:, :, 0, :], hot[:, :, 1, :], ALU.add).then_inc(member_ok, 1)

            def gate_weights(m, p):
                dve.wait_ge(gate_in, G * m + 12)
                dve.tensor_tensor(pay[p][:, :, :, WEIGHT], top8[:, :, 0:TOP],
                                  rwsum[:, :].rearrange("p (t o) -> p t o", o=1).broadcast_to([P, 2, TOP]),
                                  ALU.mult).then_inc(w_ok, 1)

            def members_sum(m, p):
                dve.wait_ge(member_ok, m + 1)
                dve.tensor_tensor(msum[:, :], member[p][:, 0, :], member[p][:, 1, :], ALU.add).then_inc(msum_ok, 1)

            def members_count(m, p):
                dve.wait_ge(msum_ok, m + 1)
                dve.tensor_tensor(macc[1 - p][:, :], macc[p][:, :], msum[:, :], ALU.add).then_inc(macc_ok, 1)

            def return_rows(m, p):
                dve.wait_ge(sent, m + 1)
                dve.tensor_copy(pay[p][:, :, :, RETURN].bitcast(I32), returns[:, bass.ds(2 * m, 2), :]).then_inc(returns_ok, 1)

            def row_base(m):
                dve.wait_ge(pos_ps, m + 1)
                dve.tensor_tensor(place[:, :, :], GATE[:, 2 * EXPERTS:4 * EXPERTS].rearrange("p (t e) -> p t e", t=2),
                                  base_e[:, :].rearrange("p (o e) -> p o e", o=1).broadcast_to([P, 2, EXPERTS]),
                                  ALU.add).then_inc(pos_read, 1)

            def row_pick(m):
                dve.wait_ge(pos_read, m + 2)
                dve.tensor_tensor(
                    placed[:, :, :].rearrange("p (t k) e -> p t k e", k=TOP),
                    onehot[:, :, :].rearrange("p (t k) e -> p t k e", k=TOP),
                    place[:, :, :].rearrange("p t (o e) -> p t o e", o=1).broadcast_to([P, 2, TOP, EXPERTS]),
                    ALU.mult).then_inc(row_in, 1)

            def row_sum(m):
                dve.wait_ge(row_in, 2 * m + 1)
                dve.tensor_reduce(rowf[:, :], placed[:, :, :], AX_X, ALU.add).then_inc(row_in, 1)

            def row_index(m, p):
                dve.wait_ge(row_in, 2 * m + 2)
                dve.tensor_copy(rowi[p][:, :], rowf[:, :]).then_inc(row_ok, 1)

            def step(n, p, h, s0, s1, s2, s3, s4):
                m2, m3, m4 = n - 1, n - 2, n - 3
                if at(n, PAIRS):
                    return_rows(m4, 1 - p)
                    gate_max(m4)
                    gate_shift(m4)
                    residual1(m2, 1 - p, h - 1 + p)
                    gate_sum(m4)
                    stats1(m2, 0)
                    gate_inverse(m4)
                    stats1(m2, 1)
                    gate_scores(m4)
                    moments1(m2)
                    gate_top(m4)
                    gate_index(m4)
                    gate_chosen(m4)
                    gate_weight_sum(m4)
                    shift1(m2)
                    gate_onehot(m4)
                    gate_weight_inverse(m4)
                    gate_members(m4, 1 - p)
                    gate_weights(m4, 1 - p)
                    members_sum(m4, 1 - p)
                    members_count(m4, 1 - p)
                    cross_norm(m3)
                    row_base(m4)
                    row_pick(m4)
                    row_sum(m4)
                    row_index(m4, 1 - p)
                    cosines(m3)
                    residual2(m3, p)
                    stats2(m3, p, 0)
                    stats2(m3, p, 1)
                    moments2(m3, p)
                    shift2(m3, p)
                    return
                if at(n, PAIRS + 1):
                    cross_norm(m3)
                    return_rows(m4, 1 - p)
                    cosines(m3)
                    residual2(m3, p)
                    gate_max(m4)
                    stats2(m3, p, 0)
                    gate_shift(m4)
                    stats2(m3, p, 1)
                    gate_sum(m4)
                    moments2(m3, p)
                    gate_inverse(m4)
                    gate_scores(m4)
                    gate_top(m4)
                    gate_index(m4)
                    gate_chosen(m4)
                    shift2(m3, p)
                    gate_weight_sum(m4)
                    gate_onehot(m4)
                    gate_weight_inverse(m4)
                    gate_members(m4, 1 - p)
                    gate_weights(m4, 1 - p)
                    members_sum(m4, 1 - p)
                    members_count(m4, 1 - p)
                    row_base(m4)
                    row_pick(m4)
                    row_sum(m4)
                    row_index(m4, 1 - p)
                    return
                if at(n, 1):
                    more_constants()
                if s1:
                    q_dot_sum(n, p)
                if s4:
                    return_rows(m4, 1 - p)
                if s1:
                    norm_sum(n)
                    outer(n, p, 1, 2)
                    norm_floor(n)
                    norm_inverse(n)
                    normalize_q(n, p)
                    weigh(n, 0)
                if s4:
                    gate_max(m4)
                    gate_shift(m4)
                if s1:
                    weigh(n, 1)
                if at(n, 0):
                    ctx_norms_out()
                if s4:
                    gate_sum(m4)
                if s3:
                    cross_norm(m3)
                if s4:
                    gate_inverse(m4)
                    gate_scores(m4)
                    gate_top(m4)
                    gate_index(m4)
                    gate_chosen(m4)
                    gate_weight_sum(m4)
                    gate_onehot(m4)
                if s3:
                    cosines(m3)
                if s4:
                    gate_weight_inverse(m4)
                if s3:
                    residual2(m3, p)
                if s4:
                    gate_members(m4, 1 - p)
                if s3:
                    stats2(m3, p, 0)
                    stats2(m3, p, 1)
                if s4:
                    gate_weights(m4, 1 - p)
                    members_sum(m4, 1 - p)
                if s3:
                    moments2(m3, p)
                if s4:
                    members_count(m4, 1 - p)
                if s2:
                    residual1(m2, 1 - p, h - 1 + p)
                if s4:
                    row_base(m4)
                if s2:
                    stats1(m2, 0)
                    stats1(m2, 1)
                if s4:
                    row_pick(m4)
                if s2:
                    moments1(m2)
                if s0:
                    features(n + 1, 1 - p)
                if s3:
                    shift2(m3, p)
                if s1:
                    weigh(n, 2)
                if s4:
                    row_sum(m4)
                if s2:
                    shift1(m2)
                if s1:
                    weigh(n, 3)
                if s4:
                    row_index(m4, 1 - p)
                if s0:
                    outer(n + 1, 1 - p, 0)

            features(0, 0)
            outer(0, 0, 0)
            pipeline(dve, step)

            dve.wait_ge(cnt_ps, 1)
            dve.tensor_copy(cnt_i[:, :], GATE[:, 0:EXPERTS]).then_inc(table_ok, 1)
            dve.wait_ge(table_ok, 1)
            link(tsteps, 1, dve.tensor_scalar(cup_i[:, :], cnt_i[:, :], float(ET - 1), None, ALU.add))
            link(tsteps, 2, dve.tensor_scalar(nt_i[:, :], cup_i[:, :], ET.bit_length() - 1, None, ALU.logical_shift_right))
            link(tsteps, 3, dve.tensor_copy(nt[:, :], nt_i[:, :]))
            link(tsteps, 4, dve.tensor_tensor_scan(ntc[:, :], ones[:, 0:EXPERTS], nt[:, :], 0.0, ALU.mult, ALU.add))
            link(tsteps, 5, dve.tensor_tensor(
                past[:, :, :], ntc[:, :].rearrange("p (o e) -> p o e", o=1).broadcast_to([P, SLOTS, EXPERTS]),
                iota_j[:, :].rearrange("p (j o) -> p j o", o=1).broadcast_to([P, SLOTS, EXPERTS]), ALU.is_le))
            link(tsteps, 6, dve.tensor_reduce(ej[:, :], past[:, :, :], AX_X, ALU.add))
            link(tsteps, 7, dve.tensor_tensor(
                pnt[:, :, :], past[:, :, :], nt[:, :].rearrange("p (o e) -> p o e", o=1).broadcast_to([P, SLOTS, EXPERTS]),
                ALU.mult))
            link(tsteps, 8, dve.tensor_reduce(first_j[:, :], pnt[:, :, :], AX_X, ALU.add))
            link(tsteps, 9, dve.tensor_tensor(off_j[:, :], iota_j[:, :], first_j[:, :], ALU.subtract))
            link(tsteps, 10, dve.tensor_scalar(off_rows[:, :], off_j[:, :], float(ET), None, ALU.mult))
            link(tsteps, 11, dve.scalar_tensor_tensor(out=row_j[:, :], in0=ej[:, :], scalar=float(CAP), in1=off_rows[:, :],
                                              op0=ALU.mult, op1=ALU.add))
            dve.tensor_copy(row_i[:, :], row_j[:, :]).then_inc(table_ok, 1)
            dve.tensor_scalar(e_i[:, :], ej[:, :], float(EXPERTS - 1), None, ALU.min).then_inc(table_ok, 1)
            dve.wait_ge(table_ok, 3)
            dve.wait_ge(ld_big, 16 * BIG_LOADS)

            def take(j, i, r):
                dve.wait_ge(xe_ps, j + 1)
                at_least(dve, h_ps, j - 1)
                dve.tensor_copy(xeT[r % 2][:, :], XB[r % 2][:, 0:ET].bitcast(F16)).then_inc(xe_ok, 1)

            def take_returns(j, i, r):
                dve.wait_ge(ld_row[r], 16 * (i + 1))
                at_least(dve, returned[r], 2 * 16 * i)
                dve.tensor_copy(ridx[r][:, :], xrow[r][:, :, RETURN].bitcast(I32)).then_inc(ridx_ok, 1)
                dve.tensor_copy(wrow[r][:, :], xrow[r][:, :, WEIGHT]).then_inc(wrow_ok, 1)

            def give(j, i, r):
                e = dve.value_load(e_i[0:1, bass.ds(j, 1)], min_val=0, max_val=EXPERTS - 1)
                dve.wait_ge(y2_ps, j + 1)
                at_least(dve, yw_ok, 2 * j)
                dve.tensor_tensor(ysum[:, :, :], YB[r % 2][:, 0:2 * P].rearrange("p (t d) -> p t d", t=2),
                                  b2_sb[:, bass.ds(e * P, P)].rearrange("p (o d) -> p o d", o=1).broadcast_to([P, 2, P]),
                                  ALU.add).then_inc(y2_ok, 1)
                dve.wait_ge(y2_ok, j + 1)
                dve.wait_ge(wrow_ok, j + 1)
                for t in range(2):
                    dve.tensor_scalar(y_sb[r][:, t, :], ysum[:, t, :], wrow[r][:, t:t + 1], None, ALU.mult).then_inc(yw_ok, 1)

            def expert_tile(j, i, r):
                if there(j + 1):
                    take(*near(j, i, r, 1))
                if there(j - 1):
                    give(*near(j, i, r, -1))
                if there(j):
                    take_returns(j, i, r)

            take(0, 0, 0)
            expert_tiles(dve, expert_tile, behind=1)

            for p in range(2):
                dve.wait_ge(kept[p], 16 * (PAIRS // 2 + 1))

            def shift3(q):
                t0, t1 = GROUPS[q]
                dve.wait_ge(rstd3_ok, q + 1)
                dve.scalar_tensor_tensor(out=nmr3[:, t0:t1], in0=mv3[:, t0:t1, 0], scalar=-1.0, in1=rstd3[:, t0:t1],
                                         op0=ALU.mult, op1=ALU.mult).then_inc(nmr3_ok, 1)

            added = 0
            for q, (t0, t1) in enumerate(GROUPS):
                if q in POOL_GROUPS:
                    dve.wait_ge(z1_pool, POOL_GROUPS.index(q) + 1)
                else:
                    dve.wait_ge(ld_y[q], 16 * TOP)
                    dve.tensor_tensor(z1[:, t0:t1, :], y_in[:, 0, t0:t1, :], y_in[:, 1, t0:t1, :], ALU.add).then_inc(z1_ok, 1)
                    added += 1
                    dve.wait_ge(z1_ok, added)
                dve.tensor_tensor(z[:, t0:t1, :], z1[:, t0:t1, :], x2_all[:, t0:t1, :], ALU.add).then_inc(z_ok, 1)
                dve.wait_ge(z_ok, q + 1)
                for t in range(t0, t1):
                    dve.bn_stats(st3[:, t, :], z[:, t, :]).then_inc(zsteps, 1)
                if q:
                    shift3(q - 1)
                for t in range(t0, t1):
                    dve.wait_ge(zsteps, t + 1)
                    dve.bn_aggr(mv3[:, t, :], st3[:, t, :]).then_inc(mv3_ok, 1)
            shift3(len(GROUPS) - 1)


def kernel(x, ctx_768, L0_attn_Wq, L0_attn_Wk, L0_attn_Wv, L0_attn_Wo, L0_xattn_Wv, L0_xattn_bv, L0_xattn_Wt, L0_xattn_bt,
           L0_ffn_gate_w, L0_ffn_w1, L0_ffn_b1, L0_ffn_w2, L0_ffn_b2):
    import numpy as np
    import concourse.bacc as bacc
    from concourse.bass_utils import run_bass_kernel_spmd

    def flat(a):
        a = np.asarray(a)
        return a.reshape(-1, a.shape[-1])

    def columns(a):
        return np.ascontiguousarray(np.asarray(a).T)

    batch, seq, hidden = np.shape(x)
    experts, ff = np.shape(L0_ffn_b1)
    arrays = {
        "x": np.ascontiguousarray(flat(x)),
        "xT": columns(flat(x)),
        "ctxT": columns(flat(ctx_768)),
        "w_qkvT": np.ascontiguousarray(np.concatenate([np.asarray(w) for w in (L0_attn_Wq, L0_attn_Wk, L0_attn_Wv)]).T),
        "w_oT": columns(L0_attn_Wo),
        "w_xvT": columns(L0_xattn_Wv),
        "b_v": np.ascontiguousarray(np.asarray(L0_xattn_bv).reshape(-1, 1)),
        "w_tT": columns(L0_xattn_Wt),
        "b_t": np.ascontiguousarray(np.asarray(L0_xattn_bt).reshape(-1, 1)),
        "gate_w": np.ascontiguousarray(L0_ffn_gate_w),
        "w1": np.ascontiguousarray(L0_ffn_w1),
        "b1T": columns(np.asarray(L0_ffn_b1).reshape(experts * ff // 128, 128)),
        "w2": np.ascontiguousarray(L0_ffn_w2),
        "b2": np.ascontiguousarray(L0_ffn_b2),
    }
    nc = bacc.Bacc("TRN2", target_bir_lowering=False, num_devices=1)
    ins = {n: nc.dram_tensor(f"{n}_dram", a.shape, mybir.dt.from_np(a.dtype), kind="ExternalInput").ap()
           for n, a in arrays.items()}
    out = nc.dram_tensor("out_dram", (batch * seq, hidden), mybir.dt.float32, kind="ExternalOutput").ap()
    decoder_layer(nc, **ins, out=out)
    r = run_bass_kernel_spmd(nc, [{f"{n}_dram": a for n, a in arrays.items()}], core_ids=[0])
    return r.results[0]["out_dram"].reshape(batch, seq, hidden)
```
